# Optimizing a Trainium2 kernel written in Bass

```python
import numpy as np
import jax
import jax.numpy as jnp

def _softmax(x, axis=-1):
    return jax.nn.softmax(x, axis=axis)

def _gelu(x):
    return jax.nn.gelu(x, approximate=True)

def _silu(x):
    return jax.nn.silu(x)

def _sigmoid(x):
    return jax.nn.sigmoid(x)

def _layernorm(x, axis=-1, eps=1e-05):
    m = jnp.mean(x, axis=axis, keepdims=True)
    v = jnp.var(x, axis=axis, keepdims=True)
    return (x - m) / jnp.sqrt(v + eps)

def _scatter_add(tgt, idx, src, axis=0):
    return tgt.at[idx].add(src)

def _segment_sum(src, seg, n):
    return jax.ops.segment_sum(src, seg, n)
kernel_name = 'mk_decoder_preln_d1_seqx_r4_7cffbd'

def setup_inputs(seed: int=0):
    np.random.seed(seed)
    _w = jnp.asarray

    def _rec_inputs():
        import jax
        import jax.numpy as jnp
        _rk = jax.random.key(seed)
        x = -0.0003929 + 0.9999 * jax.random.normal(jax.random.fold_in(_rk, 1), (2, 512, 1024), jnp.float32)
        _lenS = 512 - jax.random.randint(jax.random.fold_in(_rk, 7), (2,), 0, max(1, 512 // 4) + 1, jnp.int32)
        _lenS2 = 1024 - jax.random.randint(jax.random.fold_in(_rk, 8), (2,), 0, max(1, 1024 // 4) + 1, jnp.int32)
        pos_BxS = jnp.broadcast_to(jnp.arange(512, dtype=jnp.int32), (2, 512))
        _ctx_1024P = jax.random.normal(jax.random.fold_in(_rk, 12), (2, 16, 256), jnp.float32)
        _ctx_1024c = jax.random.dirichlet(jax.random.fold_in(_rk, 512), 0.3 * jnp.ones((16,), jnp.float32), (2, 1024))
        _ctx_1024t = jnp.einsum('bsk,bkd->bsd', _ctx_1024c, _ctx_1024P)
        _ctx_1024t = _ctx_1024t * jax.lax.rsqrt(jnp.mean(jnp.square(_ctx_1024t)) + 1e-12) * 0.953939
        ctx_1024 = 6.77073e-06 + 0.0199965 * (_ctx_1024t + 0.3 * jax.random.normal(jax.random.fold_in(_rk, 612), (2, 1024, 256), jnp.float32))
        return (x, pos_BxS, ctx_1024)
    x, pos_BxS, ctx_1024 = _rec_inputs()

    def _L0_attn_setup():
        import jax, jax.numpy as jnp
        import numpy as np
        import math
        B, S, H = (1, 512, 1024)
        NH, NKV, HD = (32, 8, 128)
        GS = 128
        WBITS = 4
        ZERO = float(2 ** (WBITS - 1))
        THETA = 10000.0

        def _dequant_matmul(x, qw, scales):
            w = (qw.astype(jnp.float32) - ZERO) * jnp.repeat(scales, GS, axis=0)
            return x @ w

        def _rope_tables(seq_len, dtype):
            inv_freq = 1.0 / THETA ** (jnp.arange(0, HD, 2, dtype=jnp.float32) / HD)
            freqs = jnp.arange(seq_len, dtype=jnp.float32)[:, None] * inv_freq
            emb = jnp.concatenate([freqs, freqs], axis=-1)
            return (jnp.cos(emb).astype(dtype), jnp.sin(emb).astype(dtype))

        def _rotate_half(x):
            x1, x2 = jnp.split(x, 2, axis=-1)
            return jnp.concatenate([-x2, x1], axis=-1)

        def _apply_rope(x, cos, sin):
            return x * cos[None, None] + _rotate_half(x) * sin[None, None]
        key = jax.random.key(seed)
        ks = jax.random.split(key, 9)
        small = lambda k, shp: jax.random.uniform(k, shp, jnp.float32) * 0.01 + 0.001
        return {'hidden_states': jax.random.normal(ks[0], (B, S, H), jnp.float32), 'scales_q': small(ks[1], (H // GS, NH * HD)), 'scales_k': small(ks[2], (H // GS, NKV * HD)), 'scales_v': small(ks[3], (H // GS, NKV * HD)), 'scales_o': small(ks[4], (NH * HD // GS, H)), 'qw_q': jax.random.randint(ks[5], (H, NH * HD), 0, 2 ** WBITS, jnp.int32), 'qw_k': jax.random.randint(ks[6], (H, NKV * HD), 0, 2 ** WBITS, jnp.int32), 'qw_v': jax.random.randint(ks[7], (H, NKV * HD), 0, 2 ** WBITS, jnp.int32), 'qw_o': jax.random.randint(ks[8], (NH * HD, H), 0, 2 ** WBITS, jnp.int32)}
    _L0_attn_all = _L0_attn_setup()
    _L0_attn_in = {k: v for k, v in _L0_attn_all.items() if k in ('scales_q', 'scales_k', 'scales_v', 'scales_o', 'qw_q', 'qw_k', 'qw_v', 'qw_o')}
    del _L0_attn_all

    def _L0_xattn_setup():
        import jax, jax.numpy as jnp
        import numpy as np
        H = 256
        C = 4
        RH = 16
        HS = H // RH
        DR = 8
        M = 1024
        NH = 16
        HD = H // NH
        A_SIZE = (C - 1) * RH
        B_SIZE = C * RH
        EPS = 1e-05
        SSM_EPS = 1e-05

        def rat_read(res, W, gamma, beta, num_outputs):
            b, l, _ = res.shape
            x = res.reshape(b, l, H, C)
            y = jnp.einsum('blhc,hoc->bloh', x, W)
            mu = y.mean(-1, keepdims=True)
            var = y.var(-1, keepdims=True)
            yn = (y - mu) * jax.lax.rsqrt(var + EPS)
            yn = yn * gamma.reshape(num_outputs, H) + beta.reshape(num_outputs, H)
            return yn.reshape(b, l, num_outputs * H)

        def rope(x, pos):
            half = HD // 2
            inv = 1.0 / 10000.0 ** (jnp.arange(half, dtype=jnp.float32) / half)
            ang = pos.astype(jnp.float32)[..., None] * inv
            cos = jnp.cos(ang)[:, :, None, :]
            sin = jnp.sin(ang)[:, :, None, :]
            x1, x2 = (x[..., :half], x[..., half:])
            return jnp.concatenate([x1 * cos - x2 * sin, x2 * cos + x1 * sin], axis=-1)

        def attention(qkv_in, qkv_w, pos):
            b, l, _ = qkv_in.shape
            q, k, v = jnp.split(qkv_in, 3, axis=-1)
            q = jnp.einsum('bli,oi->blo', q, qkv_w[0]).reshape(b, l, NH, HD)
            k = jnp.einsum('bli,oi->blo', k, qkv_w[1]).reshape(b, l, NH, HD)
            v = jnp.einsum('bli,oi->blo', v, qkv_w[2]).reshape(b, l, NH, HD)
            q = rope(q, pos)
            k = rope(k, pos)
            scores = jnp.einsum('bqhd,bkhd->bhqk', q, k) / np.sqrt(HD).astype(np.float32)
            mask = jnp.tril(jnp.ones((l, l), dtype=bool))
            scores = jnp.where(mask, scores, jnp.float32(-1e+30))
            p = jax.nn.softmax(scores, axis=-1)
            o = jnp.einsum('bhqk,bkhd->bqhd', p, v)
            return o.reshape(b, l, H)

        def rat_write(res, y, wod_w, wab_w, wab_b, du_w, du_b):
            b, l, _ = res.shape
            o_d = y @ wod_w.T
            A_B = y @ wab_w.T + wab_b
            out = o_d[..., :H]
            delta_low = o_d[..., H:]
            A_logit = A_B[..., :A_SIZE]
            B_proj = A_B[..., A_SIZE:2 * A_SIZE]
            B_skip = A_B[..., 2 * A_SIZE:]
            delta = jax.nn.softplus(delta_low @ du_w.T + du_b)
            hs = res.reshape(b, l, HS, RH, C)
            out = out.reshape(b, l, HS, RH, 1)
            delta = delta.reshape(b, l, HS, RH, 1)
            A_logit = A_logit.reshape(b, l, 1, RH, C - 1)
            B_proj = B_proj.reshape(b, l, 1, RH, C - 1)
            B_skip = B_skip.reshape(b, l, 1, RH, 1)
            A_neg = -jax.nn.softplus(A_logit)
            A_bar = jnp.exp(delta * A_neg)
            B_bar = (A_bar - 1.0) / (A_neg - SSM_EPS) * B_proj
            B_bar_skip = delta * B_skip
            A_full = jnp.concatenate([A_bar, jnp.ones_like(A_bar[..., :1])], axis=-1)
            B_full = jnp.concatenate([B_bar, B_bar_skip], axis=-1)
            return (hs * A_full + out * B_full).reshape(b, l, H * C)

        def layer_forward(hidden_states, position_ids, attn_read_w, attn_read_g, attn_read_b, qkv_w, attn_wod_w, attn_wab_w, attn_wab_b, attn_du_w, attn_du_b, mlp_read_w, mlp_read_g, mlp_read_b, mlp_in_w, mlp_wod_w, mlp_wab_w, mlp_wab_b, mlp_du_w, mlp_du_b):
            qkv_in = rat_read(hidden_states, attn_read_w, attn_read_g, attn_read_b, 3)
            attn_out = attention(qkv_in, qkv_w, position_ids)
            hidden_states = rat_write(hidden_states, attn_out, attn_wod_w, attn_wab_w, attn_wab_b, attn_du_w, attn_du_b)
            mlp_in = rat_read(hidden_states, mlp_read_w, mlp_read_g, mlp_read_b, 2)
            g_in, u_in = (mlp_in[..., :H], mlp_in[..., H:])
            gate = jnp.einsum('bli,oi->blo', g_in, mlp_in_w[0])
            up = jnp.einsum('bli,oi->blo', u_in, mlp_in_w[1])
            mlp_out = jax.nn.silu(gate) * up
            hidden_states = rat_write(hidden_states, mlp_out, mlp_wod_w, mlp_wab_w, mlp_wab_b, mlp_du_w, mlp_du_b)
            return hidden_states
        key = jax.random.key(seed)
        ks = jax.random.split(key, 20)
        B, L = (2, 512)
        s = 0.02
        return {'hidden_states': jax.random.normal(ks[0], (B, L, H * C), jnp.float32), 'position_ids': jnp.tile(jnp.arange(L, dtype=jnp.int64), (B, 1)), 'attn_read_w': jax.random.normal(ks[1], (H, 3, C), jnp.float32) / np.sqrt(C).astype(np.float32), 'attn_read_g': jnp.ones((3 * H,), jnp.float32), 'attn_read_b': jnp.zeros((3 * H,), jnp.float32), 'qkv_w': jax.random.normal(ks[2], (3, H, H), jnp.float32) * s, 'attn_wod_w': jax.random.normal(ks[3], (H + DR, H), jnp.float32) * s, 'attn_wab_w': jax.random.normal(ks[4], (A_SIZE + B_SIZE, H), jnp.float32) * s, 'attn_wab_b': jax.random.normal(ks[5], (A_SIZE + B_SIZE,), jnp.float32) * s, 'attn_du_w': jax.random.normal(ks[6], (H, DR), jnp.float32) * s, 'attn_du_b': jax.random.normal(ks[7], (H,), jnp.float32) * s, 'mlp_read_w': jax.random.normal(ks[8], (H, 2, C), jnp.float32) / np.sqrt(C).astype(np.float32), 'mlp_read_g': jnp.ones((2 * H,), jnp.float32), 'mlp_read_b': jnp.zeros((2 * H,), jnp.float32), 'mlp_in_w': jax.random.normal(ks[9], (2, M, H), jnp.float32) * s, 'mlp_wod_w': jax.random.normal(ks[10], (H + DR, M), jnp.float32) * s, 'mlp_wab_w': jax.random.normal(ks[11], (A_SIZE + B_SIZE, M), jnp.float32) * s, 'mlp_wab_b': jax.random.normal(ks[12], (A_SIZE + B_SIZE,), jnp.float32) * s, 'mlp_du_w': jax.random.normal(ks[13], (H, DR), jnp.float32) * s, 'mlp_du_b': jax.random.normal(ks[14], (H,), jnp.float32) * s}
    _L0_xattn_all = _L0_xattn_setup()
    _L0_xattn_in = {k: v for k, v in _L0_xattn_all.items() if k in ('attn_read_w', 'attn_read_g', 'attn_read_b', 'qkv_w', 'attn_wod_w', 'attn_wab_w', 'attn_wab_b', 'attn_du_w', 'attn_du_b', 'mlp_read_w', 'mlp_read_g', 'mlp_read_b', 'mlp_wod_w', 'mlp_wab_w', 'mlp_wab_b', 'mlp_du_w', 'mlp_du_b')}
    del _L0_xattn_all

    def _L0_ffn_setup():
        import jax, jax.numpy as jnp
        import numpy as np
        B_L, B_H = (4, 8)
        LIN_SLOPE, LIN_INTER, EST_T = (1.0, 0.0, 64.0)
        BATCH, SEQ, IN_F, OUT_F = (4, 512, 1024, 1024)
        MAX_BITS = 8

        def dequant_kbit(qweight, lut, bit):
            O, I32 = (qweight.shape[1], qweight.shape[2])
            shifts = jnp.arange(32, dtype=jnp.int32)
            idx = jnp.zeros((O, I32 * 32), dtype=jnp.int32)
            for p in range(bit):
                bits = (qweight[p][:, :, None] >> shifts & 1).reshape(O, I32 * 32)
                idx = idx | bits << p
            return jnp.take_along_axis(lut, idx, axis=1)
        key = jax.random.key(seed)
        k = jax.random.split(key, 5)
        x = jax.random.normal(k[0], (BATCH, SEQ, IN_F), dtype=jnp.float32)
        qweight = jax.random.randint(k[1], (MAX_BITS, OUT_F, IN_F // 32), 0, 2147483647, dtype=jnp.int32)
        lut4 = jax.random.normal(k[2], (OUT_F, 2 ** B_L), dtype=jnp.float32) * 0.02
        lut8 = jax.random.normal(k[3], (OUT_F, 2 ** B_H), dtype=jnp.float32) * 0.02
        bias = jax.random.normal(k[4], (OUT_F,), dtype=jnp.float32) * 0.01
        return {'x': x, 'qweight': qweight, 'lut4': lut4, 'lut8': lut8, 'bias': bias}
    _L0_ffn_all = _L0_ffn_setup()
    _L0_ffn_in = {k: v for k, v in _L0_ffn_all.items() if k in ('qweight', 'lut4', 'lut8', 'bias')}
    del _L0_ffn_all
    return {'x': x, 'pos_BxS': pos_BxS, 'ctx_1024': ctx_1024, 'L0_attn_scales_q': _L0_attn_in['scales_q'], 'L0_attn_scales_k': _L0_attn_in['scales_k'], 'L0_attn_scales_v': _L0_attn_in['scales_v'], 'L0_attn_scales_o': _L0_attn_in['scales_o'], 'L0_attn_qw_q': _L0_attn_in['qw_q'], 'L0_attn_qw_k': _L0_attn_in['qw_k'], 'L0_attn_qw_v': _L0_attn_in['qw_v'], 'L0_attn_qw_o': _L0_attn_in['qw_o'], 'L0_xattn_attn_read_w': _L0_xattn_in['attn_read_w'], 'L0_xattn_attn_read_g': _L0_xattn_in['attn_read_g'], 'L0_xattn_attn_read_b': _L0_xattn_in['attn_read_b'], 'L0_xattn_qkv_w': _L0_xattn_in['qkv_w'], 'L0_xattn_attn_wod_w': _L0_xattn_in['attn_wod_w'], 'L0_xattn_attn_wab_w': _L0_xattn_in['attn_wab_w'], 'L0_xattn_attn_wab_b': _L0_xattn_in['attn_wab_b'], 'L0_xattn_attn_du_w': _L0_xattn_in['attn_du_w'], 'L0_xattn_attn_du_b': _L0_xattn_in['attn_du_b'], 'L0_xattn_mlp_read_w': _L0_xattn_in['mlp_read_w'], 'L0_xattn_mlp_read_g': _L0_xattn_in['mlp_read_g'], 'L0_xattn_mlp_read_b': _L0_xattn_in['mlp_read_b'], 'L0_xattn_mlp_wod_w': _L0_xattn_in['mlp_wod_w'], 'L0_xattn_mlp_wab_w': _L0_xattn_in['mlp_wab_w'], 'L0_xattn_mlp_wab_b': _L0_xattn_in['mlp_wab_b'], 'L0_xattn_mlp_du_w': _L0_xattn_in['mlp_du_w'], 'L0_xattn_mlp_du_b': _L0_xattn_in['mlp_du_b'], 'L0_ffn_qweight': _L0_ffn_in['qweight'], 'L0_ffn_lut4': _L0_ffn_in['lut4'], 'L0_ffn_lut8': _L0_ffn_in['lut8'], 'L0_ffn_bias': _L0_ffn_in['bias']}

def reference(x, pos_BxS, ctx_1024, L0_attn_scales_q, L0_attn_scales_k, L0_attn_scales_v, L0_attn_scales_o, L0_attn_qw_q, L0_attn_qw_k, L0_attn_qw_v, L0_attn_qw_o, L0_xattn_attn_read_w, L0_xattn_attn_read_g, L0_xattn_attn_read_b, L0_xattn_qkv_w, L0_xattn_attn_wod_w, L0_xattn_attn_wab_w, L0_xattn_attn_wab_b, L0_xattn_attn_du_w, L0_xattn_attn_du_b, L0_xattn_mlp_read_w, L0_xattn_mlp_read_g, L0_xattn_mlp_read_b, L0_xattn_mlp_wod_w, L0_xattn_mlp_wab_w, L0_xattn_mlp_wab_b, L0_xattn_mlp_du_w, L0_xattn_mlp_du_b, L0_ffn_qweight, L0_ffn_lut4, L0_ffn_lut8, L0_ffn_bias):
    import jax
    import jax.numpy as jnp

    def _L0_attn_ref(hidden_states, scales_q, scales_k, scales_v, scales_o, qw_q, qw_k, qw_v, qw_o):
        import jax, jax.numpy as jnp
        import numpy as np
        import math
        B, S, H = (1, 512, 1024)
        NH, NKV, HD = (32, 8, 128)
        GS = 128
        WBITS = 4
        ZERO = float(2 ** (WBITS - 1))
        THETA = 10000.0

        def _dequant_matmul(x, qw, scales):
            w = (qw.astype(jnp.float32) - ZERO) * jnp.repeat(scales, GS, axis=0)
            return x @ w

        def _rope_tables(seq_len, dtype):
            inv_freq = 1.0 / THETA ** (jnp.arange(0, HD, 2, dtype=jnp.float32) / HD)
            freqs = jnp.arange(seq_len, dtype=jnp.float32)[:, None] * inv_freq
            emb = jnp.concatenate([freqs, freqs], axis=-1)
            return (jnp.cos(emb).astype(dtype), jnp.sin(emb).astype(dtype))

        def _rotate_half(x):
            x1, x2 = jnp.split(x, 2, axis=-1)
            return jnp.concatenate([-x2, x1], axis=-1)

        def _apply_rope(x, cos, sin):
            return x * cos[None, None] + _rotate_half(x) * sin[None, None]
        b, s, _ = hidden_states.shape
        q = _dequant_matmul(hidden_states, qw_q, scales_q).reshape(b, s, NH, HD).transpose(0, 2, 1, 3)
        k = _dequant_matmul(hidden_states, qw_k, scales_k).reshape(b, s, NKV, HD).transpose(0, 2, 1, 3)
        v = _dequant_matmul(hidden_states, qw_v, scales_v).reshape(b, s, NKV, HD).transpose(0, 2, 1, 3)
        cos, sin = _rope_tables(s, hidden_states.dtype)
        q = _apply_rope(q, cos, sin)
        k = _apply_rope(k, cos, sin)
        rep = NH // NKV
        k = jnp.repeat(k, rep, axis=1)
        v = jnp.repeat(v, rep, axis=1)
        scores = jnp.einsum('bhqd,bhkd->bhqk', q, k) / math.sqrt(HD)
        causal = jnp.tril(jnp.ones((s, s), dtype=bool))
        scores = jnp.where(causal[None, None], scores, jnp.finfo(scores.dtype).min)
        attn = jax.nn.softmax(scores.astype(jnp.float32), axis=-1).astype(q.dtype)
        ctx = jnp.einsum('bhqk,bhkd->bhqd', attn, v)
        ctx = ctx.transpose(0, 2, 1, 3).reshape(b, s, NH * HD)
        return _dequant_matmul(ctx, qw_o, scales_o)

    def _L0_xattn_ref(hidden_states, position_ids, attn_read_w, attn_read_g, attn_read_b, qkv_w, attn_wod_w, attn_wab_w, attn_wab_b, attn_du_w, attn_du_b, mlp_read_w, mlp_read_g, mlp_read_b, mlp_in_w, mlp_wod_w, mlp_wab_w, mlp_wab_b, mlp_du_w, mlp_du_b):
        import jax, jax.numpy as jnp
        import numpy as np
        H = 256
        C = 4
        RH = 16
        HS = H // RH
        DR = 8
        M = 1024
        NH = 16
        HD = H // NH
        A_SIZE = (C - 1) * RH
        B_SIZE = C * RH
        EPS = 1e-05
        SSM_EPS = 1e-05

        def rat_read(res, W, gamma, beta, num_outputs):
            b, l, _ = res.shape
            x = res.reshape(b, l, H, C)
            y = jnp.einsum('blhc,hoc->bloh', x, W)
            mu = y.mean(-1, keepdims=True)
            var = y.var(-1, keepdims=True)
            yn = (y - mu) * jax.lax.rsqrt(var + EPS)
            yn = yn * gamma.reshape(num_outputs, H) + beta.reshape(num_outputs, H)
            return yn.reshape(b, l, num_outputs * H)

        def rope(x, pos):
            half = HD // 2
            inv = 1.0 / 10000.0 ** (jnp.arange(half, dtype=jnp.float32) / half)
            ang = pos.astype(jnp.float32)[..., None] * inv
            cos = jnp.cos(ang)[:, :, None, :]
            sin = jnp.sin(ang)[:, :, None, :]
            x1, x2 = (x[..., :half], x[..., half:])
            return jnp.concatenate([x1 * cos - x2 * sin, x2 * cos + x1 * sin], axis=-1)

        def attention(qkv_in, qkv_w, pos):
            b, l, _ = qkv_in.shape
            q, k, v = jnp.split(qkv_in, 3, axis=-1)
            q = jnp.einsum('bli,oi->blo', q, qkv_w[0]).reshape(b, l, NH, HD)
            k = jnp.einsum('bli,oi->blo', k, qkv_w[1]).reshape(b, l, NH, HD)
            v = jnp.einsum('bli,oi->blo', v, qkv_w[2]).reshape(b, l, NH, HD)
            q = rope(q, pos)
            k = rope(k, pos)
            scores = jnp.einsum('bqhd,bkhd->bhqk', q, k) / np.sqrt(HD).astype(np.float32)
            mask = jnp.tril(jnp.ones((l, l), dtype=bool))
            scores = jnp.where(mask, scores, jnp.float32(-1e+30))
            p = jax.nn.softmax(scores, axis=-1)
            o = jnp.einsum('bhqk,bkhd->bqhd', p, v)
            return o.reshape(b, l, H)

        def rat_write(res, y, wod_w, wab_w, wab_b, du_w, du_b):
            b, l, _ = res.shape
            o_d = y @ wod_w.T
            A_B = y @ wab_w.T + wab_b
            out = o_d[..., :H]
            delta_low = o_d[..., H:]
            A_logit = A_B[..., :A_SIZE]
            B_proj = A_B[..., A_SIZE:2 * A_SIZE]
            B_skip = A_B[..., 2 * A_SIZE:]
            delta = jax.nn.softplus(delta_low @ du_w.T + du_b)
            hs = res.reshape(b, l, HS, RH, C)
            out = out.reshape(b, l, HS, RH, 1)
            delta = delta.reshape(b, l, HS, RH, 1)
            A_logit = A_logit.reshape(b, l, 1, RH, C - 1)
            B_proj = B_proj.reshape(b, l, 1, RH, C - 1)
            B_skip = B_skip.reshape(b, l, 1, RH, 1)
            A_neg = -jax.nn.softplus(A_logit)
            A_bar = jnp.exp(delta * A_neg)
            B_bar = (A_bar - 1.0) / (A_neg - SSM_EPS) * B_proj
            B_bar_skip = delta * B_skip
            A_full = jnp.concatenate([A_bar, jnp.ones_like(A_bar[..., :1])], axis=-1)
            B_full = jnp.concatenate([B_bar, B_bar_skip], axis=-1)
            return (hs * A_full + out * B_full).reshape(b, l, H * C)

        def layer_forward(hidden_states, position_ids, attn_read_w, attn_read_g, attn_read_b, qkv_w, attn_wod_w, attn_wab_w, attn_wab_b, attn_du_w, attn_du_b, mlp_read_w, mlp_read_g, mlp_read_b, mlp_in_w, mlp_wod_w, mlp_wab_w, mlp_wab_b, mlp_du_w, mlp_du_b):
            qkv_in = rat_read(hidden_states, attn_read_w, attn_read_g, attn_read_b, 3)
            attn_out = attention(qkv_in, qkv_w, position_ids)
            hidden_states = rat_write(hidden_states, attn_out, attn_wod_w, attn_wab_w, attn_wab_b, attn_du_w, attn_du_b)
            mlp_in = rat_read(hidden_states, mlp_read_w, mlp_read_g, mlp_read_b, 2)
            g_in, u_in = (mlp_in[..., :H], mlp_in[..., H:])
            gate = jnp.einsum('bli,oi->blo', g_in, mlp_in_w[0])
            up = jnp.einsum('bli,oi->blo', u_in, mlp_in_w[1])
            mlp_out = jax.nn.silu(gate) * up
            hidden_states = rat_write(hidden_states, mlp_out, mlp_wod_w, mlp_wab_w, mlp_wab_b, mlp_du_w, mlp_du_b)
            return hidden_states
        return layer_forward(hidden_states, position_ids, attn_read_w, attn_read_g, attn_read_b, qkv_w, attn_wod_w, attn_wab_w, attn_wab_b, attn_du_w, attn_du_b, mlp_read_w, mlp_read_g, mlp_read_b, mlp_in_w, mlp_wod_w, mlp_wab_w, mlp_wab_b, mlp_du_w, mlp_du_b)

    def _L0_ffn_ref(x, qweight, lut4, lut8, bias):
        import jax, jax.numpy as jnp
        import numpy as np
        B_L, B_H = (4, 8)
        LIN_SLOPE, LIN_INTER, EST_T = (1.0, 0.0, 64.0)
        BATCH, SEQ, IN_F, OUT_F = (4, 512, 1024, 1024)
        MAX_BITS = 8

        def dequant_kbit(qweight, lut, bit):
            O, I32 = (qweight.shape[1], qweight.shape[2])
            shifts = jnp.arange(32, dtype=jnp.int32)
            idx = jnp.zeros((O, I32 * 32), dtype=jnp.int32)
            for p in range(bit):
                bits = (qweight[p][:, :, None] >> shifts & 1).reshape(O, I32 * 32)
                idx = idx | bits << p
            return jnp.take_along_axis(lut, idx, axis=1)
        e = jnp.linalg.norm(x, axis=-1) * LIN_SLOPE + LIN_INTER
        mask = e > EST_T
        w_l = dequant_kbit(qweight, lut4, B_L)
        w_h = dequant_kbit(qweight, lut8, B_H)
        y_l = jnp.einsum('bsi,oi->bso', x, w_l)
        y_h = jnp.einsum('bsi,oi->bso', x, w_h)
        y = jnp.where(mask[..., None], y_h, y_l) + bias
        return y
    x = x + _L0_attn_ref(_layernorm(x, axis=-1), L0_attn_scales_q, L0_attn_scales_k, L0_attn_scales_v, L0_attn_scales_o, L0_attn_qw_q, L0_attn_qw_k, L0_attn_qw_v, L0_attn_qw_o)
    x = x + _L0_xattn_ref(_layernorm(x, axis=-1), pos_BxS, L0_xattn_attn_read_w, L0_xattn_attn_read_g, L0_xattn_attn_read_b, L0_xattn_qkv_w, L0_xattn_attn_wod_w, L0_xattn_attn_wab_w, L0_xattn_attn_wab_b, L0_xattn_attn_du_w, L0_xattn_attn_du_b, L0_xattn_mlp_read_w, L0_xattn_mlp_read_g, L0_xattn_mlp_read_b, ctx_1024, L0_xattn_mlp_wod_w, L0_xattn_mlp_wab_w, L0_xattn_mlp_wab_b, L0_xattn_mlp_du_w, L0_xattn_mlp_du_b)
    x = x + _L0_ffn_ref(_layernorm(x, axis=-1), L0_ffn_qweight, L0_ffn_lut4, L0_ffn_lut8, L0_ffn_bias)
    return x

_drawn_inputs = setup_inputs


def setup_inputs(seed=0):
    import zlib

    import numpy as np

    out = dict(_drawn_inputs(seed))
    spreads = {'L0_xattn_attn_read_g': (1.0, 0.2),
     'L0_xattn_attn_read_b': (0.0, 0.1),
     'L0_xattn_mlp_read_g': (1.0, 0.2),
     'L0_xattn_mlp_read_b': (0.0, 0.1)}
    factors = {}
    for name, (base, spread) in spreads.items():
        noise = np.random.default_rng([zlib.crc32(name.encode()), seed]).standard_normal(out[name].shape)
        drawn = base * np.exp(spread * noise) if base else spread * noise
        out[name] = jnp.asarray(drawn.astype(out[name].dtype))
    for name, factor in factors.items():
        out[name] = (out[name] * factor).astype(out[name].dtype)
    return out
```

```python
from contextlib import ExitStack

import numpy as np

import concourse.bass as bass
from concourse import mybir

F32 = mybir.dt.float32
F32R = mybir.dt.float32r
BF16 = mybir.dt.bfloat16
I32 = mybir.dt.int32
ALU = mybir.AluOpType
ACT = mybir.ActivationFunctionType
AX = mybir.AxisListType

P = 128
B, S, D = 2, 512, 1024
TOK = B * S
NT = TOK // P
KT = D // P
NH, NKV, HD = 32, 8, 128
REP = NH // NKV
QT = S // P
LN_EPS = 1e-5
ZERO = 8.0
MASKED = 1e30

TILES = [(b, qt) for b in range(B) for qt in (3, 2, 1, 0)]
KVU = 2 * KT // REP


PLACES = 2 * KT + KVU


def slot_units(j, last):
    out = {}
    if not (last and j == REP - 1):
        out.update({kt: ("Q", kt) for kt in range(KT)})
    if not last:
        out.update({KT + i: ("KV"[j * KVU // KT], (j * KVU) % KT + i) for i in range(KVU)})
    out.update({KT + KVU + n: ("O", n) for n in range(KT)})
    return out


def on_scalar(kind, n):
    return n == 0 and kind != "O"


PRO = [("K", n) for n in range(KT)] + [("V", n) for n in range(KT)] + [("Q", n) for n in range(KT)]


class Count:

    def __init__(self, before, each):
        self.before, self.each = before, each

    def at(self, g, k):
        return g * self.each + (self.before + k)


def retire(nc, sems):
    with nc.Block() as block:
        @block.gpsimd
        def _(pool):
            for s in sems:
                pool.sem_clear(s)


def due(eng, sem, value):
    if not isinstance(value, int) or value > 0:
        eng.wait_ge(sem, value)


def attention_program(nc, ctx, a):

    def sb(name, shape, dt=F32, c=ctx):
        return c.enter_context(nc.sbuf_tensor(name, shape, dt))

    def sem(name):
        return ctx.enter_context(nc.semaphore(name))

    acc = sb("acc", [P, KT, TOK])
    ident = sb("ident", [P, P])
    ident_bf = sb("ident_bf", [P, P], BF16)
    with ExitStack() as att:
        zT_hi = sb("zT_hi", [P, KT, TOK], F32R, att)
        zT_lo = sb("zT_lo", [P, KT, TOK], F32R, att)
        mask = sb("mask", [P, P], BF16, att)
        eps = sb("eps", [P, 1], F32, att)
        layernorm_in(nc, a, acc, zT_hi, zT_lo, ident, ident_bf, mask, eps)
        attention_loop(nc, a, acc, zT_hi, zT_lo, ident, ident_bf, mask)
    return acc, ident, ident_bf


def layernorm_in(nc, a, acc, zT_hi, zT_lo, ident, ident_bf, mask, eps):
    x_t = a["x"].rearrange("b (t p) d -> (b t) p d", p=P)
    with ExitStack() as ctx:
        def sb(name, shape, dt=F32):
            return ctx.enter_context(nc.sbuf_tensor(name, shape, dt))

        used = []

        def sem(name):
            used.append(ctx.enter_context(nc.semaphore(name)))
            return used[-1]

        x = sb("ln_x", [P, NT, D])
        z = sb("ln_z", [P, 2, D])
        st = sb("ln_st", [P, NT, 2, 6])
        mv = sb("ln_mv", [P, NT, 2])
        sd = sb("ln_sd", [P, NT])
        r = sb("ln_r", [P, NT])
        t = sb("ln_t", [P, NT])
        pt = ctx.enter_context(nc.psum_tensor("ln_pt", [P, 4, 512], F32))
        loaded = [sem(f"ln_loaded{i}") for i in range(NT)]
        made, var_ready, sd_ready = sem("ln_made"), sem("ln_var"), sem("ln_sd_ready")
        chain, z_ready, turned, hi_done, lo_done = (sem(f"ln_{n}") for n in
                                                    ("chain", "z_ready", "turned", "hi", "lo"))
        ctx.callback(lambda: retire(nc, used))
        block = ctx.enter_context(nc.Block())

        @block.sync
        def _(sp):
            for i in range(NT):
                sp.dma_start(x[:, i, :], x_t[i]).then_inc(loaded[i], 16)

        @block.gpsimd
        def _(pool):
            pool.memset(ident[:], 1.0).then_inc(made, 1)
            pool.memset(mask[:], 0.0).then_inc(made, 1)
            pool.memset(eps[:], LN_EPS).then_inc(made, 1)
            pool.wait_ge(made, 3)
            pool.affine_select(out=ident[:], in_=ident[:], compare_op=ALU.is_equal, fill=0.0, base=0,
                               pattern=[[-1, P]], channel_multiplier=1).then_inc(made, 1)
            pool.affine_select(out=mask[:], in_=mask[:], compare_op=ALU.is_ge, fill=MASKED, base=0,
                               pattern=[[1, P]], channel_multiplier=-1).then_inc(made, 1)
            pool.wait_ge(made, 5)
            pool.tensor_copy(ident_bf[:], ident[:]).then_inc(made, 1)
            pool.memset(acc[:], 0.0).then_inc(made, 1)

        @block.vector
        def _(dve):
            n = [0]

            def link(ins):
                n[0] += 1
                ins.then_inc(chain, 1)
                dve.wait_ge(chain, n[0])

            def stats(i):
                dve.wait_ge(loaded[i], 16)
                for h in range(2):
                    ins = dve.bn_stats(st[:, i, h, :], x[:, i, h * 512:(h + 1) * 512])
                link(ins)
                dve.bn_aggr(mv[:, i, :], st[:, i].rearrange("p h s -> p (h s)")).then_inc(var_ready, 1)

            def normalise(i):
                c = slice(i, i + 1)
                var = mv[:, i, 1:2]
                dve.wait_ge(sd_ready, i + 1)
                link(dve.reciprocal(r[:, c], sd[:, c]))
                link(dve.tensor_scalar(t[:, c], var, LN_EPS, r[:, c], ALU.add, ALU.mult))
                link(dve.tensor_scalar(t[:, c], t[:, c], r[:, c], -0.5, ALU.mult, ALU.mult))
                link(dve.tensor_scalar(t[:, c], t[:, c], 1.5, r[:, c], ALU.add, ALU.mult))
                if i >= 2:
                    dve.wait_ge(turned, 2 * (i - 1))
                dve.tensor_scalar(z[:, i % 2, :], x[:, i, :], mv[:, i, 0:1], t[:, c],
                                  ALU.subtract, ALU.mult).then_inc(z_ready, 1)

            def low(i):
                for h in range(2):
                    dve.wait_ge(hi_done, 2 * i + h + 1)
                    dve.tensor_tensor(zT_lo[:, 4 * h:4 * h + 4, i * P:(i + 1) * P],
                                      pt[:, (2 * i + h) % 4, :].rearrange("p (k c) -> p k c", c=P),
                                      zT_hi[:, 4 * h:4 * h + 4, i * P:(i + 1) * P],
                                      ALU.subtract).then_inc(lo_done, 1)

            stats(0)
            for i in range(NT):
                if i + 1 < NT:
                    stats(i + 1)
                normalise(i)
                if i:
                    low(i - 1)
            low(NT - 1)

        @block.scalar
        def _(act):
            act.wait_ge(made, 3)
            for i in range(NT + 1):
                if i < NT:
                    act.wait_ge(var_ready, i + 1)
                    act.activation(sd[:, i:i + 1], mv[:, i, 1:2], ACT.Sqrt, bias=eps[:]).then_inc(sd_ready, 1)
                if i:
                    for h in range(2):
                        u = 2 * (i - 1) + h
                        act.wait_ge(turned, u + 1)
                        act.activation(zT_hi[:, 4 * h:4 * h + 4, (i - 1) * P:i * P],
                                       pt[:, u % 4, :].rearrange("p (k c) -> p k c", c=P),
                                       ACT.Copy).then_inc(hi_done, 1)

        @block.tensor
        def _(pe):
            pe.wait_ge(made, 4)
            for i in range(NT):
                pe.wait_ge(z_ready, i + 1)
                for h in range(2):
                    u = 2 * i + h
                    if u >= 4:
                        pe.wait_ge(lo_done, u - 3)
                    for k in range(4):
                        c = (4 * h + k) * P
                        ins = pe.transpose(pt[:, u % 4, k * P:(k + 1) * P], z[:, i % 2, c:c + P], ident[:])
                    ins.then_inc(turned, 1)


def attention_loop(nc, a, acc, zT_hi, zT_lo, ident, ident_bf, mask):
    with ExitStack() as ctx:
        def sb(name, shape, dt=F32):
            return ctx.enter_context(nc.sbuf_tensor(name, shape, dt))

        def psum(name, shape):
            return ctx.enter_context(nc.psum_tensor(name, shape, F32))

        used = []

        def sem(name):
            used.append(ctx.enter_context(nc.semaphore(name)))
            return used[-1]

        cos_t, sin_t = sb("cos_t", [P, S]), sb("sin_t", [P, S])
        sc_q, sc_o = sb("sc_q", [P, NH * KT]), sb("sc_o", [P, (NH + 1) * KT])
        sc_k, sc_v = sb("sc_k", [P, NKV * KT]), sb("sc_v", [P, NKV * KT])
        raw_q, raw_o, raw_kv = (sb(f"raw_{n}", [P, D], I32) for n in ("q", "o", "kv"))
        w_q, w_o, w_kv = (sb(f"w_{n}", [P, D], F32R) for n in ("q", "o", "kv"))
        kT, v = sb("kT", [P, 2, TOK]), sb("v", [P, 2, TOK])
        kv_acc, q_acc, swapped, qT = (sb(n, [P, TOK]) for n in ("kv_acc", "q_acc", "swapped", "qT"))
        prob = sb("prob", [P, 4, S])
        probT = sb("probT", [P, B, QT, S])
        ctx_hi, ctx_lo = sb("ctx_hi", [P, 2, TOK], F32R), sb("ctx_lo", [P, 2, TOK], F32R)
        low_max = sb("low_max", [P, len(TILES)])
        total, inv_total = sb("total", [P, len(TILES)]), sb("inv_total", [P, len(TILES)])
        pj = [psum(f"pj{i}", [P, TOK]) for i in range(2)]
        ps = [psum(f"ps{i}", [P, S]) for i in range(2)]
        pt = psum("pt", [P, S])
        pv = psum("pv", [P, S])

        s_tab = sem("s_tab")
        ld_q, ld_o, ld_kv = sem("ld_q"), sem("ld_o"), sem("ld_kv")
        w_q_ready, w_o_ready, w_kv_ready = sem("w_q_ready"), sem("w_o_ready"), sem("w_kv_ready")
        unit_done, evac_v, evac_s = sem("unit_done"), sem("evac_v"), sem("evac_s")
        s_done, max_done, exp_done, inv_done, norm_done = (sem(n) for n in (
            "s_done", "max_done", "exp_done", "inv_done", "norm_done"))
        t_done, t_copied, vt_done, v_copied = (sem(n) for n in ("t_done", "t_copied", "vt_done", "v_copied"))
        pv_done, hi_done, lo_done = sem("pv_done"), sem("ctx_hi_done"), sem("ctx_lo_done")
        q_swapped, q_mul, qT_ready = sem("q_swapped"), sem("q_mul"), sem("qT_ready")
        k_swapped, k_mul, kT_ready = sem("k_swapped"), sem("k_mul"), sem("kT_ready")
        zeroed = sem("zeroed")

        n_units = sum(len(slot_units(j, False)) for j in range(REP))
        unit_c = Count(len(PRO), n_units)
        s_units = REP + 2
        evac_s_c = Count(3, s_units)
        evac_v_c = Count(len(PRO) - 3, n_units - s_units)
        tile_c = Count(0, REP * len(TILES))
        slot_c = Count(0, REP)
        lead_c = Count(1, REP)
        pv_c = Count(0, REP * B)
        wkv_c = Count(3, 2)
        wq_c = Count(2, REP)

        def order(last):
            out, v_n, s_n = [], 0, 0
            for j in range(REP):
                for i, (kind, n) in slot_units(j, last).items():
                    out.append((j, i, kind, n, v_n, s_n))
                    if on_scalar(kind, n):
                        s_n += 1
                    else:
                        v_n += 1
            return out

        def place(last):
            return {(j, kind, n): (u, v_n, s_n)
                    for u, (j, _, kind, n, v_n, s_n) in enumerate(order(last))}

        def groups(eng, emit):
            emit(0, 0, False)
            emit(1, 1, False)
            with eng.Fori(1, NKV // 2 - 1) as i:
                for par in range(2):
                    emit(i * 2 + par, par, False)
            emit(NKV - 2, 0, False)
            emit(NKV - 1, 1, True)

        ctx.callback(lambda: retire(nc, used))
        block = ctx.enter_context(nc.Block())

        @block.sync
        def _(sp):
            for t, name in ((cos_t, "cos"), (sin_t, "sin"), (sc_q, "sc_q"), (sc_k, "sc_k"),
                            (sc_v, "sc_v")):
                sp.dma_start(t[:], a[name]).then_inc(s_tab, 16)
            sp.dma_start(sc_o[:, KT:], a["sc_o"]).then_inc(s_tab, 16)
            sp.dma_start(raw_kv[:], a["w_k"][0]).then_inc(ld_kv, 16)
            sp.dma_start(raw_q[:], a["w_q"][0]).then_inc(ld_q, 16)
            sp.dma_start(raw_o[:], a["w_o"][0]).then_inc(ld_o, 16)
            sp.wait_ge(w_kv_ready, 1)
            sp.dma_start(raw_kv[:], a["w_v"][0]).then_inc(ld_kv, 16)
            sp.wait_ge(w_q_ready, 1)
            sp.dma_start(raw_q[:], a["w_q"][1]).then_inc(ld_q, 16)
            sp.wait_ge(w_kv_ready, 2)
            sp.dma_start(raw_kv[:], a["w_k"][1]).then_inc(ld_kv, 16)
            sp.wait_ge(w_q_ready, 2)
            sp.dma_start(raw_q[:], a["w_q"][2]).then_inc(ld_q, 16)
            sp.wait_ge(w_kv_ready, 3)
            sp.dma_start(raw_kv[:], a["w_v"][1]).then_inc(ld_kv, 16)

            def emit(g, par, last):
                for j in range(REP):
                    due(sp, w_o_ready, slot_c.at(g, j + 1))
                    sp.dma_start(raw_o[:], a["w_o"][g * REP + j]).then_inc(ld_o, 16)
                    if not (last and j > 0):
                        due(sp, w_q_ready, wq_c.at(g, j + 1))
                        sp.dma_start(raw_q[:], a["w_q"][g * REP + (j + 3)]).then_inc(ld_q, 16)
                    if not (isinstance(g, int) and g >= NKV - 2) and j % 2 == 1:
                        due(sp, w_kv_ready, wkv_c.at(g, j // 2 + 1))
                        sp.dma_start(raw_kv[:], a["w_k" if j == 1 else "w_v"][g + 2]).then_inc(ld_kv, 16)

            groups(sp, emit)

        @block.scalar
        def _(act):
            def convert(dst, src, loaded, count, ready):
                due(act, loaded, count)
                act.activation(dst[:], src[:], ACT.Copy, bias=-ZERO).then_inc(ready, 1)

            def scaled_copy(dst, slot, scale, unit):
                due(act, unit_done, unit)
                act.activation(dst[:], pj[slot][:], ACT.Copy, scale=scale).then_inc(evac_s, 1)

            def swap(src, ready_sem, ready, free_sem, free, done):
                due(act, ready_sem, ready)
                due(act, free_sem, free)
                h = HD // 2
                act.activation(swapped[0:h, :], src[h:HD, :], ACT.Copy).then_inc(done, 1)
                act.activation(swapped[h:HD, :], src[0:h, :], ACT.Copy).then_inc(done, 1)

            def copy_v(dst, count):
                for h in range(B):
                    due(act, vt_done, count + h)
                    act.activation(dst[:, h * S:(h + 1) * S], pt[:], ACT.Copy).then_inc(v_copied, 1)

            act.wait_ge(s_tab, 16 * 6)
            convert(w_kv, raw_kv, ld_kv, 16, w_kv_ready)
            convert(w_q, raw_q, ld_q, 16, w_q_ready)
            scaled_copy(kv_acc, 0, sc_k[:, 0:1], 1)
            act.wait_ge(unit_done, KT)
            convert(w_kv, raw_kv, ld_kv, 32, w_kv_ready)
            swap(kv_acc, evac_v, KT - 1, k_mul, 0, k_swapped)
            act.wait_ge(k_mul, 2)
            act.wait_ge(kT_ready, 1)
            scaled_copy(kv_acc, 0, sc_v[:, 0:1], KT + 1)
            act.wait_ge(unit_done, 2 * KT)
            convert(w_kv, raw_kv, ld_kv, 48, w_kv_ready)
            scaled_copy(q_acc, 0, sc_q[:, 0:1], 2 * KT + 1)
            copy_v(v[:, 0, :], 1)
            act.wait_ge(unit_done, 3 * KT)
            convert(w_q, raw_q, ld_q, 32, w_q_ready)
            swap(q_acc, evac_v, 3 * (KT - 1), kT_ready, 1, q_swapped)

            def emit(g, par, last):
                at = place(last)
                for j in range(REP):
                    units = slot_units(j, last)
                    hp = j % 2
                    has_q = ("Q", 0) in units.values()
                    for i in range(PLACES):
                        if i == 0 and has_q:
                            due(act, qT_ready, lead_c.at(g, j))
                            scaled_copy(q_acc, 0, sc_q[:, bass.ds((g * REP + (j + 1)) * KT, 1)],
                                        unit_c.at(g, at[j, "Q", 0][0] + 1))
                        if 1 <= i <= len(TILES):
                            n = i - 1
                            k = j * len(TILES) + n
                            b, qt = TILES[n]
                            w = (qt + 1) * P
                            due(act, max_done, tile_c.at(g, k + 1))
                            due(act, t_done, tile_c.at(g, k - 3))
                            act.activation(prob[:, n % 4, 0:w], ps[n % 2][:, 0:w], ACT.Exp,
                                           bias=low_max[:, n:n + 1], scale=-1.0,
                                           accum_out=total[:, n:n + 1]).then_inc(exp_done, 1)
                        if i == 4:
                            due(act, unit_done, unit_c.at(g, at[j - 1, "O", KT - 1][0] + 1 if j else 0))
                            convert(w_o, raw_o, ld_o, (g * REP + (j + 1)) * 16, w_o_ready)
                        if 4 <= i < 4 + len(TILES):
                            n = i - 4
                            k = j * len(TILES) + n
                            b, qt = TILES[n]
                            due(act, t_done, tile_c.at(g, k + 1))
                            due(act, pv_done, pv_c.at(g, j * B + b - 1))
                            act.activation(probT[:, b, 0:qt + 1, qt * P:(qt + 1) * P],
                                           pt[:, 0:(qt + 1) * P].rearrange("p (k c) -> p k c", c=P),
                                           ACT.Copy).then_inc(t_copied, 1)
                        if i == 8 and ("K", 0) in units.values():
                            scaled_copy(kv_acc, 0, sc_k[:, bass.ds((g + 1) * KT, 1)],
                                        unit_c.at(g, at[j, "K", 0][0] + 1))
                        if i == 8 and ("V", 0) in units.values():
                            due(act, kT_ready, g + 2)
                            scaled_copy(kv_acc, 0, sc_v[:, bass.ds((g + 1) * KT, 1)],
                                        unit_c.at(g, at[j, "V", 0][0] + 1))
                        if i == 9 and has_q:
                            u, v_n, _ = at[j, "Q", KT - 1]
                            due(act, kT_ready, g + 1 if j < 2 else (g + 2 if not last else g + 1))
                            swap(q_acc, evac_v, evac_v_c.at(g, v_n + 1), qT_ready, lead_c.at(g, j), q_swapped)
                        if i == 10 and has_q and not (last and j == REP - 2):
                            due(act, unit_done, unit_c.at(g, at[j, "Q", KT - 1][0] + 1))
                            convert(w_q, raw_q, ld_q, (g * REP + (j + 3)) * 16, w_q_ready)
                        if i in (10, 14):
                            b = (i - 10) // 4
                            due(act, pv_done, pv_c.at(g, j * B + b + 1))
                            act.activation(ctx_hi[:, hp, b * S:(b + 1) * S], pv[:], ACT.Copy).then_inc(hi_done, 1)
                        if i == 15 and not last and j == 1:
                            u, v_n, _ = at[j, "K", KT - 1]
                            due(act, qT_ready, lead_c.at(g, j + 1))
                            swap(kv_acc, evac_v, evac_v_c.at(g, v_n + 1), kT_ready, g + 1, k_swapped)
                        if i == 16 and not last and j % 2 == 1:
                            if j == 1:
                                due(act, unit_done, unit_c.at(g, at[j, "K", KT - 1][0] + 1))
                                convert(w_kv, raw_kv, ld_kv, g * 32 + 64, w_kv_ready)
                            elif not (isinstance(g, int) and g >= NKV - 2):
                                due(act, unit_done, unit_c.at(g, at[j, "V", KT - 1][0] + 1))
                                convert(w_kv, raw_kv, ld_kv, g * 32 + 80, w_kv_ready)
                        if i == 17 and not last and j == REP - 1:
                            copy_v(v[:, 1 - par, :], g * 2 + 3)

            groups(act, emit)
            act.wait_ge(unit_done, unit_c.at(NKV - 1, len(order(True))))
            convert(w_o, raw_o, ld_o, (NH + 1) * 16, w_o_ready)

        @block.vector
        def _(dve):
            def add_unit(dst, slot, scale, unit, evac, ready=None):
                due(dve, unit_done, unit)
                due(dve, evac_v, evac)
                dve.scalar_tensor_tensor(out=dst, in0=pj[slot][:], scalar=scale, in1=dst,
                                         op0=ALU.mult, op1=ALU.add).then_inc(evac_v, 1)

            def finish_k(count, dst):
                due(dve, k_mul, 2 * count)
                dve.scalar_tensor_tensor(out=dst, in0=kv_acc[:], scalar=-1.0, in1=swapped[:],
                                         op0=ALU.mult, op1=ALU.subtract).then_inc(kT_ready, 1)

            dve.memset(ctx_hi[:, 1, :].bitcast(F32), 0.0).then_inc(zeroed, 1)
            dve.memset(ctx_lo[:, 1, :].bitcast(F32), 0.0).then_inc(zeroed, 1)
            dve.memset(sc_o[:, 0:KT], 0.0).then_inc(zeroed, 1)
            dve.wait_ge(zeroed, 3)
            dve.wait_ge(s_tab, 16 * 6)
            v_n = 0
            for u, (kind, n) in enumerate(PRO):
                if kind == "V" and n == 1:
                    finish_k(1, kT[:, 0, :])
                if n == 0:
                    continue
                if n == 1:
                    dve.wait_ge(evac_s, "KVQ".index(kind) + 1)
                dst, sc = {"K": (kv_acc, sc_k), "V": (kv_acc, sc_v), "Q": (q_acc, sc_q)}[kind]
                add_unit(dst[:], u % 2, sc[:, n:n + 1], u + 1, v_n if n > 1 else 0)
                v_n += 1

            def emit(g, par, last):
                at = place(last)
                for j in range(REP):
                    units = slot_units(j, last)
                    hp = j % 2
                    for i in range(PLACES):
                        if i < len(TILES):
                            k = j * len(TILES) + i
                            b, qt = TILES[i]
                            due(dve, s_done, tile_c.at(g, k + 1))
                            dve.tensor_reduce(low_max[:, i:i + 1], ps[i % 2][:, 0:(qt + 1) * P],
                                              AX.X, ALU.min).then_inc(max_done, 1)
                        if 2 <= i < 2 + len(TILES):
                            n = i - 2
                            k = j * len(TILES) + n
                            due(dve, exp_done, tile_c.at(g, k + 1))
                            due(dve, norm_done, tile_c.at(g, k + 1 - len(TILES)))
                            dve.reciprocal(inv_total[:, n:n + 1], total[:, n:n + 1]).then_inc(inv_done, 1)
                        if i in units:
                            kind, n = units[i]
                            u, v_n, s_n = at[j, kind, n]
                            if not on_scalar(kind, n):
                                if n == 1 and kind != "O":
                                    due(dve, evac_s, evac_s_c.at(g, s_n))
                                sc, col, dst = {
                                    "Q": (sc_q, (g * REP + (j + 1)) * KT + n, q_acc[:]),
                                    "K": (sc_k, (g + 1) * KT + n, kv_acc[:]),
                                    "V": (sc_v, (g + 1) * KT + n, kv_acc[:]),
                                    "O": (sc_o, (g * REP + j) * KT + n, acc[:, n, :])}[kind]
                                add_unit(dst, i % 2, sc[:, bass.ds(col, 1)], unit_c.at(g, u + 1),
                                         evac_v_c.at(g, v_n - KT if kind == "O" else v_n))
                        if i in (11, 15):
                            b = (i - 11) // 4
                            due(dve, hi_done, pv_c.at(g, j * B + b + 1))
                            dve.tensor_tensor(ctx_lo[:, hp, b * S:(b + 1) * S], pv[:],
                                              ctx_hi[:, hp, b * S:(b + 1) * S].bitcast(F32),
                                              ALU.subtract).then_inc(lo_done, 1)
                    if j == 1 and not last:
                        finish_k(g + 2, kT[:, 1 - par, :])

            groups(dve, emit)
            base = len(order(True))
            v_end = sum(1 for o in order(True) if not on_scalar(o[2], o[3]))
            for n in range(KT):
                add_unit(acc[:, n, :], n % 2, sc_o[:, NH * KT + n:NH * KT + n + 1],
                         unit_c.at(NKV - 1, base + n + 1), evac_v_c.at(NKV - 1, v_end + n - KT))

        @block.gpsimd
        def _(pool):
            def rope_mul(dst, swapped_sem, swapped_count, mul):
                due(pool, swapped_sem, swapped_count)
                for t, tab in ((swapped, sin_t), (dst, cos_t)):
                    t2 = t[:].rearrange("p (b s) -> p b s", b=B)
                    pool.tensor_tensor(t2, t2, tab[:].unsqueeze(1).to_broadcast([P, B, S]),
                                       ALU.mult).then_inc(mul, 1)

            def rope_q(count, free):
                rope_mul(q_acc, q_swapped, 2 * count if isinstance(count, int) else count * 2, q_mul)
                due(pool, q_mul, 2 * count if isinstance(count, int) else count * 2)
                due(pool, s_done, free)
                pool.tensor_tensor(qT[:], q_acc[:], swapped[:], ALU.add).then_inc(qT_ready, 1)

            pool.wait_ge(s_tab, 16 * 6)
            rope_mul(kv_acc, k_swapped, 2, k_mul)
            rope_q(1, 0)

            def emit(g, par, last):
                for j in range(REP):
                    has_q = ("Q", 0) in slot_units(j, last).values()
                    for n, (b, qt) in enumerate(TILES):
                        k = j * len(TILES) + n
                        w = (qt + 1) * P
                        due(pool, inv_done, tile_c.at(g, k + 1))
                        pool.tensor_tensor(prob[:, n % 4, 0:w], prob[:, n % 4, 0:w],
                                           inv_total[:, n:n + 1].to_broadcast([P, w]),
                                           ALU.mult).then_inc(norm_done, 1)
                    if has_q:
                        rope_q(lead_c.at(g, j + 1), tile_c.at(g, (j + 1) * len(TILES)))
                    if j == 1 and not last:
                        rope_mul(kv_acc, k_swapped, (g + 2) * 2, k_mul)

            groups(pool, emit)

        @block.tensor
        def _(pe):
            def unit(slot, lhs, parts, count, free_v, free_s=None):
                due(pe, evac_v, free_v)
                if free_s is not None:
                    due(pe, evac_s, free_s)
                for b in range(B):
                    for n, part in enumerate(parts):
                        ins = pe.matmul(pj[slot][:, b * S:(b + 1) * S], lhs, part[:, b * S:(b + 1) * S],
                                        start=n == 0, stop=n == 1)
                ins.then_inc(unit_done, 1)

            def z_parts(kt):
                return zT_hi[:, kt, :], zT_lo[:, kt, :]

            def turn_v(free_copied, free_t, evac):
                for h in range(B):
                    due(pe, v_copied, free_copied + h)
                    if h == 0:
                        due(pe, t_copied, free_t)
                        due(pe, evac_v, evac)
                    for c in range(QT):
                        ins = pe.transpose(pt[:, c * P:(c + 1) * P],
                                           kv_acc[:, h * S + c * P:h * S + (c + 1) * P], ident[:])
                    ins.then_inc(vt_done, 1)

            evacs_v = evacs_s = 0
            done = []
            for u, (kind, n) in enumerate(PRO):
                if n == 0:
                    if kind == "Q":
                        pe.wait_ge(w_q_ready, 1)
                    else:
                        pe.wait_ge(w_kv_ready, "KV".index(kind) + 1)
                fv, fs = done[u - 2] if u >= 2 else (0, 0)
                unit(u % 2, (w_q if kind == "Q" else w_kv)[:, n * P:(n + 1) * P], z_parts(n), u + 1, fv, fs)
                if on_scalar(kind, n):
                    evacs_s += 1
                else:
                    evacs_v += 1
                done.append((evacs_v, evacs_s))
            turn_v(0, 0, 2 * (KT - 1))
            pe.wait_ge(zeroed, 3)

            def emit(g, par, last):
                at = place(last)
                flat = order(last)
                for j in range(REP):
                    units = slot_units(j, last)
                    hp = j % 2
                    for i in range(PLACES):
                        if i < len(TILES):
                            b, qt = TILES[i]
                            k = j * len(TILES) + i
                            if i == 0:
                                due(pe, qT_ready, lead_c.at(g, j))
                                if j == 0:
                                    due(pe, kT_ready, g + 1)
                            due(pe, exp_done, tile_c.at(g, k - 1))
                            w = (qt + 1) * P
                            pe.matmul(ps[i % 2][:, 0:w], qT[:, b * S + qt * P:b * S + (qt + 1) * P],
                                      kT[:, par, b * S:b * S + w], start=True, stop=False)
                            pe.matmul(ps[i % 2][:, qt * P:w], mask_neg, ident_bf[:],
                                      start=False, stop=True).then_inc(s_done, 1)
                        if 3 <= i < 3 + len(TILES):
                            n = i - 3
                            b, qt = TILES[n]
                            k = j * len(TILES) + n
                            due(pe, norm_done, tile_c.at(g, k + 1))
                            due(pe, t_copied, tile_c.at(g, k))
                            if n == 0 and j == 0:
                                due(pe, v_copied, g * 2 + 2)
                            for c in range(qt + 1):
                                ins = pe.transpose(pt[:, c * P:(c + 1) * P], prob[:, n % 4, c * P:(c + 1) * P],
                                                   ident[:])
                            ins.then_inc(t_done, 1)
                        if i in (8, 12):
                            b = (i - 8) // 4
                            due(pe, t_copied, tile_c.at(g, j * len(TILES) + 4 * (b + 1)))
                            due(pe, hi_done, pv_c.at(g, j * B + b))
                            due(pe, lo_done, pv_c.at(g, j * B + b))
                            for c in range(QT):
                                ins = pe.matmul(pv[:, c * P:S], v[:, par, b * S + c * P:b * S + (c + 1) * P],
                                                probT[:, b, c, c * P:S], start=c == 0, stop=c == QT - 1)
                            ins.then_inc(pv_done, 1)
                        if i in units:
                            kind, n = units[i]
                            u, v_n, s_n = at[j, kind, n]
                            if kind == "Q" and n == 0:
                                due(pe, w_q_ready, wq_c.at(g, j))
                            if kind == "K" and n == 0:
                                due(pe, w_kv_ready, g * 2 + 3)
                            if kind == "V" and n == 0:
                                due(pe, w_kv_ready, g * 2 + 4)
                            if kind == "O" and n == 0:
                                due(pe, w_o_ready, slot_c.at(g, j + 1))
                                due(pe, hi_done, pv_c.at(g, j * B))
                                due(pe, lo_done, pv_c.at(g, j * B))
                            if kind == "O":
                                lhs, parts = w_o, (ctx_hi[:, 1 - hp, :], ctx_lo[:, 1 - hp, :])
                            else:
                                lhs, parts = (w_q if kind == "Q" else w_kv), z_parts(n)
                            if u >= 2:
                                p = flat[u - 2]
                                own_s = on_scalar(p[2], p[3])
                                fv, fs = p[4] + (not own_s), p[5] + own_s
                            else:
                                fv, fs, own_s = u - 1, 0, False
                            unit(i % 2, lhs[:, n * P:(n + 1) * P], parts, None, evac_v_c.at(g, fv),
                                 evac_s_c.at(g, fs) if own_s else None)
                        if i == 14 and j == REP - 1 and not last:
                            turn_v(g * 2 + 2, tile_c.at(g, REP * len(TILES)),
                                   evac_v_c.at(g, at[j, "V", KT - 1][1] + 1))

            mask_neg = mask[:]
            groups(pe, emit)
            n_last = len(order(True))
            v_end = sum(1 for o in order(True) if not on_scalar(o[2], o[3]))
            pe.wait_ge(w_o_ready, NH + 1)
            pe.wait_ge(hi_done, NH * B)
            pe.wait_ge(lo_done, NH * B)
            for n in range(KT):
                unit(n % 2, w_o[:, n * P:(n + 1) * P], (ctx_hi[:, 1, :], ctx_lo[:, 1, :]), None,
                     evac_v_c.at(NKV - 1, v_end + n - 1))


XH, XC = 256, 4
IC = XH // P
XNH, XHD = 16, 16
RH, HS = 16, 16
DR = 8
M = 1024
MT = M // P
N_B, N_SKIP, N_A = RH * (XC - 1), RH, RH * (XC - 1)
C_DL, C_B, C_SKIP, C_A = XH, XH + DR, XH + DR + N_B, XH + DR + N_B + N_SKIP
OD = C_A + N_A
SP = N_A + XH
PARTS = 4
SSM_EPS = 1e-5
TWO_PI = 2.0 * np.pi
PI_A, PI_B = 6.28125, float(np.float32(TWO_PI - 6.28125))
PI_C = float(np.float32(TWO_PI - 6.28125 - float(np.float32(TWO_PI - 6.28125))))
PI = 3.1415925


class Chain:

    def __init__(self, eng, sem):
        self.eng, self.sem, self.n = eng, sem, 0

    def __call__(self, ins):
        self.n += 1
        ins.then_inc(self.sem, 1)
        self.eng.wait_ge(self.sem, self.n)


def scope(nc, ctx):
    def sb(name, shape, dt=F32):
        return ctx.enter_context(nc.sbuf_tensor(name, shape, dt))

    def psum(name, shape, dt=F32):
        return ctx.enter_context(nc.psum_tensor(name, shape, dt))

    def sem(name):
        return ctx.enter_context(nc.semaphore(name))

    return sb, psum, sem


def rsqrt_newton(dve, link, r, sd, var, t, eps):
    link(dve.reciprocal(r, sd))
    link(dve.tensor_scalar(t, var, eps, None, ALU.add))
    link(dve.tensor_tensor(t, t, r, ALU.mult))
    link(dve.tensor_tensor(t, t, r, ALU.mult))
    link(dve.tensor_scalar(t, t, -0.5, 1.5, ALU.mult, ALU.add))
    link(dve.tensor_tensor(t, t, r, ALU.mult))


def residual_norm(nc, a, acc, ident, eps, x1, h):
    x_t = a["x"].rearrange("b (t p) d -> (b t) p d", p=P)
    with ExitStack() as ctx:
        sb, psum, sem = scope(nc, ctx)
        st, mv = sb("r_st", [P, NT, 2, 6]), sb("r_mv", [P, NT, 2])
        sd, r, t = sb("r_sd", [P, NT]), sb("r_r", [P, NT]), sb("r_t", [P, NT])
        pt = [psum(f"r_pt{i}", [P, D]) for i in range(2)]
        loaded = [sem(f"r_loaded{i}") for i in range(NT)]
        chain, turned, added, var_ready, sd_ready, done = (sem(f"r_{n}") for n in (
            "chain", "turned", "added", "var", "sd", "done"))
        block = ctx.enter_context(nc.Block())

        @block.sync
        def _(sp):
            for i in range(NT):
                sp.dma_start(x1[:, i, :], x_t[i]).then_inc(loaded[i], 16)

        @block.tensor
        def _(pe):
            for i in range(NT):
                if i >= 2:
                    pe.wait_ge(added, i - 1)
                for k in range(KT):
                    ins = pe.transpose(pt[i % 2][:, k * P:(k + 1) * P], acc[:, k, i * P:(i + 1) * P], ident[:])
                ins.then_inc(turned, 1)

        @block.scalar
        def _(act):
            for i in range(NT):
                act.wait_ge(var_ready, i + 1)
                act.activation(sd[:, i:i + 1], mv[:, i, 1:2], ACT.Sqrt, bias=eps[:]).then_inc(sd_ready, 1)

        @block.vector
        def _(dve):
            link = Chain(dve, chain)

            def finish(i):
                c = slice(i, i + 1)
                dve.wait_ge(sd_ready, i + 1)
                rsqrt_newton(dve, link, r[:, c], sd[:, c], mv[:, i, 1:2], t[:, c], LN_EPS)
                dve.tensor_scalar(h[:, i, :], x1[:, i, :], mv[:, i, 0:1], t[:, c],
                                  ALU.subtract, ALU.mult).then_inc(done, 1)

            for i in range(NT):
                dve.wait_ge(loaded[i], 16)
                dve.wait_ge(turned, i + 1)
                dve.tensor_tensor(x1[:, i, :], pt[i % 2][:], x1[:, i, :], ALU.add).then_inc(added, 1)
                dve.wait_ge(added, i + 1)
                dve.bn_stats(st[:, i, 0, :], x1[:, i, 0:512])
                link(dve.bn_stats(st[:, i, 1, :], x1[:, i, 512:1024]))
                dve.bn_aggr(mv[:, i, :], st[:, i].rearrange("p h s -> p (h s)")).then_inc(var_ready, 1)
                if i:
                    finish(i - 1)
            finish(NT - 1)


def rat_read(nc, name, h, rw, gam, bet, n_out, ident, eps, half_mask, inT):
    W = n_out * 32
    with ExitStack() as ctx:
        sb, psum, sem = scope(nc, ctx)
        wbd = sb(name + "wbd", [P, KT, n_out, 32])
        hT = [sb(f"{name}hT{i}", [P, D]) for i in range(2)]
        yn = [sb(f"{name}yn{i}", [P, n_out * XH]) for i in range(2)]
        st, mv = sb(name + "st", [P, NT, n_out, 6]), sb(name + "mv", [P, NT, n_out, 2])
        sd, r, t = (sb(name + n, [P, NT, n_out]) for n in ("sd", "r", "t"))
        p_h = [psum(f"{name}ph{i}", [P, 512]) for i in range(2)]
        p_y = [psum(f"{name}py{i}", [P, 2, 512]) for i in range(2)]
        p_t = [psum(f"{name}pt{i}", [P, 512]) for i in range(2)]
        made, chain, ht, hc, ydone, var_ready, sd_ready, yn_done, yt, yc = (sem(name + n) for n in (
            "made", "chain", "ht", "hc", "ydone", "var", "sdr", "yn_done", "yt", "yc"))
        block = ctx.enter_context(nc.Block())
        nb = n_out * IC

        def y_view(i, o):
            return p_y[i % 2][:, :, 0:4 * W].rearrange(
                "p b (k o j) -> p b k o j", o=n_out, j=32)[:, :, :, o, :]

        @block.gpsimd
        def _(pool):
            for k in range(KT):
                ins = pool.tensor_tensor(
                    wbd[:, k], rw[:, k * n_out:(k + 1) * n_out].unsqueeze(2).to_broadcast([P, n_out, 32]),
                    half_mask[:].unsqueeze(1).to_broadcast([P, n_out, 32]), ALU.mult)
            ins.then_inc(made, 1)

        @block.tensor
        def _(pe):
            def turn_h(i):
                for g in range(2):
                    u = 2 * i + g
                    if u >= 2:
                        pe.wait_ge(hc, u - 1)
                    for k in range(4):
                        c = (4 * g + k) * P
                        ins = pe.transpose(p_h[g][:, k * P:(k + 1) * P], h[:, i, c:c + P], ident[:])
                    ins.then_inc(ht, 1)

            def products(i):
                pe.wait_ge(hc, 2 * i + 2)
                if i >= 2:
                    pe.wait_ge(yn_done, n_out * (i - 1))
                for k in range(KT):
                    ins = pe.matmul(p_y[i % 2][:, k // 4, (k % 4) * W:(k % 4 + 1) * W],
                                    hT[i % 2][:, k * P:(k + 1) * P], wbd[:, k].rearrange("p o j -> p (o j)"),
                                    start=True, stop=True)
                ins.then_inc(ydone, 1)

            def turn_y(i):
                pe.wait_ge(yn_done, n_out * (i + 1))
                for b in range(2):
                    n0, n1 = (0, min(4, nb)) if b == 0 else (4, nb)
                    if n1 <= n0:
                        continue
                    if i:
                        pe.wait_ge(yc, nb * (i - 1) + n1)
                    for n in range(n0, n1):
                        ins = pe.transpose(p_t[b][:, (n - n0) * P:(n - n0 + 1) * P],
                                           yn[i % 2][:, n * P:(n + 1) * P], ident[:])
                        ins.then_inc(yt, 1)

            pe.wait_ge(made, 1)
            turn_h(0)
            for i in range(NT):
                products(i)
                if i + 1 < NT:
                    turn_h(i + 1)
                if i:
                    turn_y(i - 1)
            turn_y(NT - 1)

        @block.vector
        def _(dve):
            link = Chain(dve, chain)

            def finish(i):
                dve.wait_ge(sd_ready, i + 1)
                rsqrt_newton(dve, link, r[:, i], sd[:, i], mv[:, i, :, 1], t[:, i], LN_EPS)
                if i >= 2:
                    dve.wait_ge(yt, nb * (i - 1))
                for o in range(n_out):
                    dve.tensor_scalar(yn[i % 2][:, o * XH:(o + 1) * XH].rearrange("p (b k j) -> p b k j", b=2, j=32),
                                      y_view(i, o), mv[:, i, o, 0:1], t[:, i, o:o + 1],
                                      ALU.subtract, ALU.mult).then_inc(yn_done, 1)

            for i in range(NT):
                dve.wait_ge(ydone, i + 1)
                for o in range(n_out):
                    ins = dve.bn_stats(st[:, i, o, :], y_view(i, o))
                link(ins)
                for o in range(n_out):
                    ins = dve.bn_aggr(mv[:, i, o, :], st[:, i, o, :])
                ins.then_inc(var_ready, 1)
                if i:
                    finish(i - 1)
            finish(NT - 1)

        @block.scalar
        def _(act):
            def copy_h(i):
                for g in range(2):
                    act.wait_ge(ht, 2 * i + g + 1)
                    if i >= 2 and g == 0:
                        act.wait_ge(ydone, i - 1)
                    act.activation(hT[i % 2][:, g * 512:(g + 1) * 512], p_h[g][:], ACT.Copy).then_inc(hc, 1)

            def root(i):
                act.wait_ge(var_ready, i + 1)
                act.activation(sd[:, i], mv[:, i, :, 1], ACT.Sqrt, bias=eps[:]).then_inc(sd_ready, 1)

            def copy_y(i):
                for n in range(nb):
                    act.wait_ge(yt, nb * i + min(4 * (n // 4) + 4, nb))
                    act.activation(inT[:, n, i * P:(i + 1) * P], p_t[n // 4][:, (n % 4) * P:(n % 4 + 1) * P],
                                   ACT.Identity, bias=bet[:, n:n + 1], scale=gam[:, n:n + 1]).then_inc(yc, 1)

            copy_h(0)
            for i in range(NT):
                if i + 1 < NT:
                    copy_h(i + 1)
                root(i)
                if i:
                    copy_y(i - 1)
            copy_y(NT - 1)


def rope_angles(nc, pos, inv, ang_cos, ang_sin):
    with ExitStack() as ctx:
        sb, psum, sem = scope(nc, ctx)
        posf, ang, n_i, n_f, red, over = (sb("a_pos", [P, NT]), sb("a_ang", [P, NT, 8]),
                                          sb("a_ni", [P, NT, 8], I32), sb("a_nf", [P, NT, 8]),
                                          sb("a_red", [P, 2, NT, 8]), sb("a_over", [P, NT, 8]))
        chain, ready = sem("a_chain"), sem("a_ready")
        block = ctx.enter_context(nc.Block())

        @block.vector
        def _(dve):
            link = Chain(dve, chain)
            link(dve.tensor_copy(posf[:], pos[:]))
            link(dve.tensor_tensor(ang[:], posf[:].unsqueeze(2).to_broadcast([P, NT, 8]),
                                   inv[:].unsqueeze(1).to_broadcast([P, NT, 8]), ALU.mult))
            link(dve.tensor_scalar(n_i[:], ang[:], 1.0 / TWO_PI, None, ALU.mult))
            link(dve.tensor_copy(n_f[:], n_i[:]))
            s = red[:, 0]
            link(dve.scalar_tensor_tensor(out=s, in0=n_f[:], scalar=-PI_A, in1=ang[:], op0=ALU.mult, op1=ALU.add))
            link(dve.scalar_tensor_tensor(out=s, in0=n_f[:], scalar=-PI_B, in1=s, op0=ALU.mult, op1=ALU.add))
            link(dve.scalar_tensor_tensor(out=s, in0=n_f[:], scalar=-PI_C, in1=s, op0=ALU.mult, op1=ALU.add))
            c = red[:, 1]
            link(dve.tensor_scalar(c, s, TWO_PI / 4, None, ALU.add))
            for v in (c, s):
                link(dve.tensor_scalar(over[:], v, PI, -TWO_PI, ALU.is_gt, ALU.mult))
                link(dve.tensor_tensor(v, v, over[:], ALU.add))
                link(dve.tensor_scalar(over[:], v, -PI, TWO_PI, ALU.is_lt, ALU.mult))
                link(dve.tensor_tensor(v, v, over[:], ALU.add))
                ins = dve.tensor_scalar(v, v, PI, -PI, ALU.min, ALU.max)
                link(ins)
            dve.tensor_copy(over[:], s).then_inc(ready, 1)

        @block.scalar
        def _(act):
            act.wait_ge(ready, 1)
            act.activation(ang_sin[:], red[:, 0], ACT.Sin)
            act.activation(ang_cos[:], red[:, 1], ACT.Sin)


def project_qkv(nc, inT, qkvT, ang_cos, ang_sin, ident, ident_r, qT, kT, v_aug):
    with ExitStack() as ctx:
        sb, psum, sem = scope(nc, ctx)
        t1 = sb("p_t1", [P, 2, XNH, 2, 8])
        t2 = sb("p_t2", [P, 2, XNH, 2, 8])
        qs = [sb(f"p_qs{i}", [P, 2, XNH, PARTS, XHD], F32R) for i in range(2)]
        p_q = [psum(f"p_proj{i}", [P, 2, 512]) for i in range(2)]
        p_t = [psum(f"p_turn{i}", [P, 1024], F32R) for i in range(2)]
        chain, proj, parts, turned, copied, v_done, prod = (sem(f"p_{n}") for n in (
            "chain", "proj", "parts", "turned", "copied", "v", "prod"))
        ones = sem("p_ones")
        block = ctx.enter_context(nc.Block())

        @block.gpsimd
        def _(pool):
            pool.memset(v_aug[:, :, :, XHD:XHD + 1], 1.0).then_inc(ones, 1)

        @block.tensor
        def _(pe):
            def project(i):
                if i >= 2:
                    pe.wait_ge(prod, i - 1)
                    pe.wait_ge(v_done, i - 1)
                for o in range(3):
                    for ic in range(IC):
                        ins = pe.matmul(p_q[i % 2][:, o // 2, (o % 2) * XH:(o % 2 + 1) * XH],
                                        inT[:, o * IC + ic, i * P:(i + 1) * P],
                                        qkvT[:, ic, o * XH:(o + 1) * XH], start=ic == 0, stop=ic == IC - 1)
                ins.then_inc(proj, 1)

            def turn(i):
                pe.wait_ge(parts, i + 1)
                for w in range(2):
                    u = 2 * i + w
                    if u >= 2:
                        pe.wait_ge(copied, u - 1)
                    for n in range(XNH // 2):
                        ins = pe.transpose(p_t[w][:, n * P:(n + 1) * P],
                                           qs[i % 2][:, w, 2 * n:2 * n + 2].rearrange("p a b c -> p (a b c)"),
                                           ident_r[:])
                    ins.then_inc(turned, 1)

            project(0)
            for i in range(NT):
                if i + 1 < NT:
                    project(i + 1)
                turn(i)

        @block.vector
        def _(dve):
            link = Chain(dve, chain)
            for i in range(NT):
                x = p_q[i % 2][:, 0, :].rearrange("p (w n f) -> p (w n) f", w=2, f=XHD)
                y1 = t1[:].rearrange("p w n f e -> p (w n) f e")
                y2 = t2[:].rearrange("p w n f e -> p (w n) f e")
                cb = ang_cos[:, i, :].unsqueeze(1).to_broadcast([P, 2 * XNH, 8])
                sb_ = ang_sin[:, i, :].unsqueeze(1).to_broadcast([P, 2 * XNH, 8])
                dve.wait_ge(proj, i + 1)
                if i:
                    dve.wait_ge(parts, i)
                dve.tensor_tensor(y1[:, :, 0, :], x[:, :, 0:8], cb, ALU.mult)
                dve.tensor_tensor(y1[:, :, 1, :], x[:, :, 8:16], cb, ALU.mult)
                dve.tensor_tensor(y2[:, :, 0, :], x[:, :, 8:16], sb_, ALU.mult)
                ins = dve.tensor_tensor(y2[:, :, 1, :], x[:, :, 0:8], sb_, ALU.mult)
                ins.then_inc(prod, 1)
                dve.wait_ge(prod, i + 1)
                dve.tensor_tensor(y1[:, :, 0, :], y1[:, :, 0, :], y2[:, :, 0, :], ALU.subtract)
                link(dve.tensor_tensor(y1[:, :, 1, :], y1[:, :, 1, :], y2[:, :, 1, :], ALU.add))
                if i >= 2:
                    dve.wait_ge(turned, 2 * (i - 1))
                full = t1[:].rearrange("p w n f e -> p w n (f e)")
                q_in = full[:, 0].unsqueeze(2).to_broadcast([P, XNH, 2, XHD])
                k_in = full[:, 1].unsqueeze(2).to_broadcast([P, XNH, 2, XHD])
                q_s, k_s = qs[i % 2][:, 0], qs[i % 2][:, 1]
                dve.tensor_copy(q_s[:, :, 0:2, :], q_in)
                link(dve.tensor_copy(k_s[:, :, 0:4:2, :], k_in))
                dve.tensor_tensor(q_s[:, :, 2:4, :], q_in, q_s[:, :, 0:2, :], ALU.subtract)
                dve.tensor_tensor(k_s[:, :, 1:4:2, :], k_in, k_s[:, :, 0:4:2, :], ALU.subtract).then_inc(parts, 1)

        @block.scalar
        def _(act):
            act.wait_ge(ones, 1)
            for i in range(NT):
                act.wait_ge(proj, i + 1)
                act.activation(v_aug[:, i, :, 0:XHD], p_q[i % 2][:, 1, 0:XH].rearrange("p (n f) -> p n f", f=XHD),
                               ACT.Copy).then_inc(v_done, 1)
                for w, dst in enumerate((qT, kT)):
                    act.wait_ge(turned, 2 * i + w + 1)
                    act.activation(dst[:, :, i * P:(i + 1) * P],
                                   p_t[w][:].bitcast(F32).rearrange("p (n c) -> p n c", c=P), ACT.Copy).then_inc(copied, 1)


def cross_attention(nc, qT, kT, v_aug, mask, sel, ident_r, ident_bf, pT, o_all):
    scale = XHD ** -0.5
    with ExitStack() as ctx:
        sb, psum, sem = scope(nc, ctx)
        mx = sb("x_mx", [P, B, QT, XNH])
        ms = sb("x_ms", [P, B, QT, 2, XNH], F32R)
        mT = sb("x_mT", [2 * XNH, B, S], F32R)
        rt = sb("x_rt", [P, QT, XNH])
        ps = [psum(f"x_ps{i}", [P, 512]) for i in range(2)]
        pe_ = [psum(f"x_pe{i}", [P, 512]) for i in range(2)]
        po = [psum(f"x_po{i}", [P, 512]) for i in range(QT)]
        s_done, m_done, ms_done, mt_done, mt_copied, e_done, exp_done, pv_done, o_done, chain, r_done = (
            sem(f"x_{n}") for n in ("s", "m", "ms", "mt", "mtc", "e", "exp", "pv", "o", "chain", "r"))
        block = ctx.enter_context(nc.Block())

        def rows(n):
            return slice(64 * (n % 2), 64 * (n % 2) + 64)

        @block.tensor
        def _(pe):
            def maxima(b, n):
                for qt in range(QT):
                    u = (b * XNH + n) * QT + qt
                    if u >= 2:
                        pe.wait_ge(m_done, u - 1)
                    w = (qt + 1) * P
                    q0 = b * S + qt * P
                    pe.matmul(ps[u % 2][:, 0:w], qT[rows(n), n // 2, q0:q0 + P], kT[rows(n), n // 2, b * S:b * S + w],
                              start=True, stop=False)
                    pe.matmul(ps[u % 2][:, qt * P:w], mask[:], ident_bf[:], start=False, stop=True).then_inc(s_done, 1)

            def turn_maxima(b):
                pe.wait_ge(ms_done, b + 1)
                for qt in range(QT):
                    ins = pe.transpose(ps[0][0:2 * XNH, qt * P:(qt + 1) * P].bitcast(F32R),
                                       ms[:, b, qt].rearrange("p a n -> p (a n)"), ident_r[:])
                ins.then_inc(mt_done, 1)
                pe.wait_ge(mt_copied, b + 1)

            def scores(b, n):
                for kt in range(QT):
                    u = (b * XNH + n) * QT + kt
                    if u >= 2:
                        pe.wait_ge(exp_done, u - 1)
                    k0 = b * S + kt * P
                    w = S - kt * P
                    pe.matmul(pe_[u % 2][:, 0:w], kT[rows(n), n // 2, k0:k0 + P], qT[rows(n), n // 2, k0:b * S + S],
                              start=True, stop=False)
                    pe.matmul(pe_[u % 2][:, 0:w], sel[:, n, :], mT[:, b, kt * P:S], start=False, stop=False)
                    pe.matmul(pe_[u % 2][:, 0:P], ident_bf[:], mask[:], start=False, stop=True).then_inc(e_done, 1)

            def weigh(b, n):
                pe.wait_ge(exp_done, (b * XNH + n + 1) * QT)
                if n == 0 and b:
                    pe.wait_ge(o_done, b * QT)
                for qt in range(QT):
                    for kt in range(qt + 1):
                        ins = pe.matmul(po[qt][:, n * 17:n * 17 + 17], pT[n % 2][:, kt, qt * P:(qt + 1) * P],
                                        v_aug[:, b * QT + kt, n, :], start=kt == 0, stop=kt == qt)
                ins.then_inc(pv_done, 1)

            for n in range(XNH):
                maxima(0, n)
            for b in range(B):
                turn_maxima(b)
                for n in range(XNH):
                    scores(b, n)
                    if b + 1 < B:
                        maxima(b + 1, n)
                    if n:
                        weigh(b, n - 1)
                weigh(b, XNH - 1)

        def finish(dve, link, b):
            dve.wait_ge(pv_done, (b + 1) * XNH)
            for qt in range(QT):
                o = po[qt][:, 0:XNH * 17].rearrange("p (n f) -> p n f", f=17)
                link(dve.reciprocal(rt[:, qt, :], o[:, :, 16]))
                dve.tensor_tensor(o_all[:, b * QT + qt].rearrange("p (n f) -> p n f", f=XHD), o[:, :, 0:16],
                                  rt[:, qt, :].unsqueeze(2).to_broadcast([P, XNH, XHD]), ALU.mult).then_inc(o_done, 1)

        @block.vector
        def _(dve):
            link = Chain(dve, chain)
            for b in range(B):
                for n in range(XNH):
                    for qt in range(QT):
                        u = (b * XNH + n) * QT + qt
                        dve.wait_ge(s_done, u + 1)
                        dve.tensor_reduce(mx[:, b, qt, n:n + 1], ps[u % 2][:, 0:(qt + 1) * P],
                                          AX.X, ALU.max).then_inc(m_done, 1)
                dve.wait_ge(m_done, (b + 1) * XNH * QT)
                link(dve.tensor_copy(ms[:, b, :, 0, :], mx[:, b]))
                dve.tensor_tensor(ms[:, b, :, 1, :], mx[:, b], ms[:, b, :, 0, :], ALU.subtract).then_inc(ms_done, 1)
                if b:
                    finish(dve, link, b - 1)
            finish(dve, link, B - 1)

        @block.scalar
        def _(act):
            for b in range(B):
                act.wait_ge(mt_done, b + 1)
                act.activation(mT[:, b, :], ps[0][0:2 * XNH, :], ACT.Copy).then_inc(mt_copied, 1)
                for n in range(XNH):
                    for kt in range(QT):
                        u = (b * XNH + n) * QT + kt
                        h = b * XNH + n
                        act.wait_ge(e_done, u + 1)
                        if kt == 0 and h >= 2:
                            act.wait_ge(pv_done, h - 1)
                        act.activation(pT[n % 2][:, kt, kt * P:S], pe_[u % 2][:, 0:S - kt * P], ACT.Exp,
                                       scale=scale).then_inc(exp_done, 1)


def rat_write(nc, name, h, srcT, n_k, odT, bias_row, duT, du_b, ones, ident, src=None):
    with ExitStack() as ctx:
        sb, psum, sem = scope(nc, ctx)
        od = sb(name + "od", [P, NT, OD + XH])
        e = sb(name + "e", [P, NT, SP])
        sp_ = sb(name + "sp", [P, NT, SP])
        dlT = sb(name + "dlT", [DR, 2, P])
        if src is not None:
            sT = sb(name + "sT", [P, 2, IC, P])
        nb_, rb = sb(name + "nb", [P, NT, N_A]), sb(name + "rb", [P, NT, N_A])
        ab = [sb(f"{name}ab{i}", [P, XH, 3]) for i in range(2)]
        bb = [sb(f"{name}bb{i}", [P, XH, 3]) for i in range(2)]
        ha = [sb(f"{name}ha{i}", [P, XH, 3]) for i in range(2)]
        sk = [sb(f"{name}sk{i}", [P, XH]) for i in range(2)]
        p_o = [psum(f"{name}po{i}", [P, 512]) for i in range(2)]
        p_d = [psum(f"{name}pd{i}", [P, 512]) for i in range(2)]
        p_t = [psum(f"{name}pt{i}", [P, 512]) for i in range(2)]
        p_l = psum(name + "pl", [P, 512])
        st_, sc_, od_done, od_copied, dl_t, dl_c, dd, dc = (sem(name + n) for n in (
            "st", "sc", "od_d", "od_c", "dl_t", "dl_c", "dd", "dc"))
        abs_done, e1, l1, sp_done, da, ex, b_done, ha_done, sk1, new3, chain, poolc = (sem(name + n) for n in (
            "abs", "e1", "l1", "sp_d", "da", "ex", "b_d", "ha_d", "sk1", "new3", "chain", "poolc"))
        block = ctx.enter_context(nc.Block())

        @block.tensor
        def _(pe):
            def turn(i):
                if i >= 2:
                    pe.wait_ge(sc_, i - 1)
                for c in range(IC):
                    ins = pe.transpose(p_t[i % 2][:, c * P:(c + 1) * P], src[:, i, c * P:(c + 1) * P], ident[:])
                ins.then_inc(st_, 1)

            def main(i):
                if src is not None:
                    pe.wait_ge(sc_, i + 1)
                if i >= 2:
                    pe.wait_ge(od_copied, i - 1)
                for k in range(n_k):
                    lhs = sT[:, i % 2, k, :] if src is not None else srcT[:, k, i * P:(i + 1) * P]
                    pe.matmul(p_o[i % 2][:, 0:OD], lhs, odT[:, k, :], start=k == 0, stop=False)
                pe.matmul(p_o[i % 2][:, 0:OD], ones[:], bias_row[:], start=False, stop=True).then_inc(od_done, 1)

            def low(i):
                pe.wait_ge(od_copied, i + 1)
                if i:
                    pe.wait_ge(dl_c, i)
                pe.transpose(p_l[0:DR, 0:P], od[:, i, C_DL:C_DL + DR], ident[:]).then_inc(dl_t, 1)

            def delta(i):
                pe.wait_ge(dl_c, i + 1)
                if i >= 2:
                    pe.wait_ge(dc, i - 1)
                pe.matmul(p_d[i % 2][:, 0:XH], dlT[:, i % 2, :], duT[:], start=True, stop=False)
                pe.matmul(p_d[i % 2][:, 0:XH], ones[:], du_b[:], start=False, stop=True).then_inc(dd, 1)

            if src is not None:
                turn(0)
            for i in range(NT + 2):
                if src is not None and i + 1 < NT:
                    turn(i + 1)
                if i < NT:
                    main(i)
                if 1 <= i <= NT:
                    low(i - 1)
                if i >= 2:
                    delta(i - 2)

        @block.scalar
        def _(act):
            for i in range(NT + 3):
                if src is not None and i < NT:
                    act.wait_ge(st_, i + 1)
                    if i >= 2:
                        act.wait_ge(od_done, i - 1)
                    act.activation(sT[:, i % 2].rearrange("p a b -> p (a b)"), p_t[i % 2][:, 0:IC * P],
                                   ACT.Copy).then_inc(sc_, 1)
                if 1 <= i <= NT:
                    act.wait_ge(od_done, i)
                    act.activation(od[:, i - 1, 0:OD], p_o[(i - 1) % 2][:, 0:OD], ACT.Copy).then_inc(od_copied, 1)
                if 2 <= i <= NT + 1:
                    act.wait_ge(dl_t, i - 1)
                    if i >= 4:
                        act.wait_ge(dd, i - 3)
                    act.activation(dlT[:, (i - 2) % 2, :], p_l[0:DR, 0:P], ACT.Copy).then_inc(dl_c, 1)
                if i >= 3:
                    act.wait_ge(dd, i - 2)
                    act.activation(od[:, i - 3, OD:OD + XH], p_d[(i - 3) % 2][:, 0:XH], ACT.Copy).then_inc(dc, 1)
            act.wait_ge(dc, NT)
            x = od[:, :, C_A:C_A + SP]
            act.activation(e[:], x, ACT.Abs).then_inc(abs_done, 1)
            act.wait_ge(abs_done, 1)
            act.activation(e[:], e[:], ACT.Exp, scale=-1.0).then_inc(e1, 1)
            act.wait_ge(e1, 1)
            act.activation(e[:], e[:], ACT.Ln, bias=1.0).then_inc(l1, 1)
            for i in range(NT):
                act.wait_ge(da, i + 1)
                act.activation(ab[i % 2][:], ab[i % 2][:], ACT.Exp, scale=-1.0).then_inc(ex, 1)

        @block.vector
        def _(dve):
            link = Chain(dve, chain)
            dve.wait_ge(l1, 1)
            dve.scalar_tensor_tensor(out=sp_[:], in0=od[:, :, C_A:C_A + SP], scalar=0.0, in1=e[:],
                                     op0=ALU.max, op1=ALU.add).then_inc(sp_done, 1)
            dve.wait_ge(sp_done, 1)
            link(dve.tensor_scalar(nb_[:], sp_[:, :, 0:N_A], SSM_EPS, -1.0, ALU.add, ALU.mult))
            link(dve.reciprocal(rb[:], nb_[:]))
            link(dve.tensor_tensor(nb_[:], rb[:], od[:, :, C_B:C_B + N_B], ALU.mult))

            def rate(i):
                if i >= 2:
                    dve.wait_ge(b_done, i - 1)
                    dve.wait_ge(ha_done, i - 1)
                dve.tensor_tensor(ab[i % 2][:].rearrange("p (s r) c -> p s r c", r=RH),
                                  sp_[:, i, N_A:SP].rearrange("p (s r) -> p s r", r=RH).unsqueeze(3).to_broadcast([P, HS, RH, 3]),
                                  sp_[:, i, 0:N_A].rearrange("p (r c) -> p r c", c=3).unsqueeze(1).to_broadcast([P, HS, RH, 3]),
                                  ALU.mult).then_inc(da, 1)

            def update(i):
                j = i % 2
                hv = h[:, i].rearrange("p (n c) -> p n c", c=XC)
                out = od[:, i, 0:XH]
                dve.wait_ge(ex, i + 1)
                dve.scalar_tensor_tensor(out=bb[j][:].rearrange("p (s r) c -> p s (r c)", r=RH),
                                         in0=ab[j][:].rearrange("p (s r) c -> p s (r c)", r=RH), scalar=1.0,
                                         in1=nb_[:, i, :].unsqueeze(1).to_broadcast([P, HS, N_A]),
                                         op0=ALU.subtract, op1=ALU.mult).then_inc(b_done, 1)
                dve.wait_ge(b_done, i + 1)
                link(dve.tensor_tensor(bb[j][:], bb[j][:], out.unsqueeze(2).to_broadcast([P, XH, 3]), ALU.mult))
                dve.wait_ge(ha_done, i + 1)
                dve.tensor_tensor(hv[:, :, 0:3], ha[j][:], bb[j][:], ALU.add).then_inc(new3, 1)

            rate(0)
            for i in range(NT):
                if i + 1 < NT:
                    rate(i + 1)
                update(i)

        @block.gpsimd
        def _(pool):
            pool.wait_ge(sp_done, 1)
            for i in range(NT):
                j = i % 2
                hv = h[:, i].rearrange("p (n c) -> p n c", c=XC)
                if i >= 2:
                    pool.wait_ge(poolc, 2 * (i - 1))
                pool.tensor_tensor(sk[j][:].rearrange("p (s r) -> p s r", r=RH),
                                   sp_[:, i, N_A:SP].rearrange("p (s r) -> p s r", r=RH),
                                   od[:, i, C_SKIP:C_SKIP + N_SKIP].unsqueeze(1).to_broadcast([P, HS, RH]),
                                   ALU.mult).then_inc(sk1, 1)
                pool.wait_ge(sk1, i + 1)
                pool.tensor_tensor(sk[j][:], sk[j][:], od[:, i, 0:XH], ALU.mult).then_inc(poolc, 1)
                pool.wait_ge(poolc, 2 * i + 1)
                pool.tensor_tensor(hv[:, :, 3], hv[:, :, 3], sk[j][:], ALU.add).then_inc(poolc, 1)
                pool.wait_ge(ex, i + 1)
                if i >= 2:
                    pool.wait_ge(new3, i - 1)
                pool.tensor_tensor(ha[j][:], hv[:, :, 0:3], ab[j][:], ALU.mult).then_inc(ha_done, 1)


def mlp(nc, inT, wT, yT):
    with ExitStack() as ctx:
        sb, psum, sem = scope(nc, ctx)
        sg = [sb(f"m_sg{i}", [P, S]) for i in range(2)]
        p_g = [psum(f"m_g{i}", [P, S]) for i in range(3)]
        p_u = [psum(f"m_u{i}", [P, S]) for i in range(3)]
        done, silu, mul = sem("m_done"), sem("m_silu"), sem("m_mul")
        block = ctx.enter_context(nc.Block())
        steps = [(b, m) for b in range(B) for m in range(MT)]

        @block.tensor
        def _(pe):
            for n, (b, m) in enumerate(steps):
                if n >= 3:
                    pe.wait_ge(mul, n - 2)
                for g, dst in enumerate((p_g, p_u)):
                    for ic in range(IC):
                        ins = pe.matmul(dst[n % 3][:], wT[:, g, ic, m * P:(m + 1) * P],
                                        inT[:, g * IC + ic, b * S:(b + 1) * S], start=ic == 0, stop=ic == IC - 1)
                ins.then_inc(done, 1)

        @block.scalar
        def _(act):
            for n in range(len(steps)):
                act.wait_ge(done, n + 1)
                if n >= 2:
                    act.wait_ge(mul, n - 1)
                act.activation(sg[n % 2][:], p_g[n % 3][:], ACT.Silu).then_inc(silu, 1)

        @block.vector
        def _(dve):
            for n, (b, m) in enumerate(steps):
                dve.wait_ge(silu, n + 1)
                dve.tensor_tensor(yT[:, m, b * S:(b + 1) * S], p_u[n % 3][:], sg[n % 2][:], ALU.mult).then_inc(mul, 1)


def final_norm(nc, x1, h, ident, eps, zT):
    with ExitStack() as ctx:
        sb, psum, sem = scope(nc, ctx)
        z = [sb(f"f_z{i}", [P, D]) for i in range(2)]
        st, mv = sb("f_st", [P, NT, 2, 6]), sb("f_mv", [P, NT, 2])
        sd, r, t = sb("f_sd", [P, NT]), sb("f_r", [P, NT]), sb("f_t", [P, NT])
        pt = [psum(f"f_pt{i}", [P, 512]) for i in range(4)]
        chain, added, var_ready, sd_ready, z_ready, turned, copied = (sem(f"f_{n}") for n in (
            "chain", "added", "var", "sdr", "z_ready", "turned", "copied"))
        block = ctx.enter_context(nc.Block())

        @block.gpsimd
        def _(pool):
            for i in range(NT):
                pool.tensor_tensor(x1[:, i, :], x1[:, i, :], h[:, i, :], ALU.add).then_inc(added, 1)

        @block.vector
        def _(dve):
            link = Chain(dve, chain)

            def finish(i):
                c = slice(i, i + 1)
                dve.wait_ge(sd_ready, i + 1)
                rsqrt_newton(dve, link, r[:, c], sd[:, c], mv[:, i, 1:2], t[:, c], LN_EPS)
                if i >= 2:
                    dve.wait_ge(turned, 2 * (i - 1))
                dve.tensor_scalar(z[i % 2][:], x1[:, i, :], mv[:, i, 0:1], t[:, c],
                                  ALU.subtract, ALU.mult).then_inc(z_ready, 1)

            for i in range(NT):
                dve.wait_ge(added, i + 1)
                dve.bn_stats(st[:, i, 0, :], x1[:, i, 0:512])
                link(dve.bn_stats(st[:, i, 1, :], x1[:, i, 512:1024]))
                dve.bn_aggr(mv[:, i, :], st[:, i].rearrange("p h s -> p (h s)")).then_inc(var_ready, 1)
                if i:
                    finish(i - 1)
            finish(NT - 1)

        @block.scalar
        def _(act):
            for i in range(NT + 1):
                if i < NT:
                    act.wait_ge(var_ready, i + 1)
                    act.activation(sd[:, i:i + 1], mv[:, i, 1:2], ACT.Sqrt, bias=eps[:]).then_inc(sd_ready, 1)
                if i:
                    for g in range(2):
                        u = 2 * (i - 1) + g
                        act.wait_ge(turned, u + 1)
                        act.activation(zT[:, 4 * g:4 * g + 4, (i - 1) * P:i * P],
                                       pt[u % 4][:].rearrange("p (k c) -> p k c", c=P), ACT.Copy).then_inc(copied, 1)

        @block.tensor
        def _(pe):
            for i in range(NT):
                pe.wait_ge(z_ready, i + 1)
                for g in range(2):
                    u = 2 * i + g
                    if u >= 4:
                        pe.wait_ge(copied, u - 3)
                    for k in range(4):
                        c = (4 * g + k) * P
                        ins = pe.transpose(pt[u % 4][:, k * P:(k + 1) * P], z[i % 2][:, c:c + P], ident[:])
                    ins.then_inc(turned, 1)


def dequantise(nc, a, ident, fT):
    with ExitStack() as ctx:
        sb, psum, sem = scope(nc, ctx)
        planes = sb("d_planes", [P, 4, 32], I32)
        lut = sb("d_lut", [P, 16])
        sh_r, sh_p, sh_j = sb("d_shr", [P, 4], I32), sb("d_shp", [P, 4], I32), sb("d_shj", [P, 8], I32)
        x = sb("d_x", [P, 4, 4, 32], I32)
        nib = sb("d_nib", [P, 4, 32], I32)
        code = sb("d_code", [P, D], I32)
        pick = [sb(f"d_pick{i}", [P, D]) for i in range(2)]
        w = [sb(f"d_w{i}", [P, D]) for i in range(2)]
        pt = [psum(f"d_pt{i}", [P, 512]) for i in range(2)]
        loaded, made, chain, picked, summed, turned, copied = (sem(f"d_{n}") for n in (
            "loaded", "made", "chain", "picked", "summed", "turned", "copied"))
        block = ctx.enter_context(nc.Block())

        @block.sync
        def _(sp):
            for o in range(KT):
                if o:
                    sp.wait_ge(picked, 16 * o)
                sp.dma_start(planes[:], a["planes"][o]).then_inc(loaded, 16)
                sp.dma_start(lut[:], a["lut4"][o]).then_inc(loaded, 16)
                sp.wait_ge(loaded, 32 * (o + 1))

        @block.gpsimd
        def _(pool):
            pool.iota(sh_r[:], pattern=[[1, 4]], base=0, channel_multiplier=0).then_inc(made, 1)
            pool.iota(sh_j[:], pattern=[[4, 8]], base=0, channel_multiplier=0).then_inc(made, 1)
            for o in range(KT):
                for v in range(16):
                    n = 16 * o + v
                    if v == 0:
                        continue
                    pool.wait_ge(picked, n + 1)
                    if v > 1:
                        pool.wait_ge(summed, 15 * o + v - 1)
                    pool.tensor_tensor(w[o % 2][:], w[o % 2][:], pick[v % 2][:], ALU.add).then_inc(summed, 1)

        @block.vector
        def _(dve):
            link = Chain(dve, chain)
            dve.wait_ge(made, 2)
            for o in range(KT):
                dve.wait_ge(loaded, 32 * (o + 1))
                link(dve.tensor_tensor(x[:], planes[:].unsqueeze(2).to_broadcast([P, 4, 4, 32]),
                                       sh_r[:].unsqueeze(1).unsqueeze(3).to_broadcast([P, 4, 4, 32]),
                                       ALU.logical_shift_right))
                for p_ in range(4):
                    ins = dve.tensor_scalar(x[:, p_], x[:, p_], 0x11111111, p_, ALU.bitwise_and, ALU.logical_shift_left)
                link(ins)
                dve.tensor_tensor(x[:, 0], x[:, 0], x[:, 1], ALU.bitwise_or)
                link(dve.tensor_tensor(x[:, 2], x[:, 2], x[:, 3], ALU.bitwise_or))
                link(dve.tensor_tensor(nib[:], x[:, 0], x[:, 2], ALU.bitwise_or))
                link(dve.tensor_tensor(code[:].rearrange("p (w j r) -> p w j r", j=8, r=4),
                                       nib[:].rearrange("p r w -> p w r").unsqueeze(2).to_broadcast([P, 32, 8, 4]),
                                       sh_j[:].unsqueeze(1).unsqueeze(3).to_broadcast([P, 32, 8, 4]),
                                       ALU.logical_shift_right))
                link(dve.tensor_scalar(code[:], code[:], 15, None, ALU.bitwise_and))
                if o >= 2:
                    dve.wait_ge(turned, 2 * (o - 1))
                for v in range(16):
                    n = 16 * o + v
                    if v >= 3:
                        dve.wait_ge(summed, 15 * o + v - 2)
                    elif v in (1, 2) and o:
                        dve.wait_ge(summed, 15 * o)
                    dst = w[o % 2] if v == 0 else pick[v % 2]
                    dve.tensor_scalar(dst[:], code[:], float(v), lut[:, v:v + 1], ALU.is_equal,
                                      ALU.mult).then_inc(picked, 1)

        @block.tensor
        def _(pe):
            for o in range(KT):
                pe.wait_ge(summed, 15 * (o + 1))
                for g in range(2):
                    u = 2 * o + g
                    if u >= 2:
                        pe.wait_ge(copied, u - 1)
                    for k in range(4):
                        c = (4 * g + k) * P
                        ins = pe.transpose(pt[g][:, k * P:(k + 1) * P], w[o % 2][:, c:c + P], ident[:])
                    ins.then_inc(turned, 1)

        @block.scalar
        def _(act):
            for u in range(2 * KT):
                act.wait_ge(turned, u + 1)
                o, g = u // 2, u % 2
                act.activation(fT[:, 4 * g:4 * g + 4, o * P:(o + 1) * P],
                               pt[g][:].rearrange("p (k c) -> p k c", c=P), ACT.Copy).then_inc(copied, 1)


def feed_forward(nc, zT, fT, x1, bias, out):
    out_t = out.rearrange("b (t p) d -> (b t) p d", p=P)
    with ExitStack() as ctx:
        sb, psum, sem = scope(nc, ctx)
        po = [psum(f"o_p{i}", [P, 512]) for i in range(4)]
        res = [sb(f"o_r{i}", [P, D]) for i in range(2)]
        xb, done, added = sem("o_xb"), sem("o_done"), sem("o_added")
        stored = [sem(f"o_stored{i}") for i in range(2)]
        block = ctx.enter_context(nc.Block())

        @block.gpsimd
        def _(pool):
            for i in range(NT):
                pool.tensor_tensor(x1[:, i, :], x1[:, i, :], bias[:], ALU.add).then_inc(xb, 1)

        @block.tensor
        def _(pe):
            for i in range(NT):
                for g in range(2):
                    u = 2 * i + g
                    if u >= 4:
                        pe.wait_ge(added, u - 3)
                    for k in range(KT):
                        ins = pe.matmul(po[u % 4][:], zT[:, k, i * P:(i + 1) * P], fT[:, k, g * 512:(g + 1) * 512],
                                        start=k == 0, stop=k == KT - 1)
                    ins.then_inc(done, 1)

        @block.vector
        def _(dve):
            for i in range(NT):
                dve.wait_ge(xb, i + 1)
                if i >= 2:
                    dve.wait_ge(stored[i % 2], 16 * (i // 2))
                for g in range(2):
                    u = 2 * i + g
                    dve.wait_ge(done, u + 1)
                    dve.tensor_tensor(res[i % 2][:, g * 512:(g + 1) * 512], po[u % 4][:],
                                      x1[:, i, g * 512:(g + 1) * 512], ALU.add).then_inc(added, 1)

        @block.sync
        def _(sp):
            for i in range(NT):
                sp.wait_ge(added, 2 * i + 2)
                sp.dma_start(out_t[i], res[i % 2][:]).then_inc(stored[i % 2], 16)
            for i in range(2):
                sp.wait_ge(stored[i], 16 * (NT // 2))



def make_constants(nc, ident, ident_r, eps, mask, half_mask, sel, ones):
    with ExitStack() as ctx:
        sb, psum, sem = scope(nc, ctx)
        a1, a2 = sb("c_a1", [2 * XNH, XNH, P]), sb("c_a2", [2 * XNH, XNH, P])
        made, done = sem("c_made"), sem("c_done")
        block = ctx.enter_context(nc.Block())

        @block.gpsimd
        def _(pool):
            for n, (t, v) in enumerate(((mask, 0.0), (half_mask, 1.0), (a1, -1.0), (a2, -1.0), (eps, LN_EPS), (ones, 1.0))):
                pool.memset(t[:], v).then_inc(made, 1)
            pool.wait_ge(made, 6)
            pool.affine_select(out=mask[:], in_=mask[:], compare_op=ALU.is_ge, fill=-MASKED, base=0,
                               pattern=[[1, P]], channel_multiplier=-1)
            pool.affine_select(out=half_mask[:], in_=half_mask[:], compare_op=ALU.is_ge, fill=0.0, base=0,
                               pattern=[[-XC, 32]], channel_multiplier=1).then_inc(made, 1)
            pool.affine_select(out=a1[:], in_=a1[:], compare_op=ALU.is_equal, fill=0.0, base=0,
                               pattern=[[-1, XNH], [0, P]], channel_multiplier=1).then_inc(made, 1)
            pool.affine_select(out=a2[:], in_=a2[:], compare_op=ALU.is_equal, fill=0.0, base=-XNH,
                               pattern=[[-1, XNH], [0, P]], channel_multiplier=1).then_inc(made, 1)
            pool.wait_ge(made, 9)
            pool.affine_select(out=half_mask[:], in_=half_mask[:], compare_op=ALU.is_ge, fill=0.0, base=XC - 1,
                               pattern=[[XC, 32]], channel_multiplier=-1).then_inc(done, 1)

        @block.vector
        def _(dve):
            dve.tensor_copy(ident_r[:], ident[:])
            dve.wait_ge(made, 9)
            dve.tensor_tensor(sel[:], a1[:], a2[:], ALU.add)


def load(nc, name, pairs):
    with ExitStack() as ctx:
        s = ctx.enter_context(nc.semaphore(name))
        block = ctx.enter_context(nc.Block())

        @block.sync
        def _(sp):
            for dst, src in pairs:
                sp.dma_start(dst, src).then_inc(s, 16)
            sp.wait_ge(s, 16 * len(pairs))


def program(nc, a, out, stop=None):
    with ExitStack() as keep:
        sb, psum, sem = scope(nc, keep)
        acc, ident, ident_bf = attention_program(nc, keep, a)
        x1, h = sb("x1", [P, NT, D]), sb("h", [P, NT, D])
        ident_r, eps, mask = sb("ident_r", [P, P], F32R), sb("eps2", [P, 1]), sb("mask2", [P, P], BF16)
        half_mask, ones = sb("half_mask", [P, 32]), sb("ones", [1, P])
        rw1, g1, b1 = sb("rw1", [P, KT * 3]), sb("g1", [P, 3 * IC]), sb("b1", [P, 3 * IC])
        rw2, g2, b2 = sb("rw2", [P, KT * 2]), sb("g2", [P, 2 * IC]), sb("b2", [P, 2 * IC])
        with ExitStack() as xat:
            sbx, _, _ = scope(nc, xat)
            qkvT, sel = sbx("qkvT", [P, IC, 3 * XH]), sbx("sel", [2 * XNH, XNH, P], F32R)
            pos, inv = sbx("pos", [P, NT], I32), sbx("inv", [P, 8])
            ang_cos, ang_sin = sbx("ang_cos", [P, NT, 8]), sbx("ang_sin", [P, NT, 8])
            load(nc, "l1", [(rw1[:], a["rw1"]), (g1[:], a["g1"]), (b1[:], a["b1"]), (rw2[:], a["rw2"]),
                            (g2[:], a["g2"]), (b2[:], a["b2"]), (qkvT[:], a["qkvT"]),
                            (pos[:], a["pos"]), (inv[:], a["inv"])])
            make_constants(nc, ident, ident_r, eps, mask, half_mask, sel, ones)
            rope_angles(nc, pos, inv, ang_cos, ang_sin)
            residual_norm(nc, a, acc, ident, eps, x1, h)
            if stop == "x1":
                return dump(nc, out, x1)
            inT = acc[:, 0:3 * IC, :]
            rat_read(nc, "r1", h, rw1, g1, b1, 3, ident, eps, half_mask, inT)
            qT = sbx("qT2", [P, XNH // 2, TOK], F32R)
            kT = sbx("kT2", [P, XNH // 2, TOK], F32R)
            v_aug = sbx("v_aug", [P, NT, XNH, XHD + 1])
            project_qkv(nc, inT, qkvT, ang_cos, ang_sin, ident, ident_r, qT, kT, v_aug)
            pT = [acc[:, 2 * i:2 * i + 2, :].rearrange("p a (b s) -> p (a b) s", s=S) for i in range(2)]
            o_all = acc[:, 4:6, :].rearrange("p a (b s) -> p (a b) s", s=XH)
            cross_attention(nc, qT, kT, v_aug, mask, sel, ident_r, ident_bf, pT, o_all)
        odT1, bias1, duT1, dub1 = (sb("odT1", [P, IC, OD]), sb("bias1", [1, OD]), sb("duT1", [DR, XH]),
                                   sb("dub1", [1, XH]))
        bias2, duT2, dub2 = sb("bias2", [1, OD]), sb("duT2", [DR, XH]), sb("dub2", [1, XH])
        load(nc, "l4", [(odT1[:], a["odT1"]), (bias1[:], a["bias1"]),
                            (duT1[:], a["duT1"]), (dub1[:], a["dub1"]), (bias2[:], a["bias2"]),
                            (duT2[:], a["duT2"]), (dub2[:], a["dub2"])])
        rat_write(nc, "w1", h, None, IC, odT1, bias1, duT1, dub1, ones, ident, src=o_all)
        if stop == "h2":
            return dump(nc, out, h)
        with ExitStack() as ml:
            sbm, _, _ = scope(nc, ml)
            odT2 = sbm("odT2", [P, MT, OD])
            with ExitStack() as inner:
                sbi, _, _ = scope(nc, inner)
                inT2, wT = sbi("inT2", [P, 2 * IC, TOK]), sbi("mlp_w", [P, 2, IC, M])
                load(nc, "l2", [(wT[:], a["mlp_wT"]), (odT2[:], a["odT2"])])
                rat_read(nc, "r2", h, rw2, g2, b2, 2, ident, eps, half_mask, inT2)
                mlp(nc, inT2, wT, acc)
            rat_write(nc, "w2", h, acc, MT, odT2, bias2, duT2, dub2, ones, ident)
        final_norm(nc, x1, h, ident, eps, acc)
        if stop == "x2":
            return dump(nc, out, x1)
        fT, bias = sb("fT", [P, KT, D]), sb("bias", [P, D])
        load(nc, "l3", [(bias[:], a["bias"].partition_broadcast(P))])
        dequantise(nc, a, ident, fT)
        feed_forward(nc, acc, fT, x1, bias, out)


def dump(nc, out, t):
    with ExitStack() as ctx:
        s = ctx.enter_context(nc.semaphore("dump"))
        block = ctx.enter_context(nc.Block())

        @block.sync
        def _(sp):
            sp.dma_start(out.rearrange("b (t p) d -> p (b t) d", p=P), t[:]).then_inc(s, 16)
            sp.wait_ge(s, 16)


def arrange(inputs):
    def c(x):
        return np.ascontiguousarray(x)

    r = {"x": c(inputs["x"])}
    for n, heads in (("q", NH), ("k", NKV), ("v", NKV)):
        w = np.asarray(inputs["L0_attn_qw_" + n]).reshape(KT, P, heads, HD)
        r["w_" + n] = c(w.transpose(2, 1, 0, 3)).reshape(heads, P, KT * HD)
        sc = np.asarray(inputs["L0_attn_scales_" + n]).reshape(KT, heads, HD)
        r["sc_" + n] = c(sc.transpose(2, 1, 0)).reshape(HD, heads * KT)
    r["w_o"] = c(inputs["L0_attn_qw_o"]).reshape(NH, P, D)
    r["sc_o"] = c(np.asarray(inputs["L0_attn_scales_o"]).reshape(NH, KT, P).transpose(2, 0, 1)).reshape(P, NH * KT)
    for i, (n, o) in enumerate((("attn", 3), ("mlp", 2)), 1):
        g = {k: np.asarray(inputs[f"L0_xattn_{n}_{k}"]) for k in
             ("read_w", "read_g", "read_b", "wod_w", "wab_w", "wab_b", "du_w", "du_b")}
        r[f"rw{i}"] = c(g["read_w"].transpose(0, 2, 1).reshape(KT, P, o).transpose(1, 0, 2)).reshape(P, KT * o)
        r[f"g{i}"] = c(g["read_g"].reshape(o * IC, P).T)
        r[f"b{i}"] = c(g["read_b"].reshape(o * IC, P).T)
        rows = [slice(N_A, N_A + N_B), slice(N_A + N_B, None), slice(0, N_A)]
        w = np.concatenate([g["wod_w"]] + [g["wab_w"][s] for s in rows])
        r[f"odT{i}"] = c(w.T.reshape(-1, P, OD).transpose(1, 0, 2))
        r[f"bias{i}"] = np.concatenate([np.zeros(C_B, g["wab_b"].dtype)] + [g["wab_b"][s] for s in rows])[None]
        r[f"duT{i}"] = c(g["du_w"].T)
        r[f"dub{i}"] = c(g["du_b"])[None]
    r["qkvT"] = c(np.asarray(inputs["L0_xattn_qkv_w"]).transpose(2, 0, 1).reshape(IC, P, 3 * XH).transpose(1, 0, 2))
    r["pos"] = c(np.asarray(inputs["pos_BxS"]).reshape(NT, P).T)
    r["mlp_wT"] = c(np.asarray(inputs["ctx_1024"]).reshape(2, M, IC, P).transpose(3, 0, 2, 1))
    r["planes"] = c(np.asarray(inputs["L0_ffn_qweight"])[:4].reshape(4, KT, P, 32).transpose(1, 2, 0, 3))
    r["lut4"] = c(inputs["L0_ffn_lut4"]).reshape(KT, P, 16)
    r["bias"] = c(inputs["L0_ffn_bias"])
    return r


def rope_constants():
    inv = (1.0 / 10000.0 ** (np.arange(0, HD, 2, dtype=np.float32) / np.float32(HD))).astype(np.float32)
    ang = np.arange(S, dtype=np.float32)[:, None] * inv
    f = np.float32(HD ** -0.25)
    cos, sin = np.cos(ang).T * f, np.sin(ang).T * f
    half = XHD // 2
    freq = (1.0 / 10000.0 ** (np.arange(half, dtype=np.float32) / np.float32(half))).astype(np.float32)
    return {"cos": np.concatenate([cos, cos]).astype(np.float32),
            "sin": np.concatenate([-sin, sin]).astype(np.float32),
            "inv": np.tile(freq, (P, 1))}


def kernel(**inputs):
    import concourse.bacc as _bacc
    from concourse.bass_utils import run_bass_kernel_spmd as _run

    nc = _bacc.Bacc("TRN2", target_bir_lowering=False, num_devices=1)
    nc.disable_value_cache = True
    arrays = {f"in_{k}": v for k, v in {**arrange(inputs), **rope_constants()}.items()}
    a = {k[3:]: nc.dram_tensor(k, v.shape, mybir.dt.from_np(v.dtype), kind="ExternalInput").ap()
         for k, v in arrays.items()}
    out = nc.dram_tensor("out_0", (B, S, D), F32, kind="ExternalOutput").ap()
    program(nc, a, out)
    r = _run(nc, [arrays], core_ids=[0])
    return r.results[0]["out_0"]
```

```python
from contextlib import ExitStack

import numpy as np

import concourse.bass as bass
from concourse import mybir

F32 = mybir.dt.float32
F32R = mybir.dt.float32r
BF16 = mybir.dt.bfloat16
I32 = mybir.dt.int32
ALU = mybir.AluOpType
ACT = mybir.ActivationFunctionType
AX = mybir.AxisListType

P = 128
B, S, D = 2, 512, 1024
TOK = B * S
NT = TOK // P
KT = D // P
NH, NKV, HD = 32, 8, 128
REP = NH // NKV
QT = S // P
LN_EPS = 1e-5
ZERO = 8.0
MASKED = 1e30

TILES = [(b, qt) for b in range(B) for qt in (3, 2, 1, 0)]
KVU = 2 * KT // REP


PLACES = 2 * KT + KVU
TURN_LAG = 4
PROBS = 4
S_PLACE = (0, 1, 2, 3, 5, 6, 7, 8)
PV_AT = {9: (0, (0,)), 10: (0, (1,)), 11: (0, (2, 3)), 15: (1, (0,)), 16: (1, (1,)), 17: (1, (2, 3))}
HI_AT = {12: 0, 18: 1}
LO_AT = {13: 0, 19: 1}


def slot_units(j, last):
    out = {}
    if not (last and j == REP - 1):
        out.update({kt: ("Q", kt) for kt in range(KT)})
    if not last:
        out.update({KT + i: ("KV"[j * KVU // KT], (j * KVU) % KT + i) for i in range(KVU)})
    out.update({KT + KVU + n: ("O", n) for n in range(KT)})
    return out


SPARED = (5,)


def on_scalar(kind, n):
    return n in SPARED if kind == "O" else n == 0


PRO = [("K", n) for n in range(KT)] + [("V", n) for n in range(KT)] + [("Q", n) for n in range(KT)]


class Count:

    def __init__(self, before, each):
        self.before, self.each = before, each

    def at(self, g, k):
        return g * self.each + (self.before + k)


def retire(nc, sems):
    with nc.Block() as block:
        @block.gpsimd
        def _(pool):
            for s in sems:
                pool.sem_clear(s)


def due(eng, sem, value):
    if not isinstance(value, int) or value > 0:
        eng.wait_ge(sem, value)


def attention_program(nc, ctx, a):

    def sb(name, shape, dt=F32, c=ctx):
        return c.enter_context(nc.sbuf_tensor(name, shape, dt))

    def sem(name):
        return ctx.enter_context(nc.semaphore(name))

    acc = sb("acc", [P, KT, TOK])
    ident = sb("ident", [P, P])
    ident_bf = sb("ident_bf", [P, P], BF16)
    with ExitStack() as att:
        zT_hi = sb("zT_hi", [P, KT, TOK], F32R, att)
        zT_lo = sb("zT_lo", [P, KT, TOK], F32R, att)
        mask = sb("mask", [P, P], BF16, att)
        eps = sb("eps", [P, 1], F32, att)
        layernorm_in(nc, a, acc, zT_hi, zT_lo, ident, ident_bf, mask, eps)
        attention_loop(nc, a, acc, zT_hi, zT_lo, ident, ident_bf, mask)
    return acc, ident, ident_bf


def layernorm_in(nc, a, acc, zT_hi, zT_lo, ident, ident_bf, mask, eps):
    x_t = a["x"].rearrange("b (t p) d -> (b t) p d", p=P)
    with ExitStack() as ctx:
        def sb(name, shape, dt=F32):
            return ctx.enter_context(nc.sbuf_tensor(name, shape, dt))

        used = []

        def sem(name):
            used.append(ctx.enter_context(nc.semaphore(name)))
            return used[-1]

        x = sb("ln_x", [P, NT, D])
        z = sb("ln_z", [P, 2, D])
        st = sb("ln_st", [P, NT, 2, 6])
        mv = sb("ln_mv", [P, NT, 2])
        sd = sb("ln_sd", [P, NT])
        r = sb("ln_r", [P, NT])
        t = sb("ln_t", [P, NT])
        pt = ctx.enter_context(nc.psum_tensor("ln_pt", [P, 4, 512], F32))
        loaded = [sem(f"ln_loaded{i}") for i in range(NT)]
        made, var_ready, sd_ready = sem("ln_made"), sem("ln_var"), sem("ln_sd_ready")
        chain, z_ready, turned, hi_done, lo_done = (sem(f"ln_{n}") for n in
                                                    ("chain", "z_ready", "turned", "hi", "lo"))
        ctx.callback(lambda: retire(nc, used))
        block = ctx.enter_context(nc.Block())

        @block.sync
        def _(sp):
            for i in range(NT):
                sp.dma_start(x[:, i, :], x_t[i]).then_inc(loaded[i], 16)

        @block.gpsimd
        def _(pool):
            pool.memset(ident[:], 1.0).then_inc(made, 1)
            pool.memset(mask[:], 0.0).then_inc(made, 1)
            pool.memset(eps[:], LN_EPS).then_inc(made, 1)
            pool.wait_ge(made, 3)
            pool.affine_select(out=ident[:], in_=ident[:], compare_op=ALU.is_equal, fill=0.0, base=0,
                               pattern=[[-1, P]], channel_multiplier=1).then_inc(made, 1)
            pool.affine_select(out=mask[:], in_=mask[:], compare_op=ALU.is_ge, fill=MASKED, base=0,
                               pattern=[[1, P]], channel_multiplier=-1).then_inc(made, 1)
            pool.wait_ge(made, 5)
            pool.tensor_copy(ident_bf[:], ident[:]).then_inc(made, 1)
            pool.memset(acc[:], 0.0).then_inc(made, 1)

        @block.vector
        def _(dve):
            n = [0]

            def link(ins):
                n[0] += 1
                ins.then_inc(chain, 1)
                dve.wait_ge(chain, n[0])

            def stats(i):
                dve.wait_ge(loaded[i], 16)
                for h in range(2):
                    ins = dve.bn_stats(st[:, i, h, :], x[:, i, h * 512:(h + 1) * 512])
                link(ins)
                dve.bn_aggr(mv[:, i, :], st[:, i].rearrange("p h s -> p (h s)")).then_inc(var_ready, 1)

            def normalise(i):
                c = slice(i, i + 1)
                var = mv[:, i, 1:2]
                dve.wait_ge(sd_ready, i + 1)
                link(dve.reciprocal(r[:, c], sd[:, c]))
                link(dve.tensor_scalar(t[:, c], var, LN_EPS, r[:, c], ALU.add, ALU.mult))
                link(dve.tensor_scalar(t[:, c], t[:, c], r[:, c], -0.5, ALU.mult, ALU.mult))
                link(dve.tensor_scalar(t[:, c], t[:, c], 1.5, r[:, c], ALU.add, ALU.mult))
                if i >= 2:
                    dve.wait_ge(turned, 2 * (i - 1))
                dve.tensor_scalar(z[:, i % 2, :], x[:, i, :], mv[:, i, 0:1], t[:, c],
                                  ALU.subtract, ALU.mult).then_inc(z_ready, 1)

            def low(i):
                for h in range(2):
                    dve.wait_ge(hi_done, 2 * i + h + 1)
                    dve.tensor_tensor(zT_lo[:, 4 * h:4 * h + 4, i * P:(i + 1) * P],
                                      pt[:, (2 * i + h) % 4, :].rearrange("p (k c) -> p k c", c=P),
                                      zT_hi[:, 4 * h:4 * h + 4, i * P:(i + 1) * P],
                                      ALU.subtract).then_inc(lo_done, 1)

            stats(0)
            for i in range(NT):
                if i + 1 < NT:
                    stats(i + 1)
                normalise(i)
                if i:
                    low(i - 1)
            low(NT - 1)

        @block.scalar
        def _(act):
            act.wait_ge(made, 3)
            for i in range(NT + 1):
                if i < NT:
                    act.wait_ge(var_ready, i + 1)
                    act.activation(sd[:, i:i + 1], mv[:, i, 1:2], ACT.Sqrt, bias=eps[:]).then_inc(sd_ready, 1)
                if i:
                    for h in range(2):
                        u = 2 * (i - 1) + h
                        act.wait_ge(turned, u + 1)
                        act.activation(zT_hi[:, 4 * h:4 * h + 4, (i - 1) * P:i * P],
                                       pt[:, u % 4, :].rearrange("p (k c) -> p k c", c=P),
                                       ACT.Copy).then_inc(hi_done, 1)

        @block.tensor
        def _(pe):
            pe.wait_ge(made, 4)
            for i in range(NT):
                pe.wait_ge(z_ready, i + 1)
                for h in range(2):
                    u = 2 * i + h
                    if u >= 4:
                        pe.wait_ge(lo_done, u - 3)
                    for k in range(4):
                        c = (4 * h + k) * P
                        ins = pe.transpose(pt[:, u % 4, k * P:(k + 1) * P], z[:, i % 2, c:c + P], ident[:])
                    ins.then_inc(turned, 1)


def attention_loop(nc, a, acc, zT_hi, zT_lo, ident, ident_bf, mask):
    with ExitStack() as ctx:
        def sb(name, shape, dt=F32):
            return ctx.enter_context(nc.sbuf_tensor(name, shape, dt))

        def psum(name, shape):
            return ctx.enter_context(nc.psum_tensor(name, shape, F32))

        used = []

        def sem(name):
            used.append(ctx.enter_context(nc.semaphore(name)))
            return used[-1]

        cos_t, sin_t = sb("cos_t", [P, S]), sb("sin_t", [P, S])
        sc_q, sc_o = sb("sc_q", [P, NH * KT]), sb("sc_o", [P, (NH + 1) * KT])
        sc_k, sc_v = sb("sc_k", [P, NKV * KT]), sb("sc_v", [P, NKV * KT])
        raw_q, raw_o, raw_kv = (sb(f"raw_{n}", [P, D], I32) for n in ("q", "o", "kv"))
        w_q, w_o, w_kv = (sb(f"w_{n}", [P, D], F32R) for n in ("q", "o", "kv"))
        kT, v = sb("kT", [P, 2, TOK]), sb("v", [P, 2, TOK])
        kv_acc, q_acc, swapped, qT = (sb(n, [P, TOK]) for n in ("kv_acc", "q_acc", "swapped", "qT"))
        spare = sb("spare", [P, TOK])
        prob = sb("prob", [P, PROBS, S])
        probT = sb("probT", [P, B, QT, S])
        ctx_hi, ctx_lo = sb("ctx_hi", [P, 2, TOK], F32R), sb("ctx_lo", [P, 2, TOK], F32R)
        low_max = sb("low_max", [P, len(TILES)])
        total, inv_total = sb("total", [P, len(TILES)]), sb("inv_total", [P, len(TILES)])
        pj = [psum(f"pj{i}", [P, TOK]) for i in range(2)]
        ps = [psum(f"ps{i}", [P, S]) for i in range(2)]
        pt = psum("pt", [P, S])
        pv = psum("pv", [P, S])

        s_tab = sem("s_tab")
        ld_q, ld_o, ld_kv = sem("ld_q"), sem("ld_o"), sem("ld_kv")
        w_q_ready, w_o_ready, w_kv_ready = sem("w_q_ready"), sem("w_o_ready"), sem("w_kv_ready")
        unit_done, evac_v, evac_s = sem("unit_done"), sem("evac_v"), sem("evac_s")
        s_done, max_done, exp_done, inv_done, norm_done = (sem(n) for n in (
            "s_done", "max_done", "exp_done", "inv_done", "norm_done"))
        t_done, t_copied, vt_done, v_copied = (sem(n) for n in ("t_done", "t_copied", "vt_done", "v_copied"))
        pv_done, hi_done, lo_done = sem("pv_done"), sem("ctx_hi_done"), sem("ctx_lo_done")
        q_swapped, q_mul, qT_ready = sem("q_swapped"), sem("q_mul"), sem("qT_ready")
        k_swapped, k_mul, kT_ready = sem("k_swapped"), sem("k_mul"), sem("kT_ready")
        zeroed, spare_added = sem("zeroed"), sem("spare_added")

        n_units = sum(len(slot_units(j, False)) for j in range(REP))
        unit_c = Count(len(PRO), n_units)
        s_units = REP + 2 + REP * len(SPARED)
        spare_c = Count(0, REP * len(SPARED))
        evac_s_c = Count(3, s_units)
        evac_v_c = Count(len(PRO) - 3, n_units - s_units)
        tile_c = Count(0, REP * len(TILES))
        slot_c = Count(0, REP)
        lead_c = Count(1, REP)
        pv_c = Count(0, REP * B)
        wkv_c = Count(3, 2)
        wq_c = Count(2, REP)

        def order(last):
            out, v_n, s_n = [], 0, 0
            for j in range(REP):
                for i, (kind, n) in slot_units(j, last).items():
                    out.append((j, i, kind, n, v_n, s_n))
                    if on_scalar(kind, n):
                        s_n += 1
                    else:
                        v_n += 1
            return out

        def place(last):
            return {(j, kind, n): (u, v_n, s_n)
                    for u, (j, _, kind, n, v_n, s_n) in enumerate(order(last))}

        def groups(eng, emit):
            emit(0, 0, False)
            emit(1, 1, False)
            with eng.Fori(1, NKV // 2 - 1) as i:
                for par in range(2):
                    emit(i * 2 + par, par, False)
            emit(NKV - 2, 0, False)
            emit(NKV - 1, 1, True)

        ctx.callback(lambda: retire(nc, used))
        block = ctx.enter_context(nc.Block())

        @block.sync
        def _(sp):
            for t, name in ((cos_t, "cos"), (sin_t, "sin"), (sc_q, "sc_q"), (sc_k, "sc_k"),
                            (sc_v, "sc_v")):
                sp.dma_start(t[:], a[name]).then_inc(s_tab, 16)
            sp.dma_start(sc_o[:, KT:], a["sc_o"]).then_inc(s_tab, 16)
            sp.dma_start(raw_kv[:], a["w_k"][0]).then_inc(ld_kv, 16)
            sp.dma_start(raw_q[:], a["w_q"][0]).then_inc(ld_q, 16)
            sp.dma_start(raw_o[:], a["w_o"][0]).then_inc(ld_o, 16)
            sp.wait_ge(w_kv_ready, 1)
            sp.dma_start(raw_kv[:], a["w_v"][0]).then_inc(ld_kv, 16)
            sp.wait_ge(w_q_ready, 1)
            sp.dma_start(raw_q[:], a["w_q"][1]).then_inc(ld_q, 16)
            sp.wait_ge(w_kv_ready, 2)
            sp.dma_start(raw_kv[:], a["w_k"][1]).then_inc(ld_kv, 16)
            sp.wait_ge(w_q_ready, 2)
            sp.dma_start(raw_q[:], a["w_q"][2]).then_inc(ld_q, 16)
            sp.wait_ge(w_kv_ready, 3)
            sp.dma_start(raw_kv[:], a["w_v"][1]).then_inc(ld_kv, 16)

            def emit(g, par, last):
                for j in range(REP):
                    due(sp, w_o_ready, slot_c.at(g, j + 1))
                    sp.dma_start(raw_o[:], a["w_o"][g * REP + j]).then_inc(ld_o, 16)
                    if not (last and j > 0):
                        due(sp, w_q_ready, wq_c.at(g, j + 1))
                        sp.dma_start(raw_q[:], a["w_q"][g * REP + (j + 3)]).then_inc(ld_q, 16)
                    if not (isinstance(g, int) and g >= NKV - 2) and j % 2 == 1:
                        due(sp, w_kv_ready, wkv_c.at(g, j // 2 + 1))
                        sp.dma_start(raw_kv[:], a["w_k" if j == 1 else "w_v"][g + 2]).then_inc(ld_kv, 16)

            groups(sp, emit)

        @block.scalar
        def _(act):
            def convert(dst, src, loaded, count, ready):
                due(act, loaded, count)
                act.activation(dst[:], src[:], ACT.Copy, bias=-ZERO).then_inc(ready, 1)

            def scaled_copy(dst, slot, scale, unit):
                due(act, unit_done, unit)
                act.activation(dst[:], pj[slot][:], ACT.Copy, scale=scale).then_inc(evac_s, 1)

            def swap(src, ready_sem, ready, free_sem, free, done):
                due(act, ready_sem, ready)
                due(act, free_sem, free)
                h = HD // 2
                act.activation(swapped[0:h, :], src[h:HD, :], ACT.Copy).then_inc(done, 1)
                act.activation(swapped[h:HD, :], src[0:h, :], ACT.Copy).then_inc(done, 1)

            def copy_v(dst, count):
                for h in range(B):
                    due(act, vt_done, count + h)
                    act.activation(dst[:, h * S:(h + 1) * S], pt[:], ACT.Copy).then_inc(v_copied, 1)

            act.wait_ge(s_tab, 16 * 6)
            convert(w_kv, raw_kv, ld_kv, 16, w_kv_ready)
            convert(w_q, raw_q, ld_q, 16, w_q_ready)
            scaled_copy(kv_acc, 0, sc_k[:, 0:1], 1)
            act.wait_ge(unit_done, KT)
            convert(w_kv, raw_kv, ld_kv, 32, w_kv_ready)
            swap(kv_acc, evac_v, KT - 1, k_mul, 0, k_swapped)
            act.wait_ge(k_mul, 2)
            act.wait_ge(kT_ready, 1)
            scaled_copy(kv_acc, 0, sc_v[:, 0:1], KT + 1)
            act.wait_ge(unit_done, 2 * KT)
            convert(w_kv, raw_kv, ld_kv, 48, w_kv_ready)
            scaled_copy(q_acc, 0, sc_q[:, 0:1], 2 * KT + 1)
            copy_v(v[:, 0, :], 1)
            act.wait_ge(unit_done, 3 * KT)
            convert(w_q, raw_q, ld_q, 32, w_q_ready)
            swap(q_acc, evac_v, 3 * (KT - 1), kT_ready, 1, q_swapped)

            def emit(g, par, last):
                at = place(last)
                for j in range(REP):
                    units = slot_units(j, last)
                    hp = j % 2
                    has_q = ("Q", 0) in units.values()
                    for i in range(PLACES):
                        if i == 0 and has_q:
                            due(act, qT_ready, lead_c.at(g, j))
                            scaled_copy(q_acc, 0, sc_q[:, bass.ds((g * REP + (j + 1)) * KT, 1)],
                                        unit_c.at(g, at[j, "Q", 0][0] + 1))
                        if i - 1 in S_PLACE:
                            n = S_PLACE.index(i - 1)
                            k = j * len(TILES) + n
                            b, qt = TILES[n]
                            w = (qt + 1) * P
                            due(act, max_done, tile_c.at(g, k + 1))
                            due(act, t_done, tile_c.at(g, k - PROBS + 1))
                            act.activation(prob[:, k % PROBS, 0:w], ps[n % 2][:, 0:w], ACT.Exp,
                                           bias=low_max[:, n:n + 1], scale=-1.0,
                                           accum_out=total[:, n:n + 1]).then_inc(exp_done, 1)
                        if i - TURN_LAG - 1 in S_PLACE:
                            n = S_PLACE.index(i - TURN_LAG - 1)
                            k = j * len(TILES) + n
                            b, qt = TILES[n]
                            due(act, t_done, tile_c.at(g, k + 1))
                            due(act, pv_done, pv_c.at(g, j * B + b - 1))
                            act.activation(probT[:, b, 0:qt + 1, qt * P:(qt + 1) * P],
                                           pt[:, 0:(qt + 1) * P].rearrange("p (k c) -> p k c", c=P),
                                           ACT.Copy).then_inc(t_copied, 1)
                        if i == 11:
                            due(act, unit_done, unit_c.at(g, at[j - 1, "O", KT - 1][0] + 1 if j else 0))
                            convert(w_o, raw_o, ld_o, (g * REP + (j + 1)) * 16, w_o_ready)
                        if i == 8 and ("K", 0) in units.values():
                            scaled_copy(kv_acc, 0, sc_k[:, bass.ds((g + 1) * KT, 1)],
                                        unit_c.at(g, at[j, "K", 0][0] + 1))
                        if i == 8 and ("V", 0) in units.values():
                            due(act, kT_ready, g + 2)
                            scaled_copy(kv_acc, 0, sc_v[:, bass.ds((g + 1) * KT, 1)],
                                        unit_c.at(g, at[j, "V", 0][0] + 1))
                        if i == 10 and has_q:
                            u, v_n, _ = at[j, "Q", KT - 1]
                            due(act, kT_ready, g + 1 if j < 2 else (g + 2 if not last else g + 1))
                            swap(q_acc, evac_v, evac_v_c.at(g, v_n + 1), qT_ready, lead_c.at(g, j), q_swapped)
                        if i == 13 and has_q and not (last and j == REP - 2):
                            due(act, unit_done, unit_c.at(g, at[j, "Q", KT - 1][0] + 1))
                            convert(w_q, raw_q, ld_q, (g * REP + (j + 3)) * 16, w_q_ready)
                        if i in HI_AT:
                            b = HI_AT[i]
                            due(act, pv_done, pv_c.at(g, j * B + b + 1))
                            act.activation(ctx_hi[:, hp, b * S:(b + 1) * S], pv[:], ACT.Copy).then_inc(hi_done, 1)
                        if i == 17 and not last and j == REP - 1:
                            copy_v(v[:, 1 - par, :], g * 2 + 3)
                        if units.get(i, ("", 0))[0] == "O" and on_scalar(*units[i]):
                            n = units[i][1]
                            k = j * len(SPARED) + SPARED.index(n)
                            due(act, spare_added, spare_c.at(g, k))
                            scaled_copy(spare, i % 2, sc_o[:, bass.ds((g * REP + j) * KT + n, 1)],
                                        unit_c.at(g, at[j, "O", n][0] + 1))
                        if i == 15 and not last and j == 1:
                            u, v_n, _ = at[j, "K", KT - 1]
                            due(act, qT_ready, lead_c.at(g, j + 1))
                            swap(kv_acc, evac_v, evac_v_c.at(g, v_n + 1), kT_ready, g + 1, k_swapped)
                        if i == 16 and not last and j % 2 == 1:
                            if j == 1:
                                due(act, unit_done, unit_c.at(g, at[j, "K", KT - 1][0] + 1))
                                convert(w_kv, raw_kv, ld_kv, g * 32 + 64, w_kv_ready)
                            elif not (isinstance(g, int) and g >= NKV - 2):
                                due(act, unit_done, unit_c.at(g, at[j, "V", KT - 1][0] + 1))
                                convert(w_kv, raw_kv, ld_kv, g * 32 + 80, w_kv_ready)

            groups(act, emit)
            act.wait_ge(unit_done, unit_c.at(NKV - 1, len(order(True))))
            convert(w_o, raw_o, ld_o, (NH + 1) * 16, w_o_ready)

        @block.vector
        def _(dve):
            def add_unit(dst, slot, scale, unit, evac):
                due(dve, unit_done, unit)
                due(dve, evac_v, evac)
                dve.scalar_tensor_tensor(out=dst, in0=pj[slot][:], scalar=scale, in1=dst,
                                         op0=ALU.mult, op1=ALU.add).then_inc(evac_v, 1)

            def finish_k(count, dst):
                due(dve, k_mul, 2 * count)
                dve.scalar_tensor_tensor(out=dst, in0=kv_acc[:], scalar=-1.0, in1=swapped[:],
                                         op0=ALU.mult, op1=ALU.subtract).then_inc(kT_ready, 1)

            dve.memset(ctx_hi[:, 1, :].bitcast(F32), 0.0).then_inc(zeroed, 1)
            dve.memset(ctx_lo[:, 1, :].bitcast(F32), 0.0).then_inc(zeroed, 1)
            dve.memset(sc_o[:, 0:KT], 0.0).then_inc(zeroed, 1)
            dve.wait_ge(zeroed, 3)
            dve.wait_ge(s_tab, 16 * 6)
            v_n = 0
            for u, (kind, n) in enumerate(PRO):
                if kind == "V" and n == 1:
                    finish_k(1, kT[:, 0, :])
                if n == 0:
                    continue
                if n == 1:
                    dve.wait_ge(evac_s, "KVQ".index(kind) + 1)
                dst, sc = {"K": (kv_acc, sc_k), "V": (kv_acc, sc_v), "Q": (q_acc, sc_q)}[kind]
                add_unit(dst[:], u % 2, sc[:, n:n + 1], u + 1, v_n if n > 1 else 0)
                v_n += 1

            def emit(g, par, last):
                at = place(last)
                for j in range(REP):
                    units = slot_units(j, last)
                    hp = j % 2
                    for i in range(PLACES):
                        if i in S_PLACE:
                            n = S_PLACE.index(i)
                            k = j * len(TILES) + n
                            b, qt = TILES[n]
                            due(dve, s_done, tile_c.at(g, k + 1))
                            dve.tensor_reduce(low_max[:, n:n + 1], ps[n % 2][:, 0:(qt + 1) * P],
                                              AX.X, ALU.min).then_inc(max_done, 1)
                        if i - 2 in S_PLACE:
                            n = S_PLACE.index(i - 2)
                            k = j * len(TILES) + n
                            due(dve, exp_done, tile_c.at(g, k + 1))
                            due(dve, norm_done, tile_c.at(g, k + 1 - len(TILES)))
                            dve.reciprocal(inv_total[:, n:n + 1], total[:, n:n + 1]).then_inc(inv_done, 1)
                        if i in LO_AT:
                            b = LO_AT[i]
                            due(dve, hi_done, pv_c.at(g, j * B + b + 1))
                            dve.tensor_tensor(ctx_lo[:, hp, b * S:(b + 1) * S], pv[:],
                                              ctx_hi[:, hp, b * S:(b + 1) * S].bitcast(F32),
                                              ALU.subtract).then_inc(lo_done, 1)
                        if i == 5 and j == 2 and not last:
                            finish_k(g + 2, kT[:, 1 - par, :])
                        if i in units:
                            kind, n = units[i]
                            u, v_n, s_n = at[j, kind, n]
                            if not on_scalar(kind, n):
                                if n == 1 and kind != "O":
                                    due(dve, evac_s, evac_s_c.at(g, s_n))
                                sc, col, dst = {
                                    "Q": (sc_q, (g * REP + (j + 1)) * KT + n, q_acc[:]),
                                    "K": (sc_k, (g + 1) * KT + n, kv_acc[:]),
                                    "V": (sc_v, (g + 1) * KT + n, kv_acc[:]),
                                    "O": (sc_o, (g * REP + j) * KT + n, acc[:, n, :])}[kind]
                                add_unit(dst, i % 2, sc[:, bass.ds(col, 1)], unit_c.at(g, u + 1),
                                         evac_v_c.at(g, v_n - (KT - len(SPARED)) if kind == "O" else v_n))

            groups(dve, emit)
            base = len(order(True))
            v_end = sum(1 for o in order(True) if not on_scalar(o[2], o[3]))
            for n in range(KT):
                if n in SPARED:
                    dve.wait_ge(spare_added, spare_c.at(NKV, 0))
                add_unit(acc[:, n, :], n % 2, sc_o[:, NH * KT + n:NH * KT + n + 1],
                         unit_c.at(NKV - 1, base + n + 1), evac_v_c.at(NKV - 1, v_end + n - (KT - len(SPARED))))

        @block.gpsimd
        def _(pool):
            def rope_mul(dst, swapped_sem, swapped_count, mul):
                due(pool, swapped_sem, swapped_count)
                for t, tab in ((swapped, sin_t), (dst, cos_t)):
                    t2 = t[:].rearrange("p (b s) -> p b s", b=B)
                    pool.tensor_tensor(t2, t2, tab[:].unsqueeze(1).to_broadcast([P, B, S]),
                                       ALU.mult).then_inc(mul, 1)

            def rope_q(count, free):
                rope_mul(q_acc, q_swapped, 2 * count if isinstance(count, int) else count * 2, q_mul)
                due(pool, q_mul, 2 * count if isinstance(count, int) else count * 2)
                due(pool, s_done, free)
                pool.tensor_tensor(qT[:], q_acc[:], swapped[:], ALU.add).then_inc(qT_ready, 1)

            pool.wait_ge(s_tab, 16 * 6)
            rope_mul(kv_acc, k_swapped, 2, k_mul)
            rope_q(1, 0)

            def add_spare(g, j, n, at):
                due(pool, evac_s, evac_s_c.at(g, at[j, "O", n][2] + 1))
                due(pool, spare_added, spare_c.at(g, j * len(SPARED) + SPARED.index(n) - (len(SPARED) - 1)))
                pool.tensor_tensor(acc[:, n, :], acc[:, n, :], spare[:], ALU.add).then_inc(spare_added, 1)

            def emit(g, par, last):
                at = place(last)
                for j in range(REP):
                    has_q = ("Q", 0) in slot_units(j, last).values()
                    for n, (b, qt) in enumerate(TILES):
                        k = j * len(TILES) + n
                        w = (qt + 1) * P
                        due(pool, inv_done, tile_c.at(g, k + 1))
                        pool.tensor_tensor(prob[:, k % PROBS, 0:w], prob[:, k % PROBS, 0:w],
                                           inv_total[:, n:n + 1].to_broadcast([P, w]),
                                           ALU.mult).then_inc(norm_done, 1)
                    if has_q:
                        rope_q(lead_c.at(g, j + 1), tile_c.at(g, (j + 1) * len(TILES)))
                    if j == 1 and not last:
                        rope_mul(kv_acc, k_swapped, (g + 2) * 2, k_mul)
                    for n in SPARED:
                        add_spare(g, j, n, at)

            groups(pool, emit)

        @block.tensor
        def _(pe):
            def unit(slot, lhs, parts, count, free_v, free_s=None):
                due(pe, evac_v, free_v)
                if free_s is not None:
                    due(pe, evac_s, free_s)
                for b in range(B):
                    for n, part in enumerate(parts):
                        ins = pe.matmul(pj[slot][:, b * S:(b + 1) * S], lhs, part[:, b * S:(b + 1) * S],
                                        start=n == 0, stop=n == 1)
                ins.then_inc(unit_done, 1)

            def z_parts(kt):
                return zT_hi[:, kt, :], zT_lo[:, kt, :]

            def turn_v(free_copied, free_t, evac):
                for h in range(B):
                    due(pe, v_copied, free_copied + h)
                    if h == 0:
                        due(pe, t_copied, free_t)
                        due(pe, evac_v, evac)
                    for c in range(QT):
                        ins = pe.transpose(pt[:, c * P:(c + 1) * P],
                                           kv_acc[:, h * S + c * P:h * S + (c + 1) * P], ident[:])
                    ins.then_inc(vt_done, 1)

            evacs_v = evacs_s = 0
            done = []
            for u, (kind, n) in enumerate(PRO):
                if n == 0:
                    if kind == "Q":
                        pe.wait_ge(w_q_ready, 1)
                    else:
                        pe.wait_ge(w_kv_ready, "KV".index(kind) + 1)
                fv, fs = done[u - 2] if u >= 2 else (0, 0)
                unit(u % 2, (w_q if kind == "Q" else w_kv)[:, n * P:(n + 1) * P], z_parts(n), u + 1, fv, fs)
                if on_scalar(kind, n):
                    evacs_s += 1
                else:
                    evacs_v += 1
                done.append((evacs_v, evacs_s))
            turn_v(0, 0, 2 * (KT - 1))
            pe.wait_ge(zeroed, 3)

            def emit(g, par, last):
                at = place(last)
                flat = order(last)
                for j in range(REP):
                    units = slot_units(j, last)
                    hp = j % 2
                    for i in range(PLACES):
                        if i in S_PLACE:
                            n = S_PLACE.index(i)
                            b, qt = TILES[n]
                            k = j * len(TILES) + n
                            if i == 0:
                                due(pe, qT_ready, lead_c.at(g, j))
                                if j == 0:
                                    due(pe, kT_ready, g + 1)
                            due(pe, exp_done, tile_c.at(g, k - 1))
                            w = (qt + 1) * P
                            pe.matmul(ps[n % 2][:, 0:w], qT[:, b * S + qt * P:b * S + (qt + 1) * P],
                                      kT[:, par, b * S:b * S + w], start=True, stop=False)
                            pe.matmul(ps[n % 2][:, qt * P:w], mask_neg, ident_bf[:],
                                      start=False, stop=True).then_inc(s_done, 1)
                        if i - TURN_LAG in S_PLACE:
                            n = S_PLACE.index(i - TURN_LAG)
                            b, qt = TILES[n]
                            k = j * len(TILES) + n
                            due(pe, norm_done, tile_c.at(g, k + 1))
                            due(pe, t_copied, tile_c.at(g, k))
                            if n == 0 and j == 0:
                                due(pe, v_copied, g * 2 + 2)
                            for c in range(qt + 1):
                                ins = pe.transpose(pt[:, c * P:(c + 1) * P], prob[:, k % PROBS, c * P:(c + 1) * P],
                                                   ident[:])
                            ins.then_inc(t_done, 1)
                        if i in PV_AT:
                            b, chunks = PV_AT[i]
                            if chunks[0] == 0:
                                due(pe, t_copied, tile_c.at(g, j * len(TILES) + 4 * (b + 1)))
                                due(pe, hi_done, pv_c.at(g, j * B + b))
                                due(pe, lo_done, pv_c.at(g, j * B + b))
                            for c in chunks:
                                ins = pe.matmul(pv[:, c * P:S], v[:, par, b * S + c * P:b * S + (c + 1) * P],
                                                probT[:, b, c, c * P:S], start=c == 0, stop=c == QT - 1)
                            if chunks[-1] == QT - 1:
                                ins.then_inc(pv_done, 1)
                        if i in units:
                            kind, n = units[i]
                            u, v_n, s_n = at[j, kind, n]
                            if kind == "Q" and n == 0:
                                due(pe, w_q_ready, wq_c.at(g, j))
                            if kind == "K" and n == 0:
                                due(pe, w_kv_ready, g * 2 + 3)
                            if kind == "V" and n == 0:
                                due(pe, w_kv_ready, g * 2 + 4)
                            if kind == "O" and n == 0:
                                due(pe, w_o_ready, slot_c.at(g, j + 1))
                                due(pe, hi_done, pv_c.at(g, j * B))
                                due(pe, lo_done, pv_c.at(g, j * B))
                            if kind == "O":
                                lhs, parts = w_o, (ctx_hi[:, 1 - hp, :], ctx_lo[:, 1 - hp, :])
                            else:
                                lhs, parts = (w_q if kind == "Q" else w_kv), z_parts(n)
                            if u >= 2:
                                p = flat[u - 2]
                                own_s = on_scalar(p[2], p[3])
                                fv, fs = p[4] + (not own_s), p[5] + own_s
                            else:
                                fv, fs, own_s = u - 1, 0, False
                            unit(i % 2, lhs[:, n * P:(n + 1) * P], parts, None, evac_v_c.at(g, fv),
                                 evac_s_c.at(g, fs) if own_s else None)
                        if i == 16 and j == REP - 1 and not last:
                            turn_v(g * 2 + 2, tile_c.at(g, REP * len(TILES)),
                                   evac_v_c.at(g, at[j, "V", KT - 1][1] + 1))

            mask_neg = mask[:]
            groups(pe, emit)
            v_end = sum(1 for o in order(True) if not on_scalar(o[2], o[3]))
            pe.wait_ge(w_o_ready, NH + 1)
            pe.wait_ge(hi_done, NH * B)
            pe.wait_ge(lo_done, NH * B)
            for n in range(KT):
                unit(n % 2, w_o[:, n * P:(n + 1) * P], (ctx_hi[:, 1, :], ctx_lo[:, 1, :]), None,
                     evac_v_c.at(NKV - 1, v_end + n - 1))


XH, XC = 256, 4
IC = XH // P
XNH, XHD = 16, 16
RH, HS = 16, 16
DR = 8
M = 1024
MT = M // P
N_B, N_SKIP, N_A = RH * (XC - 1), RH, RH * (XC - 1)
C_DL, C_B, C_SKIP, C_A = XH, XH + DR, XH + DR + N_B, XH + DR + N_B + N_SKIP
OD = C_A + N_A
SP = N_A + XH
PARTS = 4
SSM_EPS = 1e-5
TWO_PI = 2.0 * np.pi
PI_A, PI_B = 6.28125, float(np.float32(TWO_PI - 6.28125))
PI_C = float(np.float32(TWO_PI - 6.28125 - float(np.float32(TWO_PI - 6.28125))))
PI = 3.1415925


class Chain:

    def __init__(self, eng, sem):
        self.eng, self.sem, self.n = eng, sem, 0

    def __call__(self, ins):
        self.n += 1
        ins.then_inc(self.sem, 1)
        self.eng.wait_ge(self.sem, self.n)


def scope(nc, ctx):
    def sb(name, shape, dt=F32):
        return ctx.enter_context(nc.sbuf_tensor(name, shape, dt))

    def psum(name, shape, dt=F32):
        return ctx.enter_context(nc.psum_tensor(name, shape, dt))

    def sem(name):
        return ctx.enter_context(nc.semaphore(name))

    return sb, psum, sem


def rsqrt_newton(dve, link, r, sd, var, t, eps):
    link(dve.reciprocal(r, sd))
    link(dve.tensor_scalar(t, var, eps, None, ALU.add))
    link(dve.tensor_tensor(t, t, r, ALU.mult))
    link(dve.tensor_tensor(t, t, r, ALU.mult))
    link(dve.tensor_scalar(t, t, -0.5, 1.5, ALU.mult, ALU.add))
    link(dve.tensor_tensor(t, t, r, ALU.mult))


def residual_norm(nc, a, acc, ident, eps, x1, h):
    x_t = a["x"].rearrange("b (t p) d -> (b t) p d", p=P)
    with ExitStack() as ctx:
        sb, psum, sem = scope(nc, ctx)
        st, mv = sb("r_st", [P, NT, 2, 6]), sb("r_mv", [P, NT, 2])
        sd, r, t = sb("r_sd", [P, NT]), sb("r_r", [P, NT]), sb("r_t", [P, NT])
        pt = [psum(f"r_pt{i}", [P, D]) for i in range(2)]
        loaded = [sem(f"r_loaded{i}") for i in range(NT)]
        chain, turned, added, var_ready, sd_ready, done = (sem(f"r_{n}") for n in (
            "chain", "turned", "added", "var", "sd", "done"))
        block = ctx.enter_context(nc.Block())

        @block.sync
        def _(sp):
            for i in range(NT):
                sp.dma_start(x1[:, i, :], x_t[i]).then_inc(loaded[i], 16)

        @block.tensor
        def _(pe):
            for i in range(NT):
                if i >= 2:
                    pe.wait_ge(added, i - 1)
                for k in range(KT):
                    ins = pe.transpose(pt[i % 2][:, k * P:(k + 1) * P], acc[:, k, i * P:(i + 1) * P], ident[:])
                ins.then_inc(turned, 1)

        @block.scalar
        def _(act):
            for i in range(NT):
                act.wait_ge(var_ready, i + 1)
                act.activation(sd[:, i:i + 1], mv[:, i, 1:2], ACT.Sqrt, bias=eps[:]).then_inc(sd_ready, 1)

        @block.vector
        def _(dve):
            link = Chain(dve, chain)

            def finish(i):
                c = slice(i, i + 1)
                dve.wait_ge(sd_ready, i + 1)
                rsqrt_newton(dve, link, r[:, c], sd[:, c], mv[:, i, 1:2], t[:, c], LN_EPS)
                dve.tensor_scalar(h[:, i, :], x1[:, i, :], mv[:, i, 0:1], t[:, c],
                                  ALU.subtract, ALU.mult).then_inc(done, 1)

            for i in range(NT):
                dve.wait_ge(loaded[i], 16)
                dve.wait_ge(turned, i + 1)
                dve.tensor_tensor(x1[:, i, :], pt[i % 2][:], x1[:, i, :], ALU.add).then_inc(added, 1)
                dve.wait_ge(added, i + 1)
                dve.bn_stats(st[:, i, 0, :], x1[:, i, 0:512])
                link(dve.bn_stats(st[:, i, 1, :], x1[:, i, 512:1024]))
                dve.bn_aggr(mv[:, i, :], st[:, i].rearrange("p h s -> p (h s)")).then_inc(var_ready, 1)
                if i:
                    finish(i - 1)
            finish(NT - 1)


def rat_read(nc, name, h, rw, gam, bet, n_out, ident, eps, half_mask, inT, deq=None, o_deq=0, spill=()):
    W = n_out * 32
    with ExitStack() as ctx:
        sb, psum, sem = scope(nc, ctx)
        wbd = sb(name + "wbd", [P, KT, n_out, 32])
        hT = [sb(f"{name}hT{i}", [P, D]) for i in range(2)]
        yn = [sb(f"{name}yn{i}", [P, n_out * XH]) for i in range(2)]
        st, mv = sb(name + "st", [P, NT, n_out, 6]), sb(name + "mv", [P, NT, n_out, 2])
        sd, r, t = (sb(name + n, [P, NT, n_out]) for n in ("sd", "r", "t"))
        p_h = [psum(f"{name}ph{i}", [P, 512]) for i in range(2)]
        p_y = [psum(f"{name}py{i}", [P, 2, 512]) for i in range(2)]
        p_t = [psum(f"{name}pt{i}", [P, 512]) for i in range(2)]
        made, moved, chain, ht, hc, ydone, var_ready, sd_ready, yn_done, yt, yc = (sem(name + n) for n in (
            "made", "moved", "chain", "ht", "hc", "ydone", "var", "sdr", "yn_done", "yt", "yc"))
        block = ctx.enter_context(nc.Block())
        nb = n_out * IC

        def y_view(i, o):
            return p_y[i % 2][:, :, 0:4 * W].rearrange(
                "p b (k o j) -> p b k o j", o=n_out, j=32)[:, :, :, o, :]

        @block.gpsimd
        def _(pool):
            for k in range(KT):
                ins = pool.tensor_tensor(
                    wbd[:, k], rw[:, k * n_out:(k + 1) * n_out].unsqueeze(2).to_broadcast([P, n_out, 32]),
                    half_mask[:].unsqueeze(1).to_broadcast([P, n_out, 32]), ALU.mult)
            ins.then_inc(made, 1)
            if deq is not None:
                deq.add(pool, o_deq)

        @block.sync
        def _(sp):
            if deq is not None:
                deq.load(sp, o_deq)
            for dst, src in spill:
                sp.dma_start(dst, src).then_inc(moved, 16)
            if spill:
                sp.wait_ge(moved, 16 * len(spill))

        @block.tensor
        def _(pe):
            def turn_h(i):
                for g in range(2):
                    u = 2 * i + g
                    if u >= 2:
                        pe.wait_ge(hc, u - 1)
                    for k in range(4):
                        c = (4 * g + k) * P
                        ins = pe.transpose(p_h[g][:, k * P:(k + 1) * P], h[:, i, c:c + P], ident[:])
                    ins.then_inc(ht, 1)

            def products(i):
                pe.wait_ge(hc, 2 * i + 2)
                if i >= 2:
                    pe.wait_ge(yn_done, n_out * (i - 1))
                for k in range(KT):
                    ins = pe.matmul(p_y[i % 2][:, k // 4, (k % 4) * W:(k % 4 + 1) * W],
                                    hT[i % 2][:, k * P:(k + 1) * P], wbd[:, k].rearrange("p o j -> p (o j)"),
                                    start=True, stop=True)
                ins.then_inc(ydone, 1)

            def turn_y(i):
                pe.wait_ge(yn_done, n_out * (i + 1))
                for b in range(2):
                    n0, n1 = (0, min(4, nb)) if b == 0 else (4, nb)
                    if n1 <= n0:
                        continue
                    if i:
                        pe.wait_ge(yc, nb * (i - 1) + n1)
                    for n in range(n0, n1):
                        ins = pe.transpose(p_t[b][:, (n - n0) * P:(n - n0 + 1) * P],
                                           yn[i % 2][:, n * P:(n + 1) * P], ident[:])
                        ins.then_inc(yt, 1)

            pe.wait_ge(made, 1)
            turn_h(0)
            for i in range(NT):
                products(i)
                if i + 1 < NT:
                    turn_h(i + 1)
                if i:
                    turn_y(i - 1)
            turn_y(NT - 1)

        @block.vector
        def _(dve):
            link = Chain(dve, chain)

            def finish(i):
                dve.wait_ge(sd_ready, i + 1)
                rsqrt_newton(dve, link, r[:, i], sd[:, i], mv[:, i, :, 1], t[:, i], LN_EPS)
                if i >= 2:
                    dve.wait_ge(yt, nb * (i - 1))
                for o in range(n_out):
                    dve.tensor_scalar(yn[i % 2][:, o * XH:(o + 1) * XH].rearrange("p (b k j) -> p b k j", b=2, j=32),
                                      y_view(i, o), mv[:, i, o, 0:1], t[:, i, o:o + 1],
                                      ALU.subtract, ALU.mult).then_inc(yn_done, 1)

            for i in range(NT):
                dve.wait_ge(ydone, i + 1)
                for o in range(n_out):
                    ins = dve.bn_stats(st[:, i, o, :], y_view(i, o))
                link(ins)
                for o in range(n_out):
                    ins = dve.bn_aggr(mv[:, i, o, :], st[:, i, o, :])
                ins.then_inc(var_ready, 1)
                if i:
                    finish(i - 1)
                if deq is not None:
                    for v in (2 * i, 2 * i + 1):
                        deq.pick(dve, o_deq, v)
            finish(NT - 1)

        @block.scalar
        def _(act):
            def copy_h(i):
                for g in range(2):
                    act.wait_ge(ht, 2 * i + g + 1)
                    if i >= 2 and g == 0:
                        act.wait_ge(ydone, i - 1)
                    act.activation(hT[i % 2][:, g * 512:(g + 1) * 512], p_h[g][:], ACT.Copy).then_inc(hc, 1)

            def root(i):
                act.wait_ge(var_ready, i + 1)
                act.activation(sd[:, i], mv[:, i, :, 1], ACT.Sqrt, bias=eps[:]).then_inc(sd_ready, 1)

            def copy_y(i):
                for n in range(nb):
                    act.wait_ge(yt, nb * i + min(4 * (n // 4) + 4, nb))
                    act.activation(inT[:, n, i * P:(i + 1) * P], p_t[n // 4][:, (n % 4) * P:(n % 4 + 1) * P],
                                   ACT.Identity, bias=bet[:, n:n + 1], scale=gam[:, n:n + 1]).then_inc(yc, 1)

            copy_h(0)
            for i in range(NT):
                if i + 1 < NT:
                    copy_h(i + 1)
                root(i)
                if i:
                    copy_y(i - 1)
            copy_y(NT - 1)


def rope_angles(nc, pos, inv, ang_cos, ang_sin):
    with ExitStack() as ctx:
        sb, psum, sem = scope(nc, ctx)
        posf, ang, n_i, n_f, red, over = (sb("a_pos", [P, NT]), sb("a_ang", [P, NT, 8]),
                                          sb("a_ni", [P, NT, 8], I32), sb("a_nf", [P, NT, 8]),
                                          sb("a_red", [P, 2, NT, 8]), sb("a_over", [P, NT, 8]))
        chain, ready = sem("a_chain"), sem("a_ready")
        block = ctx.enter_context(nc.Block())

        @block.vector
        def _(dve):
            link = Chain(dve, chain)
            link(dve.tensor_copy(posf[:], pos[:]))
            link(dve.tensor_tensor(ang[:], posf[:].unsqueeze(2).to_broadcast([P, NT, 8]),
                                   inv[:].unsqueeze(1).to_broadcast([P, NT, 8]), ALU.mult))
            link(dve.tensor_scalar(n_i[:], ang[:], 1.0 / TWO_PI, None, ALU.mult))
            link(dve.tensor_copy(n_f[:], n_i[:]))
            s = red[:, 0]
            link(dve.scalar_tensor_tensor(out=s, in0=n_f[:], scalar=-PI_A, in1=ang[:], op0=ALU.mult, op1=ALU.add))
            link(dve.scalar_tensor_tensor(out=s, in0=n_f[:], scalar=-PI_B, in1=s, op0=ALU.mult, op1=ALU.add))
            link(dve.scalar_tensor_tensor(out=s, in0=n_f[:], scalar=-PI_C, in1=s, op0=ALU.mult, op1=ALU.add))
            c = red[:, 1]
            link(dve.tensor_scalar(c, s, TWO_PI / 4, None, ALU.add))
            for v in (c, s):
                link(dve.tensor_scalar(over[:], v, PI, -TWO_PI, ALU.is_gt, ALU.mult))
                link(dve.tensor_tensor(v, v, over[:], ALU.add))
                link(dve.tensor_scalar(over[:], v, -PI, TWO_PI, ALU.is_lt, ALU.mult))
                link(dve.tensor_tensor(v, v, over[:], ALU.add))
                ins = dve.tensor_scalar(v, v, PI, -PI, ALU.min, ALU.max)
                link(ins)
            dve.tensor_copy(over[:], s).then_inc(ready, 1)

        @block.scalar
        def _(act):
            act.wait_ge(ready, 1)
            act.activation(ang_sin[:], red[:, 0], ACT.Sin)
            act.activation(ang_cos[:], red[:, 1], ACT.Sin)


def project_qkv(nc, inT, qkvT, ang_cos, ang_sin, ident, ident_r, qT, kT, v_aug, work):
    with ExitStack() as ctx:
        sb, psum, sem = scope(nc, ctx)
        t1, t2 = (work[:, 4, n * 512:(n + 1) * 512].rearrange("p (w n f e) -> p w n f e", w=2, n=XNH, f=2)
                  for n in range(2))
        qs = [sb(f"p_qs{i}", [P, 2, XNH, PARTS, XHD], F32R) for i in range(2)]
        p_q = [psum(f"p_proj{i}", [P, 2, 512]) for i in range(2)]
        p_t = [psum(f"p_turn{i}", [P, 1024], F32R) for i in range(2)]
        chain, proj, parts, turned, copied, v_done, prod = (sem(f"p_{n}") for n in (
            "chain", "proj", "parts", "turned", "copied", "v", "prod"))
        ones = sem("p_ones")
        block = ctx.enter_context(nc.Block())

        @block.gpsimd
        def _(pool):
            pool.memset(v_aug[:, :, :, XHD:XHD + 1], 1.0).then_inc(ones, 1)

        @block.tensor
        def _(pe):
            def project(i):
                if i >= 2:
                    pe.wait_ge(prod, i - 1)
                    pe.wait_ge(v_done, i - 1)
                for o in range(3):
                    for ic in range(IC):
                        ins = pe.matmul(p_q[i % 2][:, o // 2, (o % 2) * XH:(o % 2 + 1) * XH],
                                        inT[:, o * IC + ic, i * P:(i + 1) * P],
                                        qkvT[:, ic, o * XH:(o + 1) * XH], start=ic == 0, stop=ic == IC - 1)
                ins.then_inc(proj, 1)

            def turn(i):
                pe.wait_ge(parts, i + 1)
                for w in range(2):
                    u = 2 * i + w
                    if u >= 2:
                        pe.wait_ge(copied, u - 1)
                    for n in range(XNH // 2):
                        ins = pe.transpose(p_t[w][:, n * P:(n + 1) * P],
                                           qs[i % 2][:, w, 2 * n:2 * n + 2].rearrange("p a b c -> p (a b c)"),
                                           ident_r[:])
                    ins.then_inc(turned, 1)

            project(0)
            for i in range(NT):
                if i + 1 < NT:
                    project(i + 1)
                turn(i)

        @block.vector
        def _(dve):
            link = Chain(dve, chain)
            for i in range(NT):
                x = p_q[i % 2][:, 0, :].rearrange("p (w n f) -> p (w n) f", w=2, f=XHD)
                y1 = t1.rearrange("p w n f e -> p (w n) f e")
                y2 = t2.rearrange("p w n f e -> p (w n) f e")
                cb = ang_cos[:, i, :].unsqueeze(1).to_broadcast([P, 2 * XNH, 8])
                sb_ = ang_sin[:, i, :].unsqueeze(1).to_broadcast([P, 2 * XNH, 8])
                dve.wait_ge(proj, i + 1)
                if i:
                    dve.wait_ge(parts, i)
                dve.tensor_tensor(y1[:, :, 0, :], x[:, :, 0:8], cb, ALU.mult)
                dve.tensor_tensor(y1[:, :, 1, :], x[:, :, 8:16], cb, ALU.mult)
                dve.tensor_tensor(y2[:, :, 0, :], x[:, :, 8:16], sb_, ALU.mult)
                ins = dve.tensor_tensor(y2[:, :, 1, :], x[:, :, 0:8], sb_, ALU.mult)
                ins.then_inc(prod, 1)
                dve.wait_ge(prod, i + 1)
                dve.tensor_tensor(y1[:, :, 0, :], y1[:, :, 0, :], y2[:, :, 0, :], ALU.subtract)
                link(dve.tensor_tensor(y1[:, :, 1, :], y1[:, :, 1, :], y2[:, :, 1, :], ALU.add))
                if i >= 2:
                    dve.wait_ge(turned, 2 * (i - 1))
                full = t1.rearrange("p w n f e -> p w n (f e)")
                q_in = full[:, 0].unsqueeze(2).to_broadcast([P, XNH, 2, XHD])
                k_in = full[:, 1].unsqueeze(2).to_broadcast([P, XNH, 2, XHD])
                q_s, k_s = qs[i % 2][:, 0], qs[i % 2][:, 1]
                dve.tensor_copy(q_s[:, :, 0:2, :], q_in)
                link(dve.tensor_copy(k_s[:, :, 0:4:2, :], k_in))
                dve.tensor_tensor(q_s[:, :, 2:4, :], q_in, q_s[:, :, 0:2, :], ALU.subtract)
                dve.tensor_tensor(k_s[:, :, 1:4:2, :], k_in, k_s[:, :, 0:4:2, :], ALU.subtract).then_inc(parts, 1)

        @block.scalar
        def _(act):
            act.wait_ge(ones, 1)
            for i in range(NT):
                act.wait_ge(proj, i + 1)
                act.activation(v_aug[:, i, :, 0:XHD], p_q[i % 2][:, 1, 0:XH].rearrange("p (n f) -> p n f", f=XHD),
                               ACT.Copy).then_inc(v_done, 1)
                for w, dst in enumerate((qT, kT)):
                    act.wait_ge(turned, 2 * i + w + 1)
                    act.activation(dst[:, :, i * P:(i + 1) * P],
                                   p_t[w][:].bitcast(F32).rearrange("p (n c) -> p n c", c=P), ACT.Copy).then_inc(copied, 1)


def cross_attention(nc, qT, kT, v_aug, mask, sel, ident, ident_r, ident_bf, pT, o_all, deq, fT):
    scale = XHD ** -0.5
    max_packs = [[(3, 0)], [(2, 0), (0, 3 * P)], [(1, 0)]]
    exp_packs = [[(0, 0)], [(1, 0), (3, 3 * P)], [(2, 0)]]
    place = {kt: (m, c) for m, pack in enumerate(exp_packs) for kt, c in pack}
    N = len(max_packs)
    OH = 6
    turn_after = {1: 0, 7: 1, 12: 2, 18: 3, 25: 4}
    D_TILES = KT - 2
    with ExitStack() as ctx:
        sb, psum, sem = scope(nc, ctx)
        mx = sb("x_mx", [P, B, QT, XNH])
        ms = sb("x_ms", [P, B, QT, 2, XNH], F32R)
        mT = sb("x_mT", [2 * XNH, B, S], F32R)
        rt = sb("x_rt", [P, QT, XNH])
        ps = [psum(f"x_ps{i}", [P, 512]) for i in range(2)]
        pe_ = [psum(f"x_pe{i}", [P, 512]) for i in range(2)]
        po = [psum(f"x_po{i}", [P, 512]) for i in range(3)]
        p_w = psum("x_pw", [P, 512])
        oT = pT[0][0:XHD + 1, N, :]
        ot_copied, out_done = sem("x_ot_copied"), sem("x_out_done")
        s_done, m_done, ms_done, mt_done, mt_copied, e_done, exp_done, pv_done, o_done, chain = (
            sem(f"x_{n}") for n in ("s", "m", "ms", "mt", "mtc", "e", "exp", "pv", "o", "chain"))
        block = ctx.enter_context(nc.Block())

        def rows(n):
            return slice(64 * (n % 2), 64 * (n % 2) + 64)

        def out_of(n, qt):
            c = ((n % OH) * QT + qt) * 17
            return po[n // OH][:, c:c + 17]

        @block.sync
        def _(sp):
            for o in range(D_TILES):
                deq.load(sp, o)

        @block.tensor
        def _(pe):
            def maxima(b, n, m):
                u = (b * XNH + n) * N + m
                if u >= 2:
                    pe.wait_ge(m_done, u - 1)
                for qt, c in max_packs[m]:
                    w = (qt + 1) * P
                    q0 = b * S + qt * P
                    pe.matmul(ps[u % 2][:, c:c + w], qT[rows(n), n // 2, q0:q0 + P],
                              kT[rows(n), n // 2, b * S:b * S + w], start=True, stop=False)
                    ins = pe.matmul(ps[u % 2][:, c + qt * P:c + w], mask[:], ident_bf[:], start=False, stop=True)
                ins.then_inc(s_done, 1)

            def turn_maxima(b):
                pe.wait_ge(ms_done, b + 1)
                for qt in range(QT):
                    ins = pe.transpose(ps[0][0:2 * XNH, qt * P:(qt + 1) * P].bitcast(F32R),
                                       ms[:, b, qt].rearrange("p a n -> p (a n)"), ident_r[:])
                ins.then_inc(mt_done, 1)
                pe.wait_ge(mt_copied, b + 1)

            def scores(b, n, m):
                u = (b * XNH + n) * N + m
                if u >= 2:
                    pe.wait_ge(exp_done, u - 1)
                for kt, c in exp_packs[m]:
                    k0 = b * S + kt * P
                    w = S - kt * P
                    o = pe_[u % 2]
                    pe.matmul(o[:, c:c + w], kT[rows(n), n // 2, k0:k0 + P], qT[rows(n), n // 2, k0:b * S + S],
                              start=True, stop=False)
                    pe.matmul(o[:, c:c + w], sel[:, n, :], mT[:, b, kt * P:S], start=False, stop=False)
                    ins = pe.matmul(o[:, c:c + P], ident_bf[:], mask[:], start=False, stop=True)
                ins.then_inc(e_done, 1)

            def weigh(b, n, kts):
                h = b * XNH + n
                if kts[0] == 0:
                    pe.wait_ge(exp_done, (h + 1) * N)
                    if h:
                        pe.wait_ge(ot_copied, h)
                    o = turn_after.get(h)
                    if o is not None:
                        pe.wait_ge(deq.copied, 2 * (o + 1))
                for kt in kts:
                    m, c = place[kt]
                    ins = pe.matmul(p_w[0:XHD + 1, kt * P:S], v_aug[:, b * QT + kt, n, :],
                                    pT[n % 2][:, m, c:c + S - kt * P], start=kt == 0, stop=kt == QT - 1)
                if kts[-1] == QT - 1:
                    ins.then_inc(pv_done, 1)

            def turn_out(b, n):
                pe.wait_ge(ot_copied, b * XNH + n + 1)
                if n == 0 and b:
                    pe.wait_ge(o_done, b)
                for qt in range(QT):
                    ins = pe.transpose(out_of(n, qt), oT[:, qt * P:(qt + 1) * P], ident[0:XHD + 1, 0:XHD + 1])
                ins.then_inc(out_done, 1)

            for n in range(XNH):
                for m in range(N):
                    maxima(0, n, m)
            for b in range(B):
                turn_maxima(b)
                for n in range(XNH):
                    for m in range(N):
                        scores(b, n, m)
                        if b + 1 < B:
                            maxima(b + 1, n, m)
                        if n:
                            if m == 0 and n >= 2:
                                turn_out(b, n - 2)
                            weigh(b, n - 1, ((0,), (1,), (2, 3))[m])
                    if b * XNH + n in turn_after:
                        pe.wait_ge(ot_copied, b * XNH + n)
                        deq.turn(pe, turn_after[b * XNH + n], p_w)
                turn_out(b, XNH - 2)
                weigh(b, XNH - 1, (0, 1, 2, 3))
                turn_out(b, XNH - 1)
            deq.turn(pe, D_TILES - 1, p_w)

        def finish(dve, link, b):
            dve.wait_ge(out_done, (b + 1) * XNH)
            for k in range(3):
                heads = min(OH, XNH - k * OH)
                o = po[k][:, 0:heads * QT * 17].rearrange("p (n q f) -> p q n f", q=QT, f=17)
                r = rt[:, :, k * OH:k * OH + heads]
                link(dve.reciprocal(r, o[:, :, :, 16]))
                ins = dve.tensor_tensor(
                    o_all[:, b * QT:(b + 1) * QT].rearrange("p q (n f) -> p q n f", f=XHD)[:, :, k * OH:k * OH + heads],
                    o[:, :, :, 0:16], r.unsqueeze(3).to_broadcast([P, QT, heads, XHD]), ALU.mult)
            ins.then_inc(o_done, 1)

        @block.vector
        def _(dve):
            link = Chain(dve, chain)
            picks = 0

            def pick_next():
                deq.pick(dve, picks // 16, picks % 16)

            for b in range(B):
                for n in range(XNH):
                    for m in range(N):
                        u = (b * XNH + n) * N + m
                        dve.wait_ge(s_done, u + 1)
                        for qt, c in max_packs[m]:
                            ins = dve.tensor_reduce(mx[:, b, qt, n:n + 1], ps[u % 2][:, c:c + (qt + 1) * P],
                                                    AX.X, ALU.max)
                        ins.then_inc(m_done, 1)
                        if m == 0 or b:
                            pick_next()
                            picks += 1
                dve.wait_ge(m_done, (b + 1) * XNH * N)
                link(dve.tensor_copy(ms[:, b, :, 0, :], mx[:, b]))
                dve.tensor_tensor(ms[:, b, :, 1, :], mx[:, b], ms[:, b, :, 0, :], ALU.subtract).then_inc(ms_done, 1)
                if b:
                    finish(dve, link, b - 1)
            for picks in range(picks, 16 * D_TILES):
                pick_next()
            finish(dve, link, B - 1)

        @block.gpsimd
        def _(pool):
            for o in range(D_TILES):
                deq.add(pool, o)

        @block.scalar
        def _(act):
            def copy_out(h):
                act.wait_ge(pv_done, h + 1)
                if h:
                    act.wait_ge(out_done, h)
                act.activation(oT, p_w[0:XHD + 1, :], ACT.Copy).then_inc(ot_copied, 1)

            for b in range(B):
                act.wait_ge(mt_done, b + 1)
                act.activation(mT[:, b, :], ps[0][0:2 * XNH, :], ACT.Copy).then_inc(mt_copied, 1)
                for n in range(XNH):
                    for m, pack in enumerate(exp_packs):
                        u = (b * XNH + n) * N + m
                        h = b * XNH + n
                        w = sum(S - kt * P for kt, _ in pack)
                        act.wait_ge(e_done, u + 1)
                        if m == 0 and h >= 2:
                            act.wait_ge(pv_done, h - 1)
                        act.activation(pT[n % 2][:, m, 0:w], pe_[u % 2][:, 0:w], ACT.Exp,
                                       scale=scale).then_inc(exp_done, 1)
                    if n:
                        copy_out(h - 1)
                    if h in turn_after:
                        deq.copy(act, turn_after[h], p_w, fT)
                copy_out(b * XNH + XNH - 1)
            deq.copy(act, D_TILES - 1, p_w, fT)


def rat_write(nc, name, h, srcT, n_k, odT, bias_row, duT, du_b, ones, ident, src=None, fetch=(), prefetch=()):
    with ExitStack() as ctx:
        sb, psum, sem = scope(nc, ctx)
        od = sb(name + "od", [P, NT, OD + XH])
        e = sb(name + "e", [P, NT, SP])
        sp_ = sb(name + "sp", [P, NT, SP])
        dlT = sb(name + "dlT", [DR, 2, P])
        if src is not None:
            sT = sb(name + "sT", [P, 2, IC, P])
        nb_, rb = sb(name + "nb", [P, NT, N_A]), sb(name + "rb", [P, NT, N_A])
        ab = [sb(f"{name}ab{i}", [P, XH, 3]) for i in range(2)]
        bb = [sb(f"{name}bb{i}", [P, XH, 3]) for i in range(2)]
        ha = [sb(f"{name}ha{i}", [P, XH, 3]) for i in range(2)]
        sk = [sb(f"{name}sk{i}", [P, XH]) for i in range(2)]
        p_o = [psum(f"{name}po{i}", [P, 512]) for i in range(2)]
        p_d = [psum(f"{name}pd{i}", [P, 512]) for i in range(2)]
        p_t = [psum(f"{name}pt{i}", [P, 512]) for i in range(2)]
        p_l = psum(name + "pl", [P, 512])
        st_, sc_, od_done, od_copied, dl_t, dl_c, dd, dc = (sem(name + n) for n in (
            "st", "sc", "od_d", "od_c", "dl_t", "dl_c", "dd", "dc"))
        abs_done, e1, l1, sp_done, da, ex, b_done, ha_done, sk1, new3, chain, poolc = (sem(name + n) for n in (
            "abs", "e1", "l1", "sp_d", "da", "ex", "b_d", "ha_d", "sk1", "new3", "chain", "poolc"))
        fetched = sem(name + "fetched")
        block = ctx.enter_context(nc.Block())

        @block.sync
        def _(sp):
            for dst, from_dram in prefetch:
                sp.dma_start(dst, from_dram).then_inc(fetched, 16)
            if fetch:
                sp.wait_ge(od_done, NT)
            for dst, from_dram in fetch:
                sp.dma_start(dst, from_dram).then_inc(fetched, 16)
            if fetch or prefetch:
                sp.wait_ge(fetched, 16 * (len(fetch) + len(prefetch)))

        @block.tensor
        def _(pe):
            def turn(i):
                if i >= 2:
                    pe.wait_ge(sc_, i - 1)
                for c in range(IC):
                    ins = pe.transpose(p_t[i % 2][:, c * P:(c + 1) * P], src[:, i, c * P:(c + 1) * P], ident[:])
                ins.then_inc(st_, 1)

            def main(i):
                if src is not None:
                    pe.wait_ge(sc_, i + 1)
                if i >= 2:
                    pe.wait_ge(od_copied, i - 1)
                for k in range(n_k):
                    lhs = sT[:, i % 2, k, :] if src is not None else srcT[:, k, i * P:(i + 1) * P]
                    pe.matmul(p_o[i % 2][:, 0:OD], lhs, odT[:, k, :], start=k == 0, stop=False)
                pe.matmul(p_o[i % 2][:, 0:OD], ones[:], bias_row[:], start=False, stop=True).then_inc(od_done, 1)

            def low(i):
                pe.wait_ge(od_copied, i + 1)
                if i:
                    pe.wait_ge(dl_c, i)
                pe.transpose(p_l[0:DR, 0:P], od[:, i, C_DL:C_DL + DR], ident[:]).then_inc(dl_t, 1)

            def delta(i):
                pe.wait_ge(dl_c, i + 1)
                if i >= 2:
                    pe.wait_ge(dc, i - 1)
                pe.matmul(p_d[i % 2][:, 0:XH], dlT[:, i % 2, :], duT[:], start=True, stop=False)
                pe.matmul(p_d[i % 2][:, 0:XH], ones[:], du_b[:], start=False, stop=True).then_inc(dd, 1)

            if src is not None:
                turn(0)
            for i in range(NT + 2):
                if src is not None and i + 1 < NT:
                    turn(i + 1)
                if i < NT:
                    main(i)
                if 1 <= i <= NT:
                    low(i - 1)
                if i >= 2:
                    delta(i - 2)

        @block.scalar
        def _(act):
            for i in range(NT + 3):
                if src is not None and i < NT:
                    act.wait_ge(st_, i + 1)
                    if i >= 2:
                        act.wait_ge(od_done, i - 1)
                    act.activation(sT[:, i % 2].rearrange("p a b -> p (a b)"), p_t[i % 2][:, 0:IC * P],
                                   ACT.Copy).then_inc(sc_, 1)
                if 1 <= i <= NT:
                    act.wait_ge(od_done, i)
                    act.activation(od[:, i - 1, 0:OD], p_o[(i - 1) % 2][:, 0:OD], ACT.Copy).then_inc(od_copied, 1)
                if 2 <= i <= NT + 1:
                    act.wait_ge(dl_t, i - 1)
                    if i >= 4:
                        act.wait_ge(dd, i - 3)
                    act.activation(dlT[:, (i - 2) % 2, :], p_l[0:DR, 0:P], ACT.Copy).then_inc(dl_c, 1)
                if i >= 3:
                    act.wait_ge(dd, i - 2)
                    act.activation(od[:, i - 3, OD:OD + XH], p_d[(i - 3) % 2][:, 0:XH], ACT.Copy).then_inc(dc, 1)
            act.wait_ge(dc, NT)
            x = od[:, :, C_A:C_A + SP]
            act.activation(e[:], x, ACT.Abs).then_inc(abs_done, 1)
            act.wait_ge(abs_done, 1)
            act.activation(e[:], e[:], ACT.Exp, scale=-1.0).then_inc(e1, 1)
            act.wait_ge(e1, 1)
            act.activation(e[:], e[:], ACT.Ln, bias=1.0).then_inc(l1, 1)
            for i in range(NT):
                act.wait_ge(da, i + 1)
                act.activation(ab[i % 2][:], ab[i % 2][:], ACT.Exp, scale=-1.0).then_inc(ex, 1)

        @block.vector
        def _(dve):
            link = Chain(dve, chain)
            dve.wait_ge(l1, 1)
            dve.scalar_tensor_tensor(out=sp_[:], in0=od[:, :, C_A:C_A + SP], scalar=0.0, in1=e[:],
                                     op0=ALU.max, op1=ALU.add).then_inc(sp_done, 1)
            dve.wait_ge(sp_done, 1)
            link(dve.tensor_scalar(nb_[:], sp_[:, :, 0:N_A], SSM_EPS, -1.0, ALU.add, ALU.mult))
            link(dve.reciprocal(rb[:], nb_[:]))
            link(dve.tensor_tensor(nb_[:], rb[:], od[:, :, C_B:C_B + N_B], ALU.mult))

            def rate(i):
                if i >= 2:
                    dve.wait_ge(b_done, i - 1)
                    dve.wait_ge(ha_done, i - 1)
                dve.tensor_tensor(ab[i % 2][:].rearrange("p (s r) c -> p s r c", r=RH),
                                  sp_[:, i, N_A:SP].rearrange("p (s r) -> p s r", r=RH).unsqueeze(3).to_broadcast([P, HS, RH, 3]),
                                  sp_[:, i, 0:N_A].rearrange("p (r c) -> p r c", c=3).unsqueeze(1).to_broadcast([P, HS, RH, 3]),
                                  ALU.mult).then_inc(da, 1)

            def update(i):
                j = i % 2
                hv = h[:, i].rearrange("p (n c) -> p n c", c=XC)
                out = od[:, i, 0:XH]
                dve.wait_ge(ex, i + 1)
                dve.scalar_tensor_tensor(out=bb[j][:].rearrange("p (s r) c -> p s (r c)", r=RH),
                                         in0=ab[j][:].rearrange("p (s r) c -> p s (r c)", r=RH), scalar=1.0,
                                         in1=nb_[:, i, :].unsqueeze(1).to_broadcast([P, HS, N_A]),
                                         op0=ALU.subtract, op1=ALU.mult).then_inc(b_done, 1)
                dve.wait_ge(b_done, i + 1)
                link(dve.tensor_tensor(bb[j][:], bb[j][:], out.unsqueeze(2).to_broadcast([P, XH, 3]), ALU.mult))
                dve.wait_ge(ha_done, i + 1)
                dve.tensor_tensor(hv[:, :, 0:3], ha[j][:], bb[j][:], ALU.add).then_inc(new3, 1)

            rate(0)
            for i in range(NT):
                if i + 1 < NT:
                    rate(i + 1)
                update(i)

        @block.gpsimd
        def _(pool):
            pool.wait_ge(sp_done, 1)
            for i in range(NT):
                j = i % 2
                hv = h[:, i].rearrange("p (n c) -> p n c", c=XC)
                if i >= 2:
                    pool.wait_ge(poolc, 2 * (i - 1))
                pool.tensor_tensor(sk[j][:].rearrange("p (s r) -> p s r", r=RH),
                                   sp_[:, i, N_A:SP].rearrange("p (s r) -> p s r", r=RH),
                                   od[:, i, C_SKIP:C_SKIP + N_SKIP].unsqueeze(1).to_broadcast([P, HS, RH]),
                                   ALU.mult).then_inc(sk1, 1)
                pool.wait_ge(sk1, i + 1)
                pool.tensor_tensor(sk[j][:], sk[j][:], od[:, i, 0:XH], ALU.mult).then_inc(poolc, 1)
                pool.wait_ge(poolc, 2 * i + 1)
                pool.tensor_tensor(hv[:, :, 3], hv[:, :, 3], sk[j][:], ALU.add).then_inc(poolc, 1)
                pool.wait_ge(ex, i + 1)
                if i >= 2:
                    pool.wait_ge(new3, i - 1)
                pool.tensor_tensor(ha[j][:], hv[:, :, 0:3], ab[j][:], ALU.mult).then_inc(ha_done, 1)


def mlp(nc, inT, wT, yT, deq, fT):
    with ExitStack() as ctx:
        sb, psum, sem = scope(nc, ctx)
        sg = [sb(f"m_sg{i}", [P, S]) for i in range(2)]
        p_g = [psum(f"m_g{i}", [P, S]) for i in range(3)]
        p_u = [psum(f"m_u{i}", [P, S]) for i in range(3)]
        done, silu, mul = sem("m_done"), sem("m_silu"), sem("m_mul")
        p_w = psum("m_pw", [P, 512])
        block = ctx.enter_context(nc.Block())
        steps = [(b, m) for b in range(B) for m in range(MT)]
        @block.sync
        def _(sp):
            deq.load(sp, KT - 1)

        @block.gpsimd
        def _(pool):
            deq.add(pool, KT - 1)

        @block.tensor
        def _(pe):
            deq.turn(pe, KT - 2, p_w)
            for n, (b, m) in enumerate(steps):
                if n >= 3:
                    pe.wait_ge(mul, n - 2)
                for g, dst in enumerate((p_g, p_u)):
                    for ic in range(IC):
                        ins = pe.matmul(dst[n % 3][:], wT[:, g, ic, m * P:(m + 1) * P],
                                        inT[:, g * IC + ic, b * S:(b + 1) * S], start=ic == 0, stop=ic == IC - 1)
                ins.then_inc(done, 1)
            deq.turn(pe, KT - 1, p_w)

        @block.scalar
        def _(act):
            deq.copy(act, KT - 2, p_w, fT)
            for n in range(len(steps)):
                act.wait_ge(done, n + 1)
                if n >= 2:
                    act.wait_ge(mul, n - 1)
                act.activation(sg[n % 2][:], p_g[n % 3][:], ACT.Silu).then_inc(silu, 1)
            deq.copy(act, KT - 1, p_w, fT)

        @block.vector
        def _(dve):
            for n, (b, m) in enumerate(steps):
                dve.wait_ge(silu, n + 1)
                dve.tensor_tensor(yT[:, m, b * S:(b + 1) * S], p_u[n % 3][:], sg[n % 2][:], ALU.mult).then_inc(mul, 1)
                if n < 8:
                    deq.pick(dve, KT - 1, 2 * n)
                    deq.pick(dve, KT - 1, 2 * n + 1)


def final_norm(nc, x1, h, ident, eps, zT):
    with ExitStack() as ctx:
        sb, psum, sem = scope(nc, ctx)
        z = [sb(f"f_z{i}", [P, D]) for i in range(2)]
        st, mv = sb("f_st", [P, NT, 2, 6]), sb("f_mv", [P, NT, 2])
        sd, r, t = sb("f_sd", [P, NT]), sb("f_r", [P, NT]), sb("f_t", [P, NT])
        pt = [psum(f"f_pt{i}", [P, 512]) for i in range(4)]
        chain, added, var_ready, sd_ready, z_ready, turned, copied = (sem(f"f_{n}") for n in (
            "chain", "added", "var", "sdr", "z_ready", "turned", "copied"))
        block = ctx.enter_context(nc.Block())

        @block.gpsimd
        def _(pool):
            for i in range(NT):
                pool.tensor_tensor(x1[:, i, :], x1[:, i, :], h[:, i, :], ALU.add).then_inc(added, 1)

        @block.vector
        def _(dve):
            link = Chain(dve, chain)

            def finish(i):
                c = slice(i, i + 1)
                dve.wait_ge(sd_ready, i + 1)
                rsqrt_newton(dve, link, r[:, c], sd[:, c], mv[:, i, 1:2], t[:, c], LN_EPS)
                if i >= 2:
                    dve.wait_ge(turned, 2 * (i - 1))
                dve.tensor_scalar(z[i % 2][:], x1[:, i, :], mv[:, i, 0:1], t[:, c],
                                  ALU.subtract, ALU.mult).then_inc(z_ready, 1)

            for i in range(NT):
                dve.wait_ge(added, i + 1)
                dve.bn_stats(st[:, i, 0, :], x1[:, i, 0:512])
                link(dve.bn_stats(st[:, i, 1, :], x1[:, i, 512:1024]))
                dve.bn_aggr(mv[:, i, :], st[:, i].rearrange("p h s -> p (h s)")).then_inc(var_ready, 1)
                if i:
                    finish(i - 1)
            finish(NT - 1)

        @block.scalar
        def _(act):
            for i in range(NT + 1):
                if i < NT:
                    act.wait_ge(var_ready, i + 1)
                    act.activation(sd[:, i:i + 1], mv[:, i, 1:2], ACT.Sqrt, bias=eps[:]).then_inc(sd_ready, 1)
                if i:
                    for g in range(2):
                        u = 2 * (i - 1) + g
                        act.wait_ge(turned, u + 1)
                        act.activation(zT[:, 4 * g:4 * g + 4, (i - 1) * P:i * P],
                                       pt[u % 4][:].rearrange("p (k c) -> p k c", c=P), ACT.Copy).then_inc(copied, 1)

        @block.tensor
        def _(pe):
            for i in range(NT):
                pe.wait_ge(z_ready, i + 1)
                for g in range(2):
                    u = 2 * i + g
                    if u >= 4:
                        pe.wait_ge(copied, u - 3)
                    for k in range(4):
                        c = (4 * g + k) * P
                        ins = pe.transpose(pt[u % 4][:, k * P:(k + 1) * P], z[i % 2][:, c:c + P], ident[:])
                    ins.then_inc(turned, 1)


class Dequantiser:

    def __init__(self, nc, ctx, a, ident):
        sb, psum, sem = scope(nc, ctx)
        self.a, self.ident = a, ident
        self.planes = sb("d_planes", [P, 4, 32], I32)
        self.lut = sb("d_lut", [P, 16])
        self.sh_r, self.sh_j = sb("d_shr", [P, 4], I32), sb("d_shj", [P, 8], I32)
        self.x = sb("d_x", [P, 4, 4, 32], I32)
        self.nib = sb("d_nib", [P, 4, 32], I32)
        self.code = self.picks = self.w = None
        self.loaded, self.made, self.chain, self.picked, self.summed, self.turned, self.copied = (
            sem(f"d_{n}") for n in ("loaded", "made", "chain", "picked", "summed", "turned", "copied"))
        self.link = None

    def use(self, name, ctx, nc, picks=None):
        sb, _, _ = scope(nc, ctx)
        self.code = sb(name + "code", [P, D], I32)
        self.w = [sb(f"{name}w{i}", [P, D])[:] for i in range(2)]
        self.picks = picks or [sb(f"{name}pick{i}", [P, D])[:] for i in range(2)]

    def make_shifts(self, pool):
        pool.iota(self.sh_r[:], pattern=[[1, 4]], base=0, channel_multiplier=0).then_inc(self.made, 1)
        pool.iota(self.sh_j[:], pattern=[[4, 8]], base=0, channel_multiplier=0).then_inc(self.made, 1)

    def load(self, sp, o):
        if o:
            sp.wait_ge(self.picked, 16 * o)
        sp.dma_start(self.planes[:], self.a["planes"][o]).then_inc(self.loaded, 16)
        sp.dma_start(self.lut[:], self.a["lut4"][o]).then_inc(self.loaded, 16)

    def codes(self, dve, o):
        if o == 0:
            dve.wait_ge(self.made, 2)
        if self.link is None:
            self.link = Chain(dve, self.chain)
        link = self.link
        link.eng = dve
        x, planes, nib, code = self.x, self.planes, self.nib, self.code
        dve.wait_ge(self.loaded, 32 * (o + 1))
        link(dve.tensor_tensor(x[:], planes[:].unsqueeze(2).to_broadcast([P, 4, 4, 32]),
                               self.sh_r[:].unsqueeze(1).unsqueeze(3).to_broadcast([P, 4, 4, 32]),
                               ALU.logical_shift_right))
        for p_ in range(4):
            ins = dve.tensor_scalar(x[:, p_], x[:, p_], 0x11111111, p_, ALU.bitwise_and, ALU.logical_shift_left)
        link(ins)
        dve.tensor_tensor(x[:, 0], x[:, 0], x[:, 1], ALU.bitwise_or)
        link(dve.tensor_tensor(x[:, 2], x[:, 2], x[:, 3], ALU.bitwise_or))
        link(dve.tensor_tensor(nib[:], x[:, 0], x[:, 2], ALU.bitwise_or))
        link(dve.tensor_tensor(code[:].rearrange("p (w j r) -> p w j r", j=8, r=4),
                               nib[:].rearrange("p r w -> p w r").unsqueeze(2).to_broadcast([P, 32, 8, 4]),
                               self.sh_j[:].unsqueeze(1).unsqueeze(3).to_broadcast([P, 32, 8, 4]),
                               ALU.logical_shift_right))
        link(dve.tensor_scalar(code[:], code[:], 15, None, ALU.bitwise_and))

    def pick(self, dve, o, v):
        if v == 0:
            self.codes(dve, o)
            if o >= 2:
                dve.wait_ge(self.turned, 2 * (o - 1))
        if v >= 3:
            dve.wait_ge(self.summed, 15 * o + v - 2)
        elif v in (1, 2) and o:
            dve.wait_ge(self.summed, 15 * o)
        dst = self.w[o % 2] if v == 0 else self.picks[v % 2]
        dve.tensor_scalar(dst, self.code[:], float(v), self.lut[:, v:v + 1], ALU.is_equal,
                          ALU.mult).then_inc(self.picked, 1)

    def add(self, pool, o):
        w = self.w[o % 2]
        for v in range(1, 16):
            pool.wait_ge(self.picked, 16 * o + v + 1)
            if v > 1:
                pool.wait_ge(self.summed, 15 * o + v - 1)
            pool.tensor_tensor(w, w, self.picks[v % 2], ALU.add).then_inc(self.summed, 1)

    def turn(self, pe, o, pt):
        pe.wait_ge(self.summed, 15 * (o + 1))
        for g in range(2):
            u = 2 * o + g
            if u:
                pe.wait_ge(self.copied, u)
            for k in range(4):
                c = (4 * g + k) * P
                ins = pe.transpose(pt[:, k * P:(k + 1) * P], self.w[o % 2][:, c:c + P], self.ident[:])
            ins.then_inc(self.turned, 1)

    def copy(self, act, o, pt, fT):
        for g in range(2):
            act.wait_ge(self.turned, 2 * o + g + 1)
            act.activation(fT[:, 4 * g:4 * g + 4, o * P:(o + 1) * P],
                           pt[:].rearrange("p (k c) -> p k c", c=P), ACT.Copy).then_inc(self.copied, 1)


def feed_forward(nc, zT, fT, x1, bias, out):
    out_t = out.rearrange("b (t p) d -> (b t) p d", p=P)
    with ExitStack() as ctx:
        sb, psum, sem = scope(nc, ctx)
        po = [psum(f"o_p{i}", [P, 512]) for i in range(4)]
        res = [sb(f"o_r{i}", [P, D]) for i in range(2)]
        xb, done, added = sem("o_xb"), sem("o_done"), sem("o_added")
        stored = [sem(f"o_stored{i}") for i in range(2)]
        block = ctx.enter_context(nc.Block())

        @block.gpsimd
        def _(pool):
            for i in range(NT):
                pool.tensor_tensor(x1[:, i, :], x1[:, i, :], bias[:], ALU.add).then_inc(xb, 1)

        @block.tensor
        def _(pe):
            for i in range(NT):
                for g in range(2):
                    u = 2 * i + g
                    if u >= 4:
                        pe.wait_ge(added, u - 3)
                    for k in range(KT):
                        ins = pe.matmul(po[u % 4][:], zT[:, k, i * P:(i + 1) * P], fT[:, k, g * 512:(g + 1) * 512],
                                        start=k == 0, stop=k == KT - 1)
                    ins.then_inc(done, 1)

        @block.vector
        def _(dve):
            for i in range(NT):
                dve.wait_ge(xb, i + 1)
                if i >= 2:
                    dve.wait_ge(stored[i % 2], 16 * (i // 2))
                for g in range(2):
                    u = 2 * i + g
                    dve.wait_ge(done, u + 1)
                    dve.tensor_tensor(res[i % 2][:, g * 512:(g + 1) * 512], po[u % 4][:],
                                      x1[:, i, g * 512:(g + 1) * 512], ALU.add).then_inc(added, 1)

        @block.sync
        def _(sp):
            for i in range(NT):
                sp.wait_ge(added, 2 * i + 2)
                sp.dma_start(out_t[i], res[i % 2][:]).then_inc(stored[i % 2], 16)
            for i in range(2):
                sp.wait_ge(stored[i], 16 * (NT // 2))



def make_constants(nc, ident, ident_r, eps, mask, half_mask, sel, ones, deq, loads):
    with ExitStack() as ctx:
        sb, psum, sem = scope(nc, ctx)
        a1, a2 = sb("c_a1", [2 * XNH, XNH, P]), sb("c_a2", [2 * XNH, XNH, P])
        made, done, loaded = sem("c_made"), sem("c_done"), sem("c_loaded")
        block = ctx.enter_context(nc.Block())

        @block.sync
        def _(sp):
            for dst, src in loads:
                sp.dma_start(dst, src).then_inc(loaded, 16)
            sp.wait_ge(loaded, 16 * len(loads))

        @block.gpsimd
        def _(pool):
            deq.make_shifts(pool)
            for n, (t, v) in enumerate(((mask, 0.0), (half_mask, 1.0), (a1, -1.0), (a2, -1.0), (eps, LN_EPS), (ones, 1.0))):
                pool.memset(t[:], v).then_inc(made, 1)
            pool.wait_ge(made, 6)
            pool.affine_select(out=mask[:], in_=mask[:], compare_op=ALU.is_ge, fill=-MASKED, base=0,
                               pattern=[[1, P]], channel_multiplier=-1)
            pool.affine_select(out=half_mask[:], in_=half_mask[:], compare_op=ALU.is_ge, fill=0.0, base=0,
                               pattern=[[-XC, 32]], channel_multiplier=1).then_inc(made, 1)
            pool.affine_select(out=a1[:], in_=a1[:], compare_op=ALU.is_equal, fill=0.0, base=0,
                               pattern=[[-1, XNH], [0, P]], channel_multiplier=1).then_inc(made, 1)
            pool.affine_select(out=a2[:], in_=a2[:], compare_op=ALU.is_equal, fill=0.0, base=-XNH,
                               pattern=[[-1, XNH], [0, P]], channel_multiplier=1).then_inc(made, 1)
            pool.wait_ge(made, 9)
            pool.affine_select(out=half_mask[:], in_=half_mask[:], compare_op=ALU.is_ge, fill=0.0, base=XC - 1,
                               pattern=[[XC, 32]], channel_multiplier=-1).then_inc(done, 1)

        @block.vector
        def _(dve):
            dve.tensor_copy(ident_r[:], ident[:])
            dve.wait_ge(made, 9)
            dve.tensor_tensor(sel[:], a1[:], a2[:], ALU.add)


def load(nc, name, pairs):
    with ExitStack() as ctx:
        s = ctx.enter_context(nc.semaphore(name))
        block = ctx.enter_context(nc.Block())

        @block.sync
        def _(sp):
            for dst, src in pairs:
                sp.dma_start(dst, src).then_inc(s, 16)
            sp.wait_ge(s, 16 * len(pairs))


def program(nc, a, out):
    with ExitStack() as keep:
        sb, psum, sem = scope(nc, keep)
        acc, ident, ident_bf = attention_program(nc, keep, a)
        x1, h = sb("x1", [P, NT, D]), sb("h", [P, NT, D])
        deq = Dequantiser(nc, keep, a, ident)
        ident_r, eps, mask = sb("ident_r", [P, P], F32R), sb("eps2", [P, 1]), sb("mask2", [P, P], BF16)
        half_mask, ones = sb("half_mask", [P, 32]), sb("ones", [1, P])
        rw1, g1, b1 = sb("rw1", [P, KT * 3]), sb("g1", [P, 3 * IC]), sb("b1", [P, 3 * IC])
        rw2, g2, b2 = sb("rw2", [P, KT * 2]), sb("g2", [P, 2 * IC]), sb("b2", [P, 2 * IC])
        with ExitStack() as xat:
            sbx, _, _ = scope(nc, xat)
            qkvT, sel = sbx("qkvT", [P, IC, 3 * XH]), sbx("sel", [2 * XNH, XNH, P], F32R)
            pos, inv = sbx("pos", [P, NT], I32), sbx("inv", [P, 8])
            ang_cos, ang_sin = sbx("ang_cos", [P, NT, 8]), sbx("ang_sin", [P, NT, 8])
            first = [(rw1[:], a["rw1"]), (g1[:], a["g1"]), (b1[:], a["b1"]), (rw2[:], a["rw2"]),
                            (g2[:], a["g2"]), (b2[:], a["b2"]), (qkvT[:], a["qkvT"]),
                            (pos[:], a["pos"]), (inv[:], a["inv"])]
            make_constants(nc, ident, ident_r, eps, mask, half_mask, sel, ones, deq, first)
            rope_angles(nc, pos, inv, ang_cos, ang_sin)
            residual_norm(nc, a, acc, ident, eps, x1, h)
            inT = acc[:, 0:3 * IC, :]
            x1_kept = nc.dram_tensor("x1_kept", [P, NT, D], F32, kind="Internal").ap()
            rat_read(nc, "r1", h, rw1, g1, b1, 3, ident, eps, half_mask, inT, spill=[(x1_kept, x1[:])])
            qT = sbx("qT2", [P, XNH // 2, TOK], F32R)
            kT = sbx("kT2", [P, XNH // 2, TOK], F32R)
            v_aug = sbx("v_aug", [P, NT, XNH, XHD + 1])
            project_qkv(nc, inT, qkvT, ang_cos, ang_sin, ident, ident_r, qT, kT, v_aug, x1)
            fT = x1
            pT = [acc[:, 2 * i:2 * i + 2, :].rearrange("p a (b s) -> p (a b) s", s=S) for i in range(2)]
            o_all = acc[:, 4:6, :].rearrange("p a (b s) -> p (a b) s", s=XH)
            deq.use("dx_", xat, nc, picks=[acc[:, 6 + i, :] for i in range(2)])
            cross_attention(nc, qT, kT, v_aug, mask, sel, ident, ident_r, ident_bf, pT, o_all, deq, fT)
        odT1, bias1, duT1, dub1 = (sb("odT1", [P, IC, OD]), sb("bias1", [1, OD]), sb("duT1", [DR, XH]),
                                   sb("dub1", [1, XH]))
        bias2, duT2, dub2 = sb("bias2", [1, OD]), sb("duT2", [DR, XH]), sb("dub2", [1, XH])
        load(nc, "l4", [(odT1[:], a["odT1"]), (bias1[:], a["bias1"]),
                            (duT1[:], a["duT1"]), (dub1[:], a["dub1"]), (bias2[:], a["bias2"]),
                            (duT2[:], a["duT2"]), (dub2[:], a["dub2"])])
        odT2 = sb("odT2", [P, MT, OD])
        ml = ExitStack()
        sbm, _, _ = scope(nc, ml)
        wT = sbm("mlp_w", [P, 2, IC, M])
        rat_write(nc, "w1", h, None, IC, odT1, bias1, duT1, dub1, ones, ident, src=o_all,
                  prefetch=[(wT[:], a["mlp_wT"]), (odT2[:], a["odT2"])])
        with ml:
            inT2 = sbm("inT2", [P, 2 * IC, TOK])
            deq.use("dm_", ml, nc)
            rat_read(nc, "r2", h, rw2, g2, b2, 2, ident, eps, half_mask, inT2, deq, KT - 2)
            mlp(nc, inT2, wT, acc, deq, fT)
        bias = sb("bias", [P, D])
        x1 = acc
        rat_write(nc, "w2", h, acc, MT, odT2, bias2, duT2, dub2, ones, ident,
                  fetch=[(x1[:], x1_kept), (bias[:], a["bias"].partition_broadcast(P))])
        zT = sb("zT", [P, KT, TOK])
        final_norm(nc, x1, h, ident, eps, zT)
        feed_forward(nc, zT, fT, x1, bias, out)


def arrange(inputs):
    def c(x):
        return np.ascontiguousarray(x)

    r = {"x": c(inputs["x"])}
    for n, heads in (("q", NH), ("k", NKV), ("v", NKV)):
        w = np.asarray(inputs["L0_attn_qw_" + n]).reshape(KT, P, heads, HD)
        r["w_" + n] = c(w.transpose(2, 1, 0, 3)).reshape(heads, P, KT * HD)
        sc = np.asarray(inputs["L0_attn_scales_" + n]).reshape(KT, heads, HD)
        r["sc_" + n] = c(sc.transpose(2, 1, 0)).reshape(HD, heads * KT)
    r["w_o"] = c(inputs["L0_attn_qw_o"]).reshape(NH, P, D)
    r["sc_o"] = c(np.asarray(inputs["L0_attn_scales_o"]).reshape(NH, KT, P).transpose(2, 0, 1)).reshape(P, NH * KT)
    for i, (n, o) in enumerate((("attn", 3), ("mlp", 2)), 1):
        g = {k: np.asarray(inputs[f"L0_xattn_{n}_{k}"]) for k in
             ("read_w", "read_g", "read_b", "wod_w", "wab_w", "wab_b", "du_w", "du_b")}
        r[f"rw{i}"] = c(g["read_w"].transpose(0, 2, 1).reshape(KT, P, o).transpose(1, 0, 2)).reshape(P, KT * o)
        r[f"g{i}"] = c(g["read_g"].reshape(o * IC, P).T)
        r[f"b{i}"] = c(g["read_b"].reshape(o * IC, P).T)
        rows = [slice(N_A, N_A + N_B), slice(N_A + N_B, None), slice(0, N_A)]
        w = np.concatenate([g["wod_w"]] + [g["wab_w"][s] for s in rows])
        r[f"odT{i}"] = c(w.T.reshape(-1, P, OD).transpose(1, 0, 2))
        r[f"bias{i}"] = np.concatenate([np.zeros(C_B, g["wab_b"].dtype)] + [g["wab_b"][s] for s in rows])[None]
        r[f"duT{i}"] = c(g["du_w"].T)
        r[f"dub{i}"] = c(g["du_b"])[None]
    r["qkvT"] = c(np.asarray(inputs["L0_xattn_qkv_w"]).transpose(2, 0, 1).reshape(IC, P, 3 * XH).transpose(1, 0, 2))
    r["pos"] = c(np.asarray(inputs["pos_BxS"]).reshape(NT, P).T)
    r["mlp_wT"] = c(np.asarray(inputs["ctx_1024"]).reshape(2, M, IC, P).transpose(3, 0, 2, 1))
    r["planes"] = c(np.asarray(inputs["L0_ffn_qweight"])[:4].reshape(4, KT, P, 32).transpose(1, 2, 0, 3))
    r["lut4"] = c(inputs["L0_ffn_lut4"]).reshape(KT, P, 16)
    r["bias"] = c(inputs["L0_ffn_bias"])
    return r


def rope_constants():
    inv = (1.0 / 10000.0 ** (np.arange(0, HD, 2, dtype=np.float32) / np.float32(HD))).astype(np.float32)
    ang = np.arange(S, dtype=np.float32)[:, None] * inv
    f = np.float32(HD ** -0.25)
    cos, sin = np.cos(ang).T * f, np.sin(ang).T * f
    half = XHD // 2
    freq = (1.0 / 10000.0 ** (np.arange(half, dtype=np.float32) / np.float32(half))).astype(np.float32)
    return {"cos": np.concatenate([cos, cos]).astype(np.float32),
            "sin": np.concatenate([-sin, sin]).astype(np.float32),
            "inv": np.tile(freq, (P, 1))}


def kernel(**inputs):
    import concourse.bacc as _bacc
    from concourse.bass_utils import run_bass_kernel_spmd as _run

    nc = _bacc.Bacc("TRN2", target_bir_lowering=False, num_devices=1)
    nc.disable_value_cache = True
    arrays = {f"in_{k}": v for k, v in {**arrange(inputs), **rope_constants()}.items()}
    a = {k[3:]: nc.dram_tensor(k, v.shape, mybir.dt.from_np(v.dtype), kind="ExternalInput").ap()
         for k, v in arrays.items()}
    out = nc.dram_tensor("out_0", (B, S, D), F32, kind="ExternalOutput").ap()
    program(nc, a, out)
    r = _run(nc, [arrays], core_ids=[0])
    return r.results[0]["out_0"]
```
